# Optimizing a Trainium2 kernel written in Bass

```python
import numpy as np
import jax
import jax.numpy as jnp

def _softmax(x, axis=-1):
    return jax.nn.softmax(x, axis=axis)

def _gelu(x):
    return jax.nn.gelu(x, approximate=True)

def _silu(x):
    return jax.nn.silu(x)

def _sigmoid(x):
    return jax.nn.sigmoid(x)

def _layernorm(x, axis=-1, eps=1e-05):
    m = jnp.mean(x, axis=axis, keepdims=True)
    v = jnp.var(x, axis=axis, keepdims=True)
    return (x - m) / jnp.sqrt(v + eps)

def _scatter_add(tgt, idx, src, axis=0):
    return tgt.at[idx].add(src)

def _segment_sum(src, seg, n):
    return jax.ops.segment_sum(src, seg, n)
kernel_name = 'mk_metaformer_d1_conv_nhwc768_r4_41262d'

def setup_inputs(seed: int=0):
    np.random.seed(seed)
    _w = jnp.asarray

    def _rec_inputs():
        import jax
        import jax.numpy as jnp
        _gk = jax.random.key(seed)
        x = -0.0005963 + 1.001 * jax.random.normal(jax.random.fold_in(_gk, 1), (4, 32, 32, 192), jnp.float32)
        return x
    x = _rec_inputs()

    def _L0_conv_setup():
        import jax, jax.numpy as jnp
        import numpy as np
        B, H, W, C = (4, 32, 32, 192)
        NH = 12
        HD = C // NH

        def _get_rel_pos(q_size, k_size, rel_pos):
            q_coords = jnp.arange(q_size)[:, None] * max(k_size / q_size, 1.0)
            k_coords = jnp.arange(k_size)[None, :] * max(q_size / k_size, 1.0)
            rel = (q_coords - k_coords + (k_size - 1) * max(q_size / k_size, 1.0)).astype(jnp.int32)
            return rel_pos[rel]
        key = jax.random.key(seed)
        ks = jax.random.split(key, 12)
        s = 1.0 / np.sqrt(C)
        return {'hidden_states': jax.random.normal(ks[0], (B, H, W, C), jnp.float32), 'Wq': jax.random.normal(ks[1], (C, C), jnp.float32) * s, 'bq': jax.random.normal(ks[2], (C,), jnp.float32) * 0.02, 'Wk': jax.random.normal(ks[3], (C, C), jnp.float32) * s, 'bk': jax.random.normal(ks[4], (C,), jnp.float32) * 0.02, 'Wv': jax.random.normal(ks[5], (C, C), jnp.float32) * s, 'bv': jax.random.normal(ks[6], (C,), jnp.float32) * 0.02, 'Wp': jax.random.normal(ks[7], (C, C), jnp.float32) * s, 'bp': jax.random.normal(ks[8], (C,), jnp.float32) * 0.02, 'rel_h': jax.random.normal(ks[9], (2 * H - 1, HD), jnp.float32) * 0.02, 'rel_w': jax.random.normal(ks[10], (2 * W - 1, HD), jnp.float32) * 0.02}
    _L0_conv_all = _L0_conv_setup()
    _L0_conv_in = {k: v for k, v in _L0_conv_all.items() if k in ('Wq', 'bq', 'Wk', 'bk', 'Wv', 'bv', 'Wp', 'bp', 'rel_h', 'rel_w')}
    del _L0_conv_all

    def _L0_ffn_setup():
        import jax, jax.numpy as jnp
        import numpy as np
        QN, QP = (-8, 7)

        def round_pass(x):
            return x + jax.lax.stop_gradient(jnp.round(x) - x)

        def _quant_act(x, alpha_a):
            a = alpha_a.mean()
            return round_pass(jnp.clip(x / a, QN, QP))

        def _quant_w(w, alpha_w):
            return round_pass(jnp.clip(w / alpha_w[:, None], QN, QP))
        key = jax.random.key(seed)
        ks = jax.random.split(key, 9)
        B, S, D, H = (16, 256, 192, 768)

        def unif(k, shape):
            return jax.random.uniform(k, shape, jnp.float32, 0.02, 0.1)
        return {'x0': jax.random.normal(ks[0], (B, S, D), jnp.float32), 'w1': jax.random.normal(ks[1], (H, D), jnp.float32) * 0.02, 'b1': jax.random.normal(ks[2], (H,), jnp.float32) * 0.02, 'alpha_w1': unif(ks[3], (H,)), 'alpha_a1': unif(ks[4], (D,)), 'w2': jax.random.normal(ks[5], (D, H), jnp.float32) * 0.02, 'b2': jax.random.normal(ks[6], (D,), jnp.float32) * 0.02, 'alpha_w2': unif(ks[7], (D,)), 'alpha_a2': unif(ks[8], (H,))}
    _L0_ffn_all = _L0_ffn_setup()
    _L0_ffn_in = {k: v for k, v in _L0_ffn_all.items() if k in ('w1', 'b1', 'alpha_w1', 'alpha_a1', 'w2', 'b2', 'alpha_w2', 'alpha_a2')}
    del _L0_ffn_all
    return {'x': x, 'L0_conv_Wq': _L0_conv_in['Wq'], 'L0_conv_bq': _L0_conv_in['bq'], 'L0_conv_Wk': _L0_conv_in['Wk'], 'L0_conv_bk': _L0_conv_in['bk'], 'L0_conv_Wv': _L0_conv_in['Wv'], 'L0_conv_bv': _L0_conv_in['bv'], 'L0_conv_Wp': _L0_conv_in['Wp'], 'L0_conv_bp': _L0_conv_in['bp'], 'L0_conv_rel_h': _L0_conv_in['rel_h'], 'L0_conv_rel_w': _L0_conv_in['rel_w'], 'L0_ffn_w1': _L0_ffn_in['w1'], 'L0_ffn_b1': _L0_ffn_in['b1'], 'L0_ffn_alpha_w1': _L0_ffn_in['alpha_w1'], 'L0_ffn_alpha_a1': _L0_ffn_in['alpha_a1'], 'L0_ffn_w2': _L0_ffn_in['w2'], 'L0_ffn_b2': _L0_ffn_in['b2'], 'L0_ffn_alpha_w2': _L0_ffn_in['alpha_w2'], 'L0_ffn_alpha_a2': _L0_ffn_in['alpha_a2']}

def reference(x, L0_conv_Wq, L0_conv_bq, L0_conv_Wk, L0_conv_bk, L0_conv_Wv, L0_conv_bv, L0_conv_Wp, L0_conv_bp, L0_conv_rel_h, L0_conv_rel_w, L0_ffn_w1, L0_ffn_b1, L0_ffn_alpha_w1, L0_ffn_alpha_a1, L0_ffn_w2, L0_ffn_b2, L0_ffn_alpha_w2, L0_ffn_alpha_a2):
    import jax
    import jax.numpy as jnp

    def _L0_conv_ref(hidden_states, Wq, bq, Wk, bk, Wv, bv, Wp, bp, rel_h, rel_w):
        import jax, jax.numpy as jnp
        import numpy as np
        B, H, W, C = (4, 32, 32, 192)
        NH = 12
        HD = C // NH

        def _get_rel_pos(q_size, k_size, rel_pos):
            q_coords = jnp.arange(q_size)[:, None] * max(k_size / q_size, 1.0)
            k_coords = jnp.arange(k_size)[None, :] * max(q_size / k_size, 1.0)
            rel = (q_coords - k_coords + (k_size - 1) * max(q_size / k_size, 1.0)).astype(jnp.int32)
            return rel_pos[rel]
        b, h, w, c = hidden_states.shape
        hw = h * w
        x = hidden_states.reshape(b, hw, c)

        def heads(t):
            return t.reshape(b, hw, NH, HD).transpose(0, 2, 1, 3).reshape(b * NH, hw, HD)
        q = heads(x @ Wq + bq)
        k = heads(x @ Wk + bk)
        v = heads(x @ Wv + bv)
        attn = jnp.einsum('bqd,bkd->bqk', q, k) / np.sqrt(HD)
        Rh = _get_rel_pos(h, h, rel_h)
        Rw = _get_rel_pos(w, w, rel_w)
        rq = q.reshape(b * NH, h, w, HD)
        rel_bias_h = jnp.einsum('bhwc,hkc->bhwk', rq, Rh)
        rel_bias_w = jnp.einsum('bhwc,wkc->bhwk', rq, Rw)
        attn = (attn.reshape(b * NH, h, w, h, w) + rel_bias_h[:, :, :, :, None] + rel_bias_w[:, :, :, None, :]).reshape(b * NH, hw, hw)
        attn = jax.nn.softmax(attn, axis=-1)
        out = jnp.einsum('bqk,bkd->bqd', attn, v)
        out = out.reshape(b, NH, h, w, HD).transpose(0, 2, 3, 1, 4).reshape(b, h, w, c)
        return out @ Wp + bp

    def _L0_ffn_ref(x0, w1, b1, alpha_w1, alpha_a1, w2, b2, alpha_w2, alpha_a2):
        import jax, jax.numpy as jnp
        import numpy as np
        QN, QP = (-8, 7)

        def round_pass(x):
            return x + jax.lax.stop_gradient(jnp.round(x) - x)

        def _quant_act(x, alpha_a):
            a = alpha_a.mean()
            return round_pass(jnp.clip(x / a, QN, QP))

        def _quant_w(w, alpha_w):
            return round_pass(jnp.clip(w / alpha_w[:, None], QN, QP))
        xq = _quant_act(x0, alpha_a1)
        wq1 = _quant_w(w1, alpha_w1)
        x1 = jnp.einsum('bsd,hd->bsh', xq, wq1)
        x1 = x1 * alpha_w1 * alpha_a1.mean() + b1
        x1 = jax.nn.gelu(x1, approximate=False)
        x1 = jnp.clip(x1, -10.0, 10.0)
        hq = _quant_act(x1, alpha_a2)
        wq2 = _quant_w(w2, alpha_w2)
        x2 = jnp.einsum('bsh,dh->bsd', hq, wq2)
        x2 = x2 * alpha_w2 * alpha_a2.mean() + b2
        return x2

    def _gn(v, G=32, eps=1e-05):
        B_, H_, W_, C_ = v.shape
        g = v.reshape(B_, H_, W_, G, C_ // G)
        m = jnp.mean(g, axis=(1, 2, 4), keepdims=True)
        s = jnp.var(g, axis=(1, 2, 4), keepdims=True)
        return ((g - m) / jnp.sqrt(s + eps)).reshape(v.shape)

    def _ln_c(v, eps=1e-06):
        m = jnp.mean(v, axis=-1, keepdims=True)
        s = jnp.var(v, axis=-1, keepdims=True)
        return (v - m) / jnp.sqrt(s + eps)

    def _ln_t(v, eps=1e-05):
        m = jnp.mean(v, axis=-1, keepdims=True)
        s = jnp.var(v, axis=-1, keepdims=True)
        return (v - m) / jnp.sqrt(s + eps)

    def _to_tokens(v):
        B_, H_, W_, C_ = v.shape
        return v.reshape(B_, H_ * W_, C_)

    def _from_tokens(t, like):
        return t.reshape(like.shape)
    x = x + _L0_conv_ref(_ln_c(x), L0_conv_Wq, L0_conv_bq, L0_conv_Wk, L0_conv_bk, L0_conv_Wv, L0_conv_bv, L0_conv_Wp, L0_conv_bp, L0_conv_rel_h, L0_conv_rel_w)
    t = _to_tokens(x)
    t = t + _L0_ffn_ref(_ln_t(t), L0_ffn_w1, L0_ffn_b1, L0_ffn_alpha_w1, L0_ffn_alpha_a1, L0_ffn_w2, L0_ffn_b2, L0_ffn_alpha_w2, L0_ffn_alpha_a2)
    x = _from_tokens(t, x)
    return x

_drawn_inputs = setup_inputs


def setup_inputs(seed=0):
    import zlib

    import numpy as np

    out = dict(_drawn_inputs(seed))
    spreads = {}
    factors = {'L0_conv_bq': 23.13,
     'L0_conv_bk': 200.0,
     'L0_conv_rel_h': 8.0,
     'L0_conv_rel_w': 8.0,
     'L0_ffn_b1': 44.136,
     'L0_ffn_alpha_w1': 21.672,
     'L0_ffn_b2': 2.737,
     'L0_ffn_alpha_w2': 22.84,
     'L0_ffn_alpha_a2': 200.0,
     'L0_conv_bp': 2.695,
     'L0_ffn_w1': 8.0,
     'L0_ffn_w2': 8.0}
    for name, (base, spread) in spreads.items():
        noise = np.random.default_rng([zlib.crc32(name.encode()), seed]).standard_normal(out[name].shape)
        drawn = base * np.exp(spread * noise) if base else spread * noise
        out[name] = jnp.asarray(drawn.astype(out[name].dtype))
    for name, factor in factors.items():
        out[name] = (out[name] * factor).astype(out[name].dtype)
    return out
```

```python
from contextlib import ExitStack

import concourse.bass as bass
from concourse import mybir

F32 = mybir.dt.float32
F16 = mybir.dt.float16
BF16 = mybir.dt.bfloat16
ALU = mybir.AluOpType
ACT = mybir.ActivationFunctionType
AX_X = mybir.AxisListType.X

P = 128
BATCH, GRID, C = 4, 32, 192
SEQ = GRID * GRID
TOKENS = BATCH * SEQ
NH = 12
HD = C // NH
QUAD = 4
NQUAD = NH // QUAD
QC = QUAD * HD
UNITS = BATCH * NQUAD
REL = 2 * GRID - 1
HALF = C // 2
GROUP = 512
TILES = GROUP // P
GROUPS = TOKENS // GROUP
HID = 768
HT = HID // P
KT = SEQ // P
SLOT = 32
NLO = 2 * GRID + 2
MAGIC = 1.5 * 2.0 ** 23
QN, QP = -8.0, 7.0


def need(eng, sem, value):
    if not isinstance(value, int) or value > 0:
        eng.wait_ge(sem, value)


def each_pass(eng, passes, emit):
    emit(0)
    with eng.Fori(1, passes) as i:
        emit(i)


class Phase:

    def __init__(self, nc, name):
        self.nc, self.name, self.stack = nc, name, ExitStack()

    def __enter__(self):
        self.stack.__enter__()
        return self

    def __exit__(self, *a):
        return self.stack.__exit__(*a)

    def sb(self, name, shape, dt):
        return self.stack.enter_context(self.nc.sbuf_tensor(f"{self.name}_{name}", shape, dt))

    def ps(self, name, shape, dt):
        return self.stack.enter_context(self.nc.psum_tensor(f"{self.name}_{name}", shape, dt))

    def sem(self, name):
        return self.stack.enter_context(self.nc.semaphore(f"{self.name}_{name}"))

    def block(self):
        return self.stack.enter_context(self.nc.Block())


def make_identity(pool, tile, cleared, done):
    n = tile.shape[0]
    pool.memset(tile[:, :], 0.0).then_inc(cleared, 1)
    pool.wait_ge(cleared, 1)
    pool.affine_select(out=tile[:, :], in_=tile[:, :], compare_op=ALU.not_equal, fill=1.0, base=0,
                       pattern=[[-1, n]], channel_multiplier=1).then_inc(done, 1)


def phase_project(nc, x, wq, bq, wk, bk, wv, bv, qk_dram, v_dram, q_keep):
    with Phase(nc, "pr") as ph:
        ident = ph.sb("ident", [P, P], F32)
        w_qk = ph.sb("w_qk", [HALF, 2, 3, P], F32)
        w_v = ph.sb("w_v", [HALF, 2, C], F32)
        b_qk = ph.sb("b_qk", [P, 3], F32)
        s_qk = ph.sb("s_qk", [P, 3], F32)
        b_v = ph.sb("b_v", [P, C], F32)
        half_neg = ph.sb("half_neg", [P, TILES], F32)
        eps = ph.sb("eps", [P, TILES], F32)
        x_in = [ph.sb(f"x_in{s}", [P, TILES, C], F32) for s in range(2)]
        x_n = [ph.sb(f"x_n{s}", [P, TILES, C], F32) for s in range(2)]
        x_t = [ph.sb(f"x_t{s}", [HALF, 2, GROUP], F32) for s in range(2)]
        stats = [ph.sb(f"stats{s}", [P, TILES, 6], F32) for s in range(2)]
        meanvar = [ph.sb(f"meanvar{s}", [P, TILES, 2], F32) for s in range(2)]
        var_eps = [ph.sb(f"var_eps{s}", [P, TILES], F32) for s in range(2)]
        rstd = [ph.sb(f"rstd{s}", [P, 3, TILES], F32) for s in range(2)]
        k_f32 = [ph.sb(f"k_f32{s}", [P, GROUP], F32) for s in range(2)]
        parts = [ph.sb(f"parts{s}", [P, 3, 2, GROUP], F16) for s in range(2)]
        v_st = [ph.sb(f"v_st{s}", [P, TILES, NH, SLOT], F32) for s in range(2)]
        t_ps = ph.ps("t_ps", [P, 2, GROUP], F32)
        qk_ps = [ph.ps(f"qk_ps{c}", [P, GROUP], F32) for c in range(3)]
        v_ps = ph.ps("v_ps", [P, TILES, 256], F32)

        weights_in = ph.sem("weights_in")
        zeroed, ident_made, consts_made, pool_consts = (ph.sem(n) for n in ("zeroed", "ident_made", "consts_made", "pool_consts"))
        x_loaded = [ph.sem(f"x_loaded{s}") for s in range(2)]
        stored = [ph.sem(f"stored{s}") for s in range(2)]
        stats_done, aggr_done, eps_done, pow_done = (ph.sem(n) for n in ("stats_done", "aggr_done", "eps_done", "pow_done"))
        newton, xn_done, xt_ready, t_done = (ph.sem(n) for n in ("newton", "xn_done", "xt_ready", "t_done"))
        qk_done, v_done, f32_done, hi_done, lo_done, v_out = (
            ph.sem(n) for n in ("qk_done", "v_done", "f32_done", "hi_done", "lo_done", "v_out"))
        n_weights, per_group = 10, 9
        block = ph.block()
        x_v = x.rearrange("(n t p) c -> n p t c", t=TILES, p=P)

        @block.sync
        def _(sp):
            def load(n, s):
                sp.dma_start(x_in[s][:, :, :], x_v[bass.ds(n, 1), :, :, :].rearrange("n p t c -> (n p) t c")).then_inc(x_loaded[s], 16)

            load(0, 0)
            load(1, 1)
            for w, c0, c1, q0 in ((wq, 0, P, 0), (wk, 0, P, 1)):
                sp.dma_start(w_qk[:, :, q0, :], w[:, c0:c1].rearrange("(h p) c -> p h c", h=2)).then_inc(weights_in, 16)
            for w, b, at in ((wq, bq, 0), (wk, bk, QC)):
                sp.dma_start(w_qk[:, :, 2, at:at + QC], w[:, P:C].rearrange("(h p) c -> p h c", h=2)).then_inc(weights_in, 16)
                sp.dma_start(b_qk[at:at + QC, 2:3], b[P:C].rearrange("(p o) -> p o", o=1)).then_inc(weights_in, 16)
            for b, q0 in ((bq, 0), (bk, 1)):
                sp.dma_start(b_qk[:, q0:q0 + 1], b[0:P].rearrange("(p o) -> p o", o=1)).then_inc(weights_in, 16)
            sp.dma_start(w_v[:, :, :], wv.rearrange("(h p) c -> p h c", h=2)).then_inc(weights_in, 16)
            sp.dma_start(b_v[:, :], bv.partition_broadcast(P)).then_inc(weights_in, 16)
            def emit(b, last):
                for s in range(2):
                    n = b * 2 + s
                    if not last:
                        sp.wait_ge(xn_done, n + 1)
                        load(n + 2, s)
                    for c in range(3):
                        sp.wait_ge(hi_done, n * 3 + c + 1)
                        sp.wait_ge(lo_done, n * 3 + c + 1)
                        for half in range(2):
                            which, quad = ((c, half), (half, 2))[c == 2]
                            dst = qk_dram[bass.ds(b * NQUAD + quad, 1), which, :, :, s * GROUP:(s + 1) * GROUP]
                            sp.dma_start(dst.rearrange("u r h t -> (u r) h t"),
                                         parts[s][half * QC:(half + 1) * QC, c, :, :]).then_inc(stored[s], 16)
                    sp.wait_ge(v_out, n + 1)
                    for quad in range(NQUAD):
                        dst = v_dram[bass.ds(b * NQUAD + quad, 1), :, s * TILES:(s + 1) * TILES, :]
                        sp.dma_start(dst.rearrange("u p t e -> (u p) t e"),
                                     v_st[s][:, :, quad * QUAD:(quad + 1) * QUAD, :].rearrange("p t h e -> p t (h e)")).then_inc(stored[s], 16)

            with sp.Fori(0, BATCH - 1) as b:
                emit(b, False)
            emit(BATCH - 1, True)
            for s in range(2):
                sp.wait_ge(stored[s], 16 * per_group * BATCH)

        @block.gpsimd
        def _(pool):
            make_identity(pool, ident, zeroed, ident_made)
            pool.memset(eps[:, :], 1e-6).then_inc(pool_consts, 1)
            pool.memset(half_neg[:, :], -0.5).then_inc(pool_consts, 1)
            pool.wait_ge(pool_consts, 2)
            def emit(b):
                for s in range(2):
                    n = b * 2 + s
                    pool.wait_ge(aggr_done, n + 1)
                    pool.tensor_tensor(out=var_eps[s][:, :], in0=meanvar[s][:, :, 1], in1=eps[:, :], op=ALU.add).then_inc(eps_done, 1)
                    pool.wait_ge(eps_done, n + 1)
                    pool.tensor_tensor(out=rstd[s][:, 0, :], in0=var_eps[s][:, :], in1=half_neg[:, :], op=ALU.pow).then_inc(pow_done, 1)
                    for c in range(3):
                        src = k_f32[s][:, :] if c == 1 else q_keep[:, c // 2, bass.ds(n * GROUP, GROUP)]
                        pool.wait_ge(hi_done, n * 3 + c + 1)
                        pool.tensor_tensor(out=parts[s][:, c, 1, :], in0=src, in1=parts[s][:, c, 0, :], op=ALU.subtract).then_inc(lo_done, 1)

            each_pass(pool, BATCH, emit)

        @block.vector
        def _(dve):
            def normalise(n, s, it):
                dve.wait_ge(x_loaded[s], 16 * (it + 1))
                for t in range(TILES):
                    last = dve.bn_stats(stats[s][:, t, :], x_in[s][:, t, :])
                last.then_inc(stats_done, 1)
                dve.wait_ge(stats_done, n + 1)
                dve.memset(rstd[s][:, 1, :], 0.0)
                for t in range(TILES):
                    last = dve.bn_aggr(meanvar[s][:, t, :], stats[s][:, t, :])
                last.then_inc(aggr_done, 1)
                dve.wait_ge(pow_done, n + 1)
                r0, r1, r2 = (rstd[s][:, i, :] for i in range(3))
                dve.tensor_tensor(r1, r0, r0, ALU.mult).then_inc(newton, 1)
                dve.wait_ge(newton, n * 3 + 1)
                dve.scalar_tensor_tensor(out=r2, in0=r1, scalar=-0.5, in1=var_eps[s][:, :], op0=ALU.mult, op1=ALU.mult).then_inc(newton, 1)
                dve.wait_ge(newton, n * 3 + 2)
                dve.scalar_tensor_tensor(out=r1, in0=r2, scalar=1.5, in1=r0, op0=ALU.add, op1=ALU.mult).then_inc(newton, 1)
                dve.wait_ge(newton, n * 3 + 3)
                for t in range(TILES):
                    last = dve.tensor_scalar(x_n[s][:, t, :], x_in[s][:, t, :], meanvar[s][:, t, 0:1], rstd[s][:, 1, t:t + 1],
                                             ALU.subtract, ALU.mult)
                last.then_inc(xn_done, 1)

            dve.wait_ge(weights_in, 16 * n_weights)
            dve.memset(s_qk[:, :], 1.0).then_inc(consts_made, 1)
            dve.wait_ge(consts_made, 1)
            dve.memset(s_qk[:, 1:2], HD ** -0.5).then_inc(consts_made, 1)
            dve.memset(s_qk[QC:P, 2:3], HD ** -0.5).then_inc(consts_made, 1)
            for s in range(2):
                dve.memset(v_st[s][:, :, :, :], 1.0).then_inc(consts_made, 1)
            dve.wait_ge(consts_made, 5)
            def emit(b):
                for s in range(2):
                    n = b * 2 + s
                    normalise(n, s, b)
                    for c in range(3):
                        dst = k_f32[s][:, :] if c == 1 else q_keep[:, c // 2, bass.ds(n * GROUP, GROUP)]
                        dve.wait_ge(qk_done, n * 3 + c + 1)
                        dve.tensor_scalar(dst, qk_ps[c][:, :], b_qk[:, c:c + 1], s_qk[:, c:c + 1], ALU.add, ALU.mult).then_inc(f32_done, 1)
                    dve.wait_ge(v_done, n + 1)
                    need(dve, stored[s], b * (16 * per_group))
                    bias = b_v[:, :].rearrange("p (o h d) -> p o h d", o=1, d=HD)
                    for t in range(TILES):
                        last = dve.tensor_tensor(v_st[s][:, t, :, 0:HD], v_ps[:, t, 0:C].rearrange("p (h d) -> p h d", d=HD),
                                                 bias[:, 0, :, :], ALU.add)
                    last.then_inc(v_out, 1)

            each_pass(dve, BATCH, emit)

        @block.scalar
        def _(act):
            def emit(b):
                for s in range(2):
                    n = b * 2 + s
                    act.wait_ge(t_done, n + 1)
                    act.activation(x_t[s][:, :, :], t_ps[0:HALF, :, :], ACT.Copy).then_inc(xt_ready, 1)
                    for c in range(3):
                        src = k_f32[s][:, :] if c == 1 else q_keep[:, c // 2, bass.ds(n * GROUP, GROUP)]
                        act.wait_ge(f32_done, n * 3 + c + 1)
                        if c == 0:
                            need(act, stored[s], b * (16 * per_group))
                        act.activation(parts[s][:, c, 0, :], src, ACT.Copy).then_inc(hi_done, 1)

            each_pass(act, BATCH, emit)

        @block.tensor
        def _(pe):
            pe.wait_ge(ident_made, 1)
            pe.wait_ge(weights_in, 16 * n_weights)
            def emit(b):
                for s in range(2):
                    n = b * 2 + s
                    pe.wait_ge(xn_done, n + 1)
                    need(pe, xt_ready, n)
                    for t in range(TILES):
                        for h in range(2):
                            last = pe.transpose(t_ps[0:HALF, h, t * P:(t + 1) * P], x_n[s][:, t, h * HALF:(h + 1) * HALF], ident[:, :])
                    last.then_inc(t_done, 1)
                    pe.wait_ge(xt_ready, n + 1)
                    need(pe, f32_done, n * 3)
                    for c in range(3):
                        for h in range(2):
                            last = pe.matmul(qk_ps[c][:, :], w_qk[:, h, c, :], x_t[s][:, h, :], start=(h == 0), stop=(h == 1))
                        last.then_inc(qk_done, 1)
                    need(pe, v_out, n)
                    for t in range(TILES):
                        for h in range(2):
                            last = pe.matmul(v_ps[:, t, 0:C], x_t[s][:, h, t * P:(t + 1) * P], w_v[:, h, :], start=(h == 0), stop=(h == 1))
                    last.then_inc(v_done, 1)

            each_pass(pe, BATCH, emit)


def phase_rel_bias(nc, rel_h, rel_w, bias_dram, q_keep):
    PER = 8
    RING = 4
    with Phase(nc, "rb") as ph:
        rel = [ph.sb(f"rel{t}", [P, REL, QUAD], F32) for t in range(2)]
        rel_rows = [ph.sb(f"rel_rows{t}", [P, REL], F32) for t in range(2)]
        own2 = ph.sb("own2", [P, 2, QUAD], F32)
        own = ph.sb("own", [P, QUAD], F32)
        stage = [ph.sb(f"stage{i}", [P, 2, BATCH, SEQ], F16) for i in range(2)]
        b_ps = [ph.ps(f"b_ps{i}", [P, PER, BATCH, GRID], F32) for i in range(RING)]
        mask_step, rel_in, rel_made, mm_done, hi_done, lo_done = (
            ph.sem(n) for n in ("mask_step", "rel_in", "rel_made", "mm_done", "hi_done", "lo_done"))
        own_made = ph.sem("own_made")
        stored = [ph.sem(f"stored{i}") for i in range(2)]
        block = ph.block()
        work = [(quad, t) for quad in range(NQUAD) for t in range(2)]
        chunks = GRID // PER

        @block.gpsimd
        def _(pool):
            pool.memset(own2[:, :, :], 1.0).then_inc(mask_step, 1)
            pool.wait_ge(mask_step, 1)
            pool.affine_select(out=own2[:, :, :], in_=own2[:, :, :], compare_op=ALU.is_ge, fill=0.0, base=0,
                               pattern=[[-QC, 2], [-HD, QUAD]], channel_multiplier=1).then_inc(mask_step, 1)
            pool.wait_ge(mask_step, 2)
            pool.affine_select(out=own2[:, :, :], in_=own2[:, :, :], compare_op=ALU.is_ge, fill=0.0, base=HD - 1,
                               pattern=[[QC, 2], [HD, QUAD]], channel_multiplier=-1).then_inc(mask_step, 1)

        @block.sync
        def _(sp):
            for t, src in enumerate((rel_h, rel_w)):
                for r in range(0, P, HD):
                    sp.dma_start(rel_rows[t][r:r + HD, :], src).then_inc(rel_in, 16)
            for i, (quad, t) in enumerate(work):
                sp.wait_ge(hi_done, (i + 1) * chunks)
                sp.wait_ge(lo_done, (i + 1) * chunks)
                for part in range(2):
                    dst = bias_dram.rearrange("(b g) h t r q -> g h t r b q", g=NQUAD)[quad, part, t]
                    sp.dma_start(dst, stage[i % 2][:, part, :, :]).then_inc(stored[i % 2], 16)
            for i in range(2):
                sp.wait_ge(stored[i], 16 * len(work))

        @block.tensor
        def _(pe):
            pe.wait_ge(rel_made, 1)
            for i, (quad, t) in enumerate(work):
                base = QC if quad == 1 else 0
                q = q_keep[base:base + QC, quad // 2, :].rearrange("p (b r c) -> p b r c", b=BATCH, c=GRID)
                for ch in range(chunks):
                    k = i * chunks + ch
                    need(pe, lo_done, k - RING + 1)
                    for j in range(PER):
                        at = ch * PER + j
                        rhs = q[:, :, at, :] if t == 0 else q[:, :, :, at]
                        last = pe.matmul(b_ps[k % RING][:, j, :, :], rel[t][base:base + QC, GRID - 1 - at:REL - at, :].rearrange("p r h -> p (r h)"),
                                         rhs, start=True, stop=True)
                    last.then_inc(mm_done, 1)

        def spot(i, t, ch, part):
            st = stage[i % 2][:, part, :, :]
            if t == 0:
                return st.rearrange("p b (r c) -> p r b c", c=GRID)[:, ch * PER:(ch + 1) * PER]
            return st.rearrange("p b (r c) -> p c b r", c=GRID)[:, ch * PER:(ch + 1) * PER]

        @block.scalar
        def _(act):
            for i, (quad, t) in enumerate(work):
                need(act, stored[i % 2], 32 * (i // 2))
                for ch in range(chunks):
                    k = i * chunks + ch
                    act.wait_ge(mm_done, k + 1)
                    act.activation(spot(i, t, ch, 0), b_ps[k % RING][:, :, :, :], ACT.Copy).then_inc(hi_done, 1)

        @block.vector
        def _(dve):
            dve.wait_ge(mask_step, 3)
            dve.tensor_tensor(own[:, :], own2[:, 0, :], own2[:, 1, :], ALU.add).then_inc(own_made, 1)
            dve.wait_ge(own_made, 1)
            dve.wait_ge(rel_in, 16 * 2 * (P // HD))
            for t in range(2):
                for head in range(QUAD):
                    last = dve.tensor_scalar(rel[t][:, :, head], rel_rows[t][:, :], own[:, head:head + 1], None, ALU.mult)
            last.then_inc(rel_made, 1)
            for i, (quad, t) in enumerate(work):
                for ch in range(chunks):
                    k = i * chunks + ch
                    dve.wait_ge(hi_done, k + 1)
                    dve.tensor_tensor(spot(i, t, ch, 1), b_ps[k % RING][:, :, :, :], spot(i, t, ch, 0), ALU.subtract).then_inc(lo_done, 1)


def phase_attention(nc, qk_dram, v_dram, bias_dram, out_dram):
    STEPS = 2 * KT
    LAG = 2
    PRING = 4
    PIECES = QUAD * KT * 2
    PER_STEP = 5
    N_LOADS = 13
    with Phase(nc, "at") as ph:
        mix_q = [ph.sb(f"mix_q{i}", [P, QUAD, SEQ], F16) for i in range(3)]
        mix_k = [ph.sb(f"mix_k{i}", [P, QUAD, SEQ], F16) for i in range(3)]
        lo_q = [ph.sb(f"lo_q{i}", [NLO, QUAD, SEQ], F16) for i in range(3)]
        lo_k = ph.sb("lo_k", [NLO, SEQ], F16)
        v_u = [ph.sb(f"v_u{i}", [P, KT, QUAD, SLOT], F32) for i in range(3)]
        probs = [ph.sb(f"probs{i}", [P, QUAD, GROUP], F32) for i in range(PRING)]
        ident = ph.sb("ident", [P, P], F32)
        sum_pick = ph.sb("sum_pick", [P, QUAD], F32)
        piece_max = ph.sb("piece_max", [P, PIECES], F32)
        row_max = ph.sb("row_max", [P, QUAD * KT], F32)
        neg_max = ph.sb("neg_max", [QUAD * KT, 2, P], F16)
        o_sb = [ph.sb(f"o_sb{i}", [P, GROUP], F32) for i in range(2)]
        inv = ph.sb("inv", [P, TILES * QUAD], F32)
        inv_wide = ph.sb("inv_wide", [P, TILES * QUAD, SLOT], F32)
        o_n = [ph.sb(f"o_n{i}", [P, GROUP], F32) for i in range(2)]
        s_ps = [ph.ps(f"s_ps{i}", [P, 2, GROUP], F32) for i in range(2)]
        m_ps = [ph.ps(f"m_ps{i}", [P, GROUP], F32) for i in range(2)]
        o_ps = ph.ps("o_ps", [P, GROUP], F32)
        x_ps = ph.ps("x_ps", [P, GROUP], F32)

        consts, const_step, hot_out = ph.sem("consts"), ph.sem("const_step"), ph.sem("hot_out")
        loaded = [ph.sem(f"loaded{i}") for i in range(3)]
        max_loaded = [ph.sem(f"max_loaded{i}") for i in range(3)]
        scores_done, exp_done, pv_done = (ph.sem(n) for n in ("scores_done", "exp_done", "pv_done"))
        piece_done, reduced = ph.sem("piece_done"), ph.sem("reduced")
        max_done, max_turned, neg_hi, neg_done = (ph.sem(n) for n in ("max_done", "max_turned", "neg_hi", "neg_done"))
        o_out, sums_done, inv_done, wide_done, spread_done, norm_done = (
            ph.sem(n) for n in ("o_out", "sums_done", "inv_done", "wide_done", "spread_done", "norm_done"))
        o_stored = [ph.sem(f"o_stored{i}") for i in range(2)]
        block = ph.block()

        class Unit:

            def __init__(self, u, image, static):
                self.u, self.image, self.buf = u, image, static % 3
                self.quad = static % NQUAD
                self.turn = image
                self.first, self.last = isinstance(u, int) and u == 0, isinstance(u, int) and u == UNITS - 1

            def after(self, k):
                static = self.buf + k
                return Unit(self.u + k, self.image + static // 3, static)

        def each_unit(eng, emit):
            emit(Unit(0, 0, 0))
            with eng.Fori(0, 3) as r:
                for k in range(1, 4):
                    emit(Unit(r * 3 + k, r + k // 3, k))
            for u in (UNITS - 2, UNITS - 1):
                emit(Unit(u, u // 3, u))

        def pieces(n):
            return range(min(n * PER_STEP, PIECES), min((n + 1) * PER_STEP, PIECES))

        MAX_AT = -(-PIECES // PER_STEP)
        TURN_AT = MAX_AT + 1
        O_AT = (LAG - 1, KT + LAG - 1)
        SUMS_AT = (O_AT[0] + 1, O_AT[1] + 1)
        SPREAD_AT = (SUMS_AT[0] + 1, SUMS_AT[1] + 1)
        assert SPREAD_AT[0] < SUMS_AT[1] and SPREAD_AT[1] < TURN_AT < STEPS

        @block.gpsimd
        def _(pool):
            make_identity(pool, ident, const_step, consts)
            pool.memset(sum_pick[:, :], 0.0).then_inc(const_step, 1)
            pool.memset(lo_k[:, :], 0.0).then_inc(const_step, 1)
            pool.wait_ge(const_step, 3)
            pool.affine_select(out=sum_pick[:, :], in_=sum_pick[:, :], compare_op=ALU.not_equal, fill=1.0, base=-HD,
                               pattern=[[-SLOT, QUAD]], channel_multiplier=1).then_inc(consts, 1)
            hot = lo_k[0:2 * GRID, :].rearrange("p (r c) -> p r c", c=GRID)
            pool.affine_select(out=hot, in_=hot, compare_op=ALU.not_equal, fill=1.0, base=0,
                               pattern=[[-1, GRID], [0, GRID]], channel_multiplier=1).then_inc(const_step, 1)
            pool.wait_ge(const_step, 4)
            pool.affine_select(out=hot, in_=hot, compare_op=ALU.not_equal, fill=1.0, base=-GRID,
                               pattern=[[0, GRID], [-1, GRID]], channel_multiplier=1).then_inc(const_step, 1)
            pool.memset(lo_k[2 * GRID:NLO, :], 1.0).then_inc(const_step, 1)
            pool.wait_ge(const_step, 6)
            for i in range(3):
                for j in range(QUAD):
                    pool.dma_start(mix_k[i][2 * GRID:P, j, :], lo_k[0:2 * GRID, :]).then_inc(hot_out, 16)
            pool.wait_ge(hot_out, 16 * 3 * QUAD)
            pool.nop().then_inc(consts, 1)

        @block.sync
        def _(sp):
            def load(unit):
                u, i = unit.u, unit.buf

                def q_or_k(which, part):
                    src = qk_dram[bass.ds(u, 1), which, :, part, :]
                    return src.rearrange("u (j d) t -> (u d) j t", d=HD)

                for r, part in enumerate((0, 0, 1, 1)):
                    sp.dma_start(mix_q[i][r * HD:(r + 1) * HD, :, :], q_or_k(0, part)).then_inc(loaded[i], 16)
                for r, part in enumerate((0, 1, 0, 1)):
                    sp.dma_start(mix_k[i][r * HD:(r + 1) * HD, :, :], q_or_k(1, part)).then_inc(loaded[i], 16)
                for t in range(2):
                    for part, dst in ((0, mix_q[i][(2 + t) * GRID:(3 + t) * GRID, :, :]), (1, lo_q[i][t * GRID:(t + 1) * GRID, :, :])):
                        src = bias_dram[bass.ds(u, 1), part, t, :, :].rearrange("u (r j) q -> (u r) j q", j=QUAD)
                        sp.dma_start(dst, src).then_inc(loaded[i], 16)
                sp.dma_start(v_u[i][:, :, :, :].rearrange("p k h e -> p k (h e)"),
                             v_dram[bass.ds(u, 1), :, :, :].rearrange("u p k e -> (u p) k e")).then_inc(loaded[i], 16)

            def load_max(unit):
                sp.wait_ge(neg_done, unit.u + 1)
                for part in range(2):
                    sp.dma_start(lo_q[unit.buf][2 * GRID + part:2 * GRID + part + 1, :, :].rearrange("o j (t p) -> o (j t) p", p=P),
                                 neg_max[:, part, :]).then_inc(max_loaded[unit.buf], 16)

            def store(unit, half):
                sp.wait_ge(norm_done, unit.u * 2 + half + 1)
                dst = out_dram[bass.ds(unit.image * 2 + half, 1), :, unit.quad, :].rearrange("n p t -> (n p) t")
                sp.dma_start(dst, o_n[half][:, :]).then_inc(o_stored[half], 16)

            load(Unit(0, 0, 0))
            load(Unit(1, 0, 1))
            load_max(Unit(0, 0, 0))

            def emit(unit):
                if not (isinstance(unit.u, int) and unit.u + 2 >= UNITS):
                    need(sp, pv_done, unit.u * STEPS)
                    load(unit.after(2))
                if not unit.first:
                    store(unit.after(-1), 1)
                store(unit, 0)
                if not unit.last:
                    load_max(unit.after(1))

            each_unit(sp, emit)
            store(Unit(UNITS - 1, BATCH - 1, UNITS - 1), 1)
            for half in range(2):
                sp.wait_ge(o_stored[half], 16 * UNITS)

        @block.tensor
        def _(pe):
            def piece(unit, i):
                j, qt, kh = i // (2 * KT), i // 2 % KT, i % 2
                need(pe, reduced, unit.u * PIECES + i - 1)
                pe.matmul(m_ps[i % 2][:, :], mix_q[unit.buf][:, j, qt * P:(qt + 1) * P],
                          mix_k[unit.buf][:, j, kh * GROUP:(kh + 1) * GROUP], start=True, stop=True).then_inc(piece_done, 1)

            def turn(unit):
                pe.wait_ge(max_done, unit.u + 1)
                need(pe, norm_done, unit.u * 2 - 1)
                pe.transpose(x_ps[0:QUAD * KT, 0:P], row_max[:, :], ident[:, :]).then_inc(max_turned, 1)

            def scores(unit, n, j):
                half, kt = divmod(n, KT)
                pair = j // 2
                step = unit.u * STEPS + n
                if j % 2 == 0:
                    need(pe, exp_done, step * 2 + pair - 1)
                keys, queries = slice(kt * P, (kt + 1) * P), slice(half * GROUP, (half + 1) * GROUP)
                pe.matmul(s_ps[pair][:, j % 2, :], mix_k[unit.buf][:, j, keys], mix_q[unit.buf][:, j, queries], start=True, stop=False)
                last = pe.matmul(s_ps[pair][:, j % 2, :], lo_k[:, keys], lo_q[unit.buf][:, j, queries], start=False, stop=True)
                if j % 2 == 1:
                    last.then_inc(scores_done, 1)

            def weigh(unit, n):
                half, kt = divmod(n, KT)
                step = unit.u * STEPS + n
                pe.wait_ge(exp_done, step * 2 + 2)
                if kt == 0:
                    need(pe, o_out, unit.u * 2 + half)
                for j in range(QUAD):
                    last = pe.matmul(o_ps[j * SLOT:(j + 1) * SLOT, :], v_u[unit.buf][:, kt, j, :], probs[n % PRING][:, j, :],
                                     start=(kt == 0), stop=(kt == KT - 1), tile_position=(0, j * SLOT))
                last.then_inc(pv_done, 1)

            def sums(unit, half):
                pe.wait_ge(o_out, unit.u * 2 + half + 1)
                need(pe, norm_done, unit.u * 2 + half)
                if half == 1 and not unit.last:
                    pe.wait_ge(neg_done, unit.u + 2)
                for t in range(TILES):
                    last = pe.matmul(x_ps[:, t * QUAD:(t + 1) * QUAD], o_sb[half][:, t * P:(t + 1) * P], sum_pick[:, :], start=True, stop=True)
                last.then_inc(sums_done, 1)

            def spread(unit, half):
                pe.wait_ge(wide_done, unit.u * 2 + half + 1)
                for t in range(TILES):
                    last = pe.transpose(x_ps[:, t * P:(t + 1) * P],
                                        inv_wide[:, t * QUAD:(t + 1) * QUAD, :].rearrange("p h r -> p (h r)"), ident[:, :])
                last.then_inc(spread_done, 1)

            pe.wait_ge(consts, 3)
            first = Unit(0, 0, 0)
            pe.wait_ge(loaded[0], 16 * N_LOADS)
            for i in range(PIECES):
                piece(first, i)
            turn(first)

            def emit(unit):
                nxt = unit.after(1)
                pe.wait_ge(max_loaded[unit.buf], (unit.turn + 1) * 32)
                if not unit.last:
                    pe.wait_ge(loaded[nxt.buf], (nxt.turn + 1) * (16 * N_LOADS))
                for n in range(STEPS):
                    todo = [] if unit.last else list(pieces(n))
                    for j in range(QUAD):
                        scores(unit, n, j)
                        for i in todo[j:j + 1]:
                            piece(nxt, i)
                    if n >= LAG:
                        weigh(unit, n - LAG)
                    elif not unit.first:
                        weigh(unit.after(-1), STEPS + n - LAG)
                    for i in todo[QUAD:]:
                        piece(nxt, i)
                    for half, owner in ((1, None if unit.first else unit.after(-1)), (0, unit)):
                        if owner and n == SUMS_AT[1 - half]:
                            sums(owner, half)
                        if owner and n == SPREAD_AT[1 - half]:
                            spread(owner, half)
                    if n == TURN_AT and not unit.last:
                        turn(nxt)

            each_unit(pe, emit)
            last = Unit(UNITS - 1, BATCH - 1, UNITS - 1)
            for n in range(STEPS - LAG, STEPS):
                weigh(last, n)
            sums(last, 1)
            spread(last, 1)

        @block.scalar
        def _(act):
            def exps(unit, n):
                step = unit.u * STEPS + n
                need(act, pv_done, step - PRING + 1)
                for pair in range(2):
                    act.wait_ge(scores_done, step * 2 + pair + 1)
                    act.activation(probs[n % PRING][:, 2 * pair:2 * pair + 2, :], s_ps[pair][:, :, :], ACT.Exp).then_inc(exp_done, 1)

            def take_out(unit, half):
                act.wait_ge(pv_done, unit.u * STEPS + (half + 1) * KT)
                need(act, norm_done, unit.u * 2 + half - 1)
                act.activation(o_sb[half][:, :], o_ps[:, :], ACT.Copy).then_inc(o_out, 1)

            def emit(unit):
                for n in range(STEPS):
                    exps(unit, n)
                    if n == O_AT[0] and not unit.first:
                        take_out(unit.after(-1), 1)
                    if n == O_AT[1]:
                        take_out(unit, 0)

            each_unit(act, emit)
            take_out(Unit(UNITS - 1, BATCH - 1, UNITS - 1), 1)

        @block.vector
        def _(dve):
            def reduce_piece(unit, i):
                dve.wait_ge(piece_done, unit.u * PIECES + i + 1)
                dve.tensor_reduce(piece_max[:, i:i + 1], m_ps[i % 2][:, :], AX_X, ALU.max).then_inc(reduced, 1)

            def join_max(unit):
                dve.wait_ge(reduced, (unit.u + 1) * PIECES)
                need(dve, max_turned, unit.u)
                halves = piece_max[:, :].rearrange("p (r k) -> p r k", k=2)
                dve.tensor_tensor(row_max[:, :], halves[:, :, 0], halves[:, :, 1], ALU.max).then_inc(max_done, 1)

            def negate(unit):
                dve.wait_ge(max_turned, unit.u + 1)
                if not unit.first:
                    prev = unit.after(-1)
                    dve.wait_ge(max_loaded[prev.buf], (prev.turn + 1) * 32)
                turned = x_ps[0:QUAD * KT, 0:P]
                dve.tensor_scalar(neg_max[:, 0, :], turned, -1.0, None, ALU.mult).then_inc(neg_hi, 1)
                dve.wait_ge(neg_hi, unit.u + 1)
                dve.scalar_tensor_tensor(out=neg_max[:, 1, :], in0=turned, scalar=-1.0, in1=neg_max[:, 0, :],
                                         op0=ALU.mult, op1=ALU.subtract).then_inc(neg_done, 1)

            def invert(unit, half):
                dve.wait_ge(sums_done, unit.u * 2 + half + 1)
                dve.reciprocal(inv[:, :], x_ps[:, 0:TILES * QUAD]).then_inc(inv_done, 1)
                dve.wait_ge(inv_done, unit.u * 2 + half + 1)
                need(dve, spread_done, unit.u * 2 + half)
                dve.tensor_copy(inv_wide[:, :, :], inv[:, :].unsqueeze(2).to_broadcast([P, TILES * QUAD, SLOT])).then_inc(wide_done, 1)

            def normalise(unit, half):
                dve.wait_ge(spread_done, unit.u * 2 + half + 1)
                need(dve, o_stored[half], unit.u * 16)
                dve.tensor_tensor(o_n[half][:, :], o_sb[half][:, :], x_ps[:, :], ALU.mult).then_inc(norm_done, 1)

            first = Unit(0, 0, 0)
            for i in range(PIECES):
                reduce_piece(first, i)
            join_max(first)
            negate(first)

            def emit(unit):
                nxt = unit.after(1)
                for n in range(STEPS):
                    if not unit.last:
                        for i in pieces(n):
                            reduce_piece(nxt, i)
                        if n == MAX_AT:
                            join_max(nxt)
                    for half, owner in ((1, None if unit.first else unit.after(-1)), (0, unit)):
                        if owner and n == SUMS_AT[1 - half]:
                            invert(owner, half)
                        if owner and n == SPREAD_AT[1 - half]:
                            normalise(owner, half)
                    if n == TURN_AT and not unit.last:
                        negate(nxt)

            each_unit(dve, emit)
            last = Unit(UNITS - 1, BATCH - 1, UNITS - 1)
            invert(last, 1)
            normalise(last, 1)


def phase_ffn(nc, x, wp, bp, w1, b1, aw1, aa1, w2, b2, aw2, aw2_cols, aa2, att_dram, out):
    with Phase(nc, "ff") as ph:
        ident = ph.sb("ident", [P, P], BF16)
        wp_sb = ph.sb("wp_sb", [P, NQUAD, C], F32)
        bp_row = ph.sb("bp_row", [P, C], F32)
        b2_row = ph.sb("b2_row", [P, C], F32)
        s2_row = ph.sb("s2_row", [P, C], F32)
        s1 = ph.sb("s1", [P, HT], F32)
        b1_sb = ph.sb("b1_sb", [P, HT], F32)
        aw1_sb = ph.sb("aw1_sb", [P, HT], F32)
        aw2_sb = ph.sb("aw2_sb", [HALF, 2], F32)
        aa1_row = ph.sb("aa1_row", [P, C], F32)
        aa2_row = ph.sb("aa2_row", [P, HID], F32)
        step = ph.sb("step", [P, 6], F32)
        inv_w1 = ph.sb("inv_w1", [P, HT], F32)
        inv_w2 = ph.sb("inv_w2", [HALF, 2], F32)
        w1_f = ph.sb("w1_f", [P, HT, C], F32)
        w1_g = ph.sb("w1_g", [P, HT, C], F32)
        w1_q = ph.sb("w1_q", [P, HT, C], BF16)
        w2_f = ph.sb("w2_f", [HALF, 2, HID], F32)
        w2_g = ph.sb("w2_g", [HALF, 2, HID], F32)
        w2_q = ph.sb("w2_q", [HALF, 2, HID], BF16)
        w1_t = ph.sb("w1_t", [HALF, 2, HID], BF16)
        w2_t = ph.sb("w2_t", [P, HT, C], BF16)
        half_neg = ph.sb("half_neg", [P, TILES], F32)
        eps = ph.sb("eps", [P, TILES], F32)
        x_in = [ph.sb(f"x_in{s}", [P, TILES, C], F32) for s in range(2)]
        att = [ph.sb(f"att{s}", [P, NQUAD, GROUP], F32) for s in range(2)]
        y = [ph.sb(f"y{s}", [P, TILES, C], F32) for s in range(2)]
        y_b = [ph.sb(f"y_b{s}", [P, TILES, C], F32) for s in range(2)]
        stats = [ph.sb(f"stats{s}", [P, TILES, 6], F32) for s in range(2)]
        meanvar = [ph.sb(f"meanvar{s}", [P, TILES, 2], F32) for s in range(2)]
        var_eps = [ph.sb(f"var_eps{s}", [P, TILES], F32) for s in range(2)]
        rstd = [ph.sb(f"rstd{s}", [P, 3, TILES], F32) for s in range(2)]
        y_n = ph.sb("y_n", [P, TILES, C], F32)
        y_r = ph.sb("y_r", [P, TILES, C], F32)
        y_q = [ph.sb(f"y_q{s}", [P, TILES, C], BF16) for s in range(2)]
        y_t = [ph.sb(f"y_t{s}", [HALF, 2, GROUP], BF16) for s in range(2)]
        hid = [ph.sb(f"hid{s}", [P, HT, GROUP], F32) for s in range(2)]
        hid_r = ph.sb("hid_r", [P, HT, GROUP], F32)
        hid_q = [ph.sb(f"hid_q{s}", [P, HT, GROUP], BF16) for s in range(2)]
        res = [ph.sb(f"res{s}", [P, TILES, C], F32) for s in range(2)]
        p_ps = ph.ps("p_ps", [P, TILES, 256], F32)
        t_ps = ph.ps("t_ps", [P, 2, GROUP], BF16)
        h_ps = [ph.ps(f"h_ps{i}", [P, GROUP], F32) for i in range(3)]
        f_ps = ph.ps("f_ps", [P, TILES, 256], F32)

        zeroed, ident_made, wp_zeroed, pool_consts, params_in = (
            ph.sem(n) for n in ("zeroed", "ident_made", "wp_zeroed", "pool_consts", "params_in"))
        prep, w_turned, w_copied, ready = (ph.sem(n) for n in ("prep", "w_turned", "w_copied", "ready"))
        x_loaded = [ph.sem(f"x_loaded{s}") for s in range(2)]
        stored = [ph.sem(f"stored{s}") for s in range(2)]
        proj_done, y_done, stats_done, aggr_done, eps_done, pow_done, newton = (
            ph.sem(n) for n in ("proj_done", "y_done", "stats_done", "aggr_done", "eps_done", "pow_done", "newton"))
        yn_done, yr_done, yi_done, yq_done, t_done, yt_ready, yb_done = (
            ph.sem(n) for n in ("yn_done", "yr_done", "yi_done", "yq_done", "t_done", "yt_ready", "yb_done"))
        h_done, gelu_done, clip_done, round_done, bound_done, hq_done = (
            ph.sem(n) for n in ("h_done", "gelu_done", "clip_done", "round_done", "bound_done", "hq_done"))
        f_done, scaled, res_done = (ph.sem(n) for n in ("f_done", "scaled", "res_done"))
        block = ph.block()
        x_v = x.rearrange("(n t p) c -> n p t c", t=TILES, p=P)
        out_v = out.rearrange("(n t p) c -> n p t c", t=TILES, p=P)

        @block.sync
        def _(sp):
            def load(n, s):
                sp.dma_start(x_in[s][:, :, :], x_v[bass.ds(n, 1), :, :, :].rearrange("n p t c -> (n p) t c")).then_inc(x_loaded[s], 16)
                sp.dma_start(att[s][:, :, :], att_dram[bass.ds(n, 1), :, :, :].rearrange("n p g t -> (n p) g t")).then_inc(x_loaded[s], 16)

            small = [(w1_f[:, :, :], w1.rearrange("(t p) c -> p t c", p=P)), (w2_f[:, :, :], w2.rearrange("(h p) c -> p h c", h=2)),
                     (aw1_sb[:, :], aw1), (b1_sb[:, :], b1), (aw2_sb[:, :], aw2_cols), (bp_row[:, :], bp.partition_broadcast(P)),
                     (b2_row[:, :], b2.partition_broadcast(P)), (s2_row[:, :], aw2.partition_broadcast(P)),
                     (aa1_row[:, :], aa1.partition_broadcast(P)), (aa2_row[:, :], aa2.partition_broadcast(P))]
            for dst, src in small:
                sp.dma_start(dst, src).then_inc(params_in, 16)
            sp.wait_ge(wp_zeroed, 1)
            for quad in range(NQUAD):
                for head in range(QUAD):
                    r = (quad * QUAD + head) * HD
                    sp.dma_start(wp_sb[head * SLOT:head * SLOT + HD, quad, :], wp[r:r + HD, :]).then_inc(params_in, 16)
            load(0, 0)
            load(1, 1)
            with sp.Fori(0, GROUPS // 2 - 1) as it:
                for s in range(2):
                    n = it * 2 + s
                    sp.wait_ge(y_done, n + 1)
                    load(n + 2, s)
                    sp.wait_ge(res_done, n + 1)
                    sp.dma_start(out_v[bass.ds(n, 1), :, :, :].rearrange("n p t c -> (n p) t c"), res[s][:, :, :]).then_inc(stored[s], 16)
            for s in range(2):
                n = GROUPS - 2 + s
                sp.wait_ge(res_done, n + 1)
                sp.dma_start(out_v[n], res[s][:, :, :]).then_inc(stored[s], 16)
            for s in range(2):
                sp.wait_ge(stored[s], 16 * (GROUPS // 2))

        t_ps_w1 = [h_ps[0][:, :].bitcast(BF16)[:, 0:HID], h_ps[1][:, :].bitcast(BF16)[:, 0:HID]]
        t_ps_w2 = f_ps[:, :, :].rearrange("p t c -> p (t c)").bitcast(BF16).rearrange("p (t c) -> p t c", c=256)[:, 0:HT, :]

        @block.gpsimd
        def _(pool):
            pool.memset(wp_sb[:, :, :], 0.0).then_inc(wp_zeroed, 1)
            make_identity(pool, ident, zeroed, ident_made)
            pool.memset(eps[:, :], 1e-5).then_inc(pool_consts, 1)
            pool.memset(half_neg[:, :], -0.5).then_inc(pool_consts, 1)
            pool.wait_ge(pool_consts, 2)
            def emit(it):
                for s in range(2):
                    n = it * 2 + s
                    pool.wait_ge(aggr_done, n + 1)
                    pool.tensor_tensor(out=var_eps[s][:, :], in0=meanvar[s][:, :, 1], in1=eps[:, :], op=ALU.add).then_inc(eps_done, 1)
                    pool.wait_ge(eps_done, n + 1)
                    pool.tensor_tensor(out=rstd[s][:, 0, :], in0=var_eps[s][:, :], in1=half_neg[:, :], op=ALU.pow).then_inc(pow_done, 1)

            each_pass(pool, GROUPS // 2, emit)

        @block.vector
        def _(dve):
            count = [0]

            def chain(ins):
                ins.then_inc(prep, 1)
                count[0] += 1
                dve.wait_ge(prep, count[0])

            def quantise(src, tmp, dst, inv):
                chain(dve.tensor_scalar(tmp, src, inv, MAGIC, ALU.mult, ALU.add))
                chain(dve.tensor_scalar(src, tmp, MAGIC + QP, MAGIC + QN, ALU.min, ALU.max))
                chain(dve.tensor_scalar(dst, src, -MAGIC, None, ALU.add))

            dve.wait_ge(params_in, 16 * (10 + NH))
            chain(dve.tensor_reduce(step[:, 0:1], aa1_row[:, :], AX_X, ALU.add))
            chain(dve.tensor_reduce(step[:, 1:2], aa2_row[:, :], AX_X, ALU.add))
            chain(dve.tensor_scalar(step[:, 2:3], step[:, 0:1], 1.0 / C, None, ALU.mult))
            chain(dve.tensor_scalar(step[:, 3:4], step[:, 1:2], 1.0 / HID, None, ALU.mult))
            chain(dve.reciprocal(step[:, 4:6], step[:, 2:4]))
            chain(dve.tensor_scalar(s1[:, :], aw1_sb[:, :], step[:, 2:3], None, ALU.mult))
            chain(dve.tensor_scalar(s2_row[:, :], s2_row[:, :], step[:, 3:4], None, ALU.mult))
            chain(dve.reciprocal(inv_w1[:, :], aw1_sb[:, :]))
            chain(dve.reciprocal(inv_w2[:, :], aw2_sb[:, :]))
            for t in range(HT):
                quantise(w1_f[:, t, :], w1_g[:, t, :], w1_q[:, t, :], inv_w1[:, t:t + 1])
            for h in range(2):
                quantise(w2_f[:, h, :], w2_g[:, h, :], w2_q[:, h, :], inv_w2[:, h:h + 1])
            dve.nop().then_inc(ready, 1)
            dve.wait_ge(w_turned, 1)
            dve.tensor_copy(w1_t[:, 0, :], t_ps_w1[0][0:HALF, :]).then_inc(w_copied, 1)
            dve.tensor_copy(w1_t[:, 1, :], t_ps_w1[1][0:HALF, :]).then_inc(w_copied, 1)
            dve.wait_ge(w_turned, 2)
            dve.tensor_copy(w2_t[:, :, :], t_ps_w2[:, :, 0:C]).then_inc(w_copied, 1)

            inv_a1, inv_a2 = step[:, 4:5], step[:, 5:6]
            def emit(it):
                for s in range(2):
                    n = it * 2 + s
                    dve.wait_ge(x_loaded[s], it * 32 + 32)
                    for t in range(TILES):
                        last = dve.tensor_tensor(x_in[s][:, t, :], x_in[s][:, t, :], bp_row[:, :], ALU.add)
                    last.then_inc(yb_done, 1)
                    dve.wait_ge(proj_done, n + 1)
                    dve.wait_ge(yb_done, n * 2 + 1)
                    dve.tensor_tensor(y[s][:, :, :], p_ps[:, :, 0:C], x_in[s][:, :, :], ALU.add).then_inc(y_done, 1)
                    dve.wait_ge(y_done, n + 1)
                    for t in range(TILES):
                        last = dve.bn_stats(stats[s][:, t, :], y[s][:, t, :])
                    last.then_inc(stats_done, 1)
                    dve.wait_ge(stats_done, n + 1)
                    for t in range(TILES):
                        last = dve.tensor_tensor(y_b[s][:, t, :], y[s][:, t, :], b2_row[:, :], ALU.add)
                    last.then_inc(yb_done, 1)
                    for t in range(TILES):
                        last = dve.bn_aggr(meanvar[s][:, t, :], stats[s][:, t, :])
                    last.then_inc(aggr_done, 1)
                    dve.wait_ge(pow_done, n + 1)
                    r0, r1, r2 = (rstd[s][:, i, :] for i in range(3))
                    dve.tensor_tensor(r1, r0, r0, ALU.mult).then_inc(newton, 1)
                    dve.wait_ge(newton, n * 3 + 1)
                    dve.scalar_tensor_tensor(out=r2, in0=r1, scalar=-0.5, in1=var_eps[s][:, :], op0=ALU.mult, op1=ALU.mult).then_inc(newton, 1)
                    dve.wait_ge(newton, n * 3 + 2)
                    dve.scalar_tensor_tensor(out=r1, in0=r2, scalar=1.5, in1=r0, op0=ALU.add, op1=ALU.mult).then_inc(newton, 1)
                    dve.wait_ge(newton, n * 3 + 3)
                    for t in range(TILES):
                        last = dve.tensor_scalar(y_n[:, t, :], y[s][:, t, :], meanvar[s][:, t, 0:1], rstd[s][:, 1, t:t + 1], ALU.subtract, ALU.mult)
                    last.then_inc(yn_done, 1)
                    dve.wait_ge(yn_done, n + 1)
                    dve.tensor_scalar(y_r[:, :, :], y_n[:, :, :], inv_a1, MAGIC, ALU.mult, ALU.add).then_inc(yr_done, 1)
                    dve.wait_ge(yr_done, n + 1)
                    dve.tensor_scalar(y_n[:, :, :], y_r[:, :, :], MAGIC + QP, MAGIC + QN, ALU.min, ALU.max).then_inc(yi_done, 1)
                    dve.wait_ge(yi_done, n + 1)
                    dve.tensor_scalar(y_q[s][:, :, :], y_n[:, :, :], -MAGIC, None, ALU.add).then_inc(yq_done, 1)
                    dve.wait_ge(t_done, n + 1)
                    dve.tensor_copy(y_t[s][:, :, :], t_ps[0:HALF, :, :]).then_inc(yt_ready, 1)
                    for hf in range(2):
                        part = slice(hf * HT // 2, (hf + 1) * HT // 2)
                        dve.wait_ge(gelu_done, n * HT + (hf + 1) * HT // 2)
                        dve.tensor_scalar(hid[s][:, part, :], hid[s][:, part, :], 10.0, -10.0, ALU.min, ALU.max).then_inc(clip_done, 1)
                        dve.wait_ge(clip_done, n * 2 + hf + 1)
                        dve.tensor_scalar(hid_r[:, part, :], hid[s][:, part, :], inv_a2, MAGIC, ALU.mult, ALU.add).then_inc(round_done, 1)
                        dve.wait_ge(round_done, n * 2 + hf + 1)
                        dve.tensor_scalar(hid[s][:, part, :], hid_r[:, part, :], MAGIC + QP, MAGIC + QN, ALU.min, ALU.max).then_inc(bound_done, 1)
                        dve.wait_ge(bound_done, n * 2 + hf + 1)
                        dve.tensor_scalar(hid_q[s][:, part, :], hid[s][:, part, :], -MAGIC, None, ALU.add).then_inc(hq_done, 1)
                    dve.wait_ge(f_done, n + 1)
                    need(dve, stored[s], it * 16)
                    for t in range(TILES):
                        last = dve.tensor_tensor(res[s][:, t, :], f_ps[:, t, 0:C], s2_row[:, :], ALU.mult)
                    last.then_inc(scaled, 1)
                    dve.wait_ge(scaled, n + 1)
                    dve.tensor_tensor(res[s][:, :, :], res[s][:, :, :], y_b[s][:, :, :], ALU.add).then_inc(res_done, 1)

            each_pass(dve, GROUPS // 2, emit)

        @block.scalar
        def _(act):
            def emit(it):
                for s in range(2):
                    n = it * 2 + s
                    for t in range(HT):
                        act.wait_ge(h_done, n * HT + t + 1)
                        act.activation(hid[s][:, t, :], h_ps[t % 3][:, :], ACT.Gelu, bias=b1_sb[:, t:t + 1], scale=s1[:, t:t + 1]).then_inc(gelu_done, 1)

            each_pass(act, GROUPS // 2, emit)

        @block.tensor
        def _(pe):
            pe.wait_ge(ident_made, 1)
            pe.wait_ge(ready, 1)
            for h in range(2):
                for t in range(HT):
                    last = pe.transpose(t_ps_w1[h][0:HALF, t * P:(t + 1) * P], w1_q[:, t, h * HALF:(h + 1) * HALF], ident[:, :])
            last.then_inc(w_turned, 1)
            for t in range(HT):
                for h in range(2):
                    last = pe.transpose(t_ps_w2[:, t, h * HALF:(h + 1) * HALF], w2_q[:, h, t * P:(t + 1) * P], ident[0:HALF, 0:HALF])
            last.then_inc(w_turned, 1)
            pe.wait_ge(w_copied, 3)
            def emit(it):
                for s in range(2):
                    n = it * 2 + s
                    pe.wait_ge(x_loaded[s], it * 32 + 32)
                    need(pe, y_done, n)
                    for t in range(TILES):
                        for quad in range(NQUAD):
                            last = pe.matmul(p_ps[:, t, 0:C], att[s][:, quad, t * P:(t + 1) * P], wp_sb[:, quad, :],
                                             start=(quad == 0), stop=(quad == NQUAD - 1))
                    last.then_inc(proj_done, 1)
                    pe.wait_ge(yq_done, n + 1)
                    need(pe, yt_ready, n)
                    for t in range(TILES):
                        for h in range(2):
                            last = pe.transpose(t_ps[0:HALF, h, t * P:(t + 1) * P], y_q[s][:, t, h * HALF:(h + 1) * HALF], ident[:, :])
                    last.then_inc(t_done, 1)
                    pe.wait_ge(yt_ready, n + 1)
                    for t in range(HT):
                        if t >= 3:
                            pe.wait_ge(gelu_done, n * HT + t - 2)
                        elif t == 0:
                            need(pe, gelu_done, n * HT)
                        for h in range(2):
                            last = pe.matmul(h_ps[t % 3][:, :], w1_t[:, h, t * P:(t + 1) * P], y_t[s][:, h, :], start=(h == 0), stop=(h == 1))
                        last.then_inc(h_done, 1)
                    need(pe, scaled, n)
                    pe.wait_ge(hq_done, n * 2 + 2)
                    for t in range(TILES):
                        for k in range(HT):
                            last = pe.matmul(f_ps[:, t, 0:C], hid_q[s][:, k, t * P:(t + 1) * P], w2_t[:, k, :], start=(k == 0), stop=(k == HT - 1))
                    last.then_inc(f_done, 1)

            each_pass(pe, GROUPS // 2, emit)


def build(nc, a, out):
    qk_dram = nc.dram_tensor("qk_parts", (UNITS, 2, QC, 2, SEQ), F16).ap()
    v_dram = nc.dram_tensor("v_units", (UNITS, P, KT, QUAD * SLOT), F32).ap()
    bias_dram = nc.dram_tensor("bias_parts", (UNITS, 2, 2, P, SEQ), F16).ap()
    att_dram = nc.dram_tensor("att", (GROUPS, P, NQUAD, GROUP), F32).ap()
    with nc.sbuf_tensor("q_keep", [P, 2, TOKENS], F32) as q_keep:
        phase_project(nc, a["x"], a["Wq"], a["bq"], a["Wk"], a["bk"], a["Wv"], a["bv"], qk_dram, v_dram, q_keep)
        phase_rel_bias(nc, a["rel_h"], a["rel_w"], bias_dram, q_keep)
    phase_attention(nc, qk_dram, v_dram, bias_dram, att_dram)
    phase_ffn(nc, a["x"], a["Wp"], a["bp"], a["w1"], a["b1"], a["alpha_w1"], a["alpha_a1"],
              a["w2"], a["b2"], a["alpha_w2"], a["alpha_w2_cols"], a["alpha_a2"], att_dram, out)


def kernel(**inputs):
    import numpy as _np
    import concourse.bacc as _bacc
    from concourse import mybir as _mybir
    from concourse.bass_utils import run_bass_kernel_spmd as _run

    nc = _bacc.Bacc("TRN2", target_bir_lowering=False, num_devices=1)
    arrays, args = {}, {}
    for name, value in inputs.items():
        value = _np.asarray(value)
        short = name.replace("L0_conv_", "").replace("L0_ffn_", "")
        if short == "x":
            value = value.reshape(TOKENS, C)
        if short in ("rel_h", "rel_w"):
            value = value[::-1].T
        laid = {short: value}
        if short in ("b1", "alpha_w1"):
            laid = {short: value.reshape(HT, P).T}
        if short == "alpha_w2":
            laid["alpha_w2_cols"] = value.reshape(2, HALF).T
        for key, array in laid.items():
            array = _np.ascontiguousarray(array)
            arrays[f"in_{key}"] = array
            args[key] = nc.dram_tensor(f"in_{key}", array.shape, _mybir.dt.from_np(array.dtype), kind="ExternalInput").ap()
    out = nc.dram_tensor("out_0", (TOKENS, C), _mybir.dt.float32, kind="ExternalOutput").ap()
    build(nc, args, out)
    r = _run(nc, [arrays], core_ids=[0])
    return r.results[0]["out_0"].reshape(BATCH, GRID, GRID, C)
```

```python
from contextlib import ExitStack

import concourse.bass as bass
from concourse import mybir

F32 = mybir.dt.float32
F16 = mybir.dt.float16
BF16 = mybir.dt.bfloat16
ALU = mybir.AluOpType
ACT = mybir.ActivationFunctionType
AX_X = mybir.AxisListType.X

P = 128
BATCH, GRID, C = 4, 32, 192
SEQ = GRID * GRID
TOKENS = BATCH * SEQ
NH = 12
HD = C // NH
QUAD = 4
NQUAD = NH // QUAD
QC = QUAD * HD
UNITS = BATCH * NQUAD
REL = 2 * GRID - 1
HALF = C // 2
GROUP = 512
TILES = GROUP // P
GROUPS = TOKENS // GROUP
HID = 768
HT = HID // P
KT = SEQ // P
SLOT = 32
NLO = 2 * GRID + 2
MAGIC = 1.5 * 2.0 ** 23
QN, QP = -8.0, 7.0


def need(eng, sem, value):
    if not isinstance(value, int) or value > 0:
        eng.wait_ge(sem, value)


class Group:

    def __init__(self, it, s):
        self.it, self.s, self.n = it, s, it * 2 + s
        self.first = isinstance(it, int) and self.n == 0
        self.last = isinstance(it, int) and self.n == GROUPS - 1

    def after(self, k):
        return Group(self.it + (self.s + k) // 2, (self.s + k) % 2)


FIRST, LAST = Group(0, 0), Group(GROUPS // 2 - 1, 1)


def each_group(eng, emit):
    for s in range(2):
        emit(Group(0, s))
    with eng.Fori(1, GROUPS // 2 - 1) as it:
        for s in range(2):
            emit(Group(it, s))
    for s in range(2):
        emit(Group(GROUPS // 2 - 1, s))


class Phase:

    def __init__(self, nc, name):
        self.nc, self.name, self.stack = nc, name, ExitStack()

    def __enter__(self):
        self.stack.__enter__()
        return self

    def __exit__(self, *a):
        return self.stack.__exit__(*a)

    def sb(self, name, shape, dt):
        return self.stack.enter_context(self.nc.sbuf_tensor(f"{self.name}_{name}", shape, dt))

    def ps(self, name, shape, dt):
        return self.stack.enter_context(self.nc.psum_tensor(f"{self.name}_{name}", shape, dt))

    def sem(self, name):
        return self.stack.enter_context(self.nc.semaphore(f"{self.name}_{name}"))

    def block(self):
        return self.stack.enter_context(self.nc.Block())


def make_identity(pool, tile, cleared, done):
    n = tile.shape[0]
    pool.memset(tile[:, :], 0.0).then_inc(cleared, 1)
    pool.wait_ge(cleared, 1)
    pool.affine_select(out=tile[:, :], in_=tile[:, :], compare_op=ALU.not_equal, fill=1.0, base=0,
                       pattern=[[-1, n]], channel_multiplier=1).then_inc(done, 1)


def phase_project(nc, x, wq, bq, wk, bk, wv, bv, qk_dram, v_dram):
    with Phase(nc, "pr") as ph:
        ident = ph.sb("ident", [P, P], F32)
        w_qk = ph.sb("w_qk", [HALF, 2, 3, P], F32)
        w_v = ph.sb("w_v", [HALF, 2, C], F32)
        b_qk = ph.sb("b_qk", [P, 3], F32)
        s_qk = ph.sb("s_qk", [P, 3], F32)
        b_v = ph.sb("b_v", [P, C], F32)
        half_neg = ph.sb("half_neg", [P, TILES], F32)
        eps = ph.sb("eps", [P, TILES], F32)
        x_in = [ph.sb(f"x_in{s}", [P, TILES, C], F32) for s in range(2)]
        x_n = [ph.sb(f"x_n{s}", [P, TILES, C], F32) for s in range(2)]
        x_t = [ph.sb(f"x_t{s}", [HALF, 2, GROUP], F32) for s in range(2)]
        stats = [ph.sb(f"stats{s}", [P, TILES, 6], F32) for s in range(2)]
        meanvar = [ph.sb(f"meanvar{s}", [P, TILES, 2], F32) for s in range(2)]
        var_eps = [ph.sb(f"var_eps{s}", [P, TILES], F32) for s in range(2)]
        rstd = [ph.sb(f"rstd{s}", [P, 3, TILES], F32) for s in range(2)]
        full = [ph.sb(f"full{s}", [P, 3, GROUP], F32) for s in range(2)]
        parts = [ph.sb(f"parts{s}", [P, 3, 2, GROUP], F16) for s in range(2)]
        v_st = [ph.sb(f"v_st{s}", [P, TILES, NH, SLOT], F32) for s in range(2)]
        t_ps = ph.ps("t_ps", [P, 2, GROUP], F32)
        qk_ps = [ph.ps(f"qk_ps{c}", [P, GROUP], F32) for c in range(3)]
        v_ps = ph.ps("v_ps", [P, TILES, 256], F32)

        weights_in = ph.sem("weights_in")
        zeroed, ident_made, consts_made, pool_consts = (ph.sem(n) for n in ("zeroed", "ident_made", "consts_made", "pool_consts"))
        x_loaded = [ph.sem(f"x_loaded{s}") for s in range(2)]
        stored = [ph.sem(f"stored{s}") for s in range(2)]
        stats_done, aggr_done, eps_done, pow_done = (ph.sem(n) for n in ("stats_done", "aggr_done", "eps_done", "pow_done"))
        newton, xn_done, xt_ready, t_done = (ph.sem(n) for n in ("newton", "xn_done", "xt_ready", "t_done"))
        qk_done, v_done, f32_done, hi_done, lo_done, v_out = (
            ph.sem(n) for n in ("qk_done", "v_done", "f32_done", "hi_done", "lo_done", "v_out"))
        n_weights, per_group = 10, 9
        block = ph.block()
        x_v = x.rearrange("(n t p) c -> n p t c", t=TILES, p=P)

        @block.sync
        def _(sp):
            def load(g):
                sp.dma_start(x_in[g.s][:, :, :], x_v[bass.ds(g.n, 1), :, :, :].rearrange("n p t c -> (n p) t c")).then_inc(x_loaded[g.s], 16)

            load(Group(0, 0))
            load(Group(0, 1))
            for w, c0, c1, q0 in ((wq, 0, P, 0), (wk, 0, P, 1)):
                sp.dma_start(w_qk[:, :, q0, :], w[:, c0:c1].rearrange("(h p) c -> p h c", h=2)).then_inc(weights_in, 16)
            for w, b, at in ((wq, bq, 0), (wk, bk, QC)):
                sp.dma_start(w_qk[:, :, 2, at:at + QC], w[:, P:C].rearrange("(h p) c -> p h c", h=2)).then_inc(weights_in, 16)
                sp.dma_start(b_qk[at:at + QC, 2:3], b[P:C].rearrange("(p o) -> p o", o=1)).then_inc(weights_in, 16)
            for b, q0 in ((bq, 0), (bk, 1)):
                sp.dma_start(b_qk[:, q0:q0 + 1], b[0:P].rearrange("(p o) -> p o", o=1)).then_inc(weights_in, 16)
            sp.dma_start(w_v[:, :, :], wv.rearrange("(h p) c -> p h c", h=2)).then_inc(weights_in, 16)
            sp.dma_start(b_v[:, :], bv.partition_broadcast(P)).then_inc(weights_in, 16)
            def emit(g):
                if not (g.last or g.after(1).last):
                    sp.wait_ge(xn_done, g.n + 1)
                    load(g.after(2))
                image = g.it
                for c in range(3):
                    sp.wait_ge(hi_done, g.n * 3 + c + 1)
                    sp.wait_ge(lo_done, g.n * 3 + c + 1)
                    for half in range(2):
                        which, quad = ((c, half), (half, 2))[c == 2]
                        dst = qk_dram[bass.ds(image * NQUAD + quad, 1), which, :, :, g.s * GROUP:(g.s + 1) * GROUP]
                        sp.dma_start(dst.rearrange("u h r t -> (u r) h t"),
                                     parts[g.s][half * QC:(half + 1) * QC, c, :, :]).then_inc(stored[g.s], 16)
                sp.wait_ge(v_out, g.n + 1)
                for quad in range(NQUAD):
                    dst = v_dram[bass.ds(image * NQUAD + quad, 1), :, g.s * TILES:(g.s + 1) * TILES, :]
                    sp.dma_start(dst.rearrange("u p t e -> (u p) t e"),
                                 v_st[g.s][:, :, quad * QUAD:(quad + 1) * QUAD, :].rearrange("p t h e -> p t (h e)")).then_inc(stored[g.s], 16)

            each_group(sp, emit)
            for s in range(2):
                sp.wait_ge(stored[s], 16 * per_group * (GROUPS // 2))

        @block.gpsimd
        def _(pool):
            make_identity(pool, ident, zeroed, ident_made)
            pool.memset(eps[:, :], 1e-6).then_inc(pool_consts, 1)
            pool.memset(half_neg[:, :], -0.5).then_inc(pool_consts, 1)
            pool.wait_ge(pool_consts, 2)

            def inverse_std(g):
                pool.wait_ge(aggr_done, g.n + 1)
                pool.tensor_tensor(out=var_eps[g.s][:, :], in0=meanvar[g.s][:, :, 1], in1=eps[:, :], op=ALU.add).then_inc(eps_done, 1)
                pool.wait_ge(eps_done, g.n + 1)
                pool.tensor_tensor(out=rstd[g.s][:, 0, :], in0=var_eps[g.s][:, :], in1=half_neg[:, :], op=ALU.pow).then_inc(pow_done, 1)

            inverse_std(FIRST)

            def emit(g):
                if not g.last:
                    inverse_std(g.after(1))
                for c in range(3):
                    pool.wait_ge(hi_done, g.n * 3 + c + 1)
                    pool.tensor_tensor(out=parts[g.s][:, c, 1, :], in0=full[g.s][:, c, :], in1=parts[g.s][:, c, 0, :],
                                       op=ALU.subtract).then_inc(lo_done, 1)

            each_group(pool, emit)

        @block.vector
        def _(dve):
            def normalise(g):
                x_g, st, mv, rs = x_in[g.s], stats[g.s], meanvar[g.s], rstd[g.s]
                dve.wait_ge(x_loaded[g.s], (g.it + 1) * 16)
                for t in range(TILES):
                    last = dve.bn_stats(st[:, t, :], x_g[:, t, :])
                last.then_inc(stats_done, 1)
                dve.wait_ge(stats_done, g.n + 1)
                dve.memset(rs[:, 1, :], 0.0)
                for t in range(TILES):
                    last = dve.bn_aggr(mv[:, t, :], st[:, t, :])
                last.then_inc(aggr_done, 1)
                dve.wait_ge(pow_done, g.n + 1)
                r0, r1, r2 = (rs[:, i, :] for i in range(3))
                dve.tensor_tensor(r1, r0, r0, ALU.mult).then_inc(newton, 1)
                dve.wait_ge(newton, g.n * 3 + 1)
                dve.scalar_tensor_tensor(out=r2, in0=r1, scalar=-0.5, in1=var_eps[g.s][:, :], op0=ALU.mult, op1=ALU.mult).then_inc(newton, 1)
                dve.wait_ge(newton, g.n * 3 + 2)
                dve.scalar_tensor_tensor(out=r1, in0=r2, scalar=1.5, in1=r0, op0=ALU.add, op1=ALU.mult).then_inc(newton, 1)
                dve.wait_ge(newton, g.n * 3 + 3)
                need(dve, t_done, g.n - 1)
                for t in range(TILES):
                    last = dve.tensor_scalar(x_n[g.s][:, t, :], x_g[:, t, :], mv[:, t, 0:1], rs[:, 1, t:t + 1], ALU.subtract, ALU.mult)
                last.then_inc(xn_done, 1)

            dve.memset(s_qk[:, :], 1.0).then_inc(consts_made, 1)
            dve.wait_ge(consts_made, 1)
            dve.memset(s_qk[:, 1:2], HD ** -0.5).then_inc(consts_made, 1)
            dve.memset(s_qk[QC:P, 2:3], HD ** -0.5).then_inc(consts_made, 1)
            for s in range(2):
                dve.memset(v_st[s][:, :, :, :], 1.0).then_inc(consts_made, 1)
            normalise(FIRST)
            dve.wait_ge(weights_in, 16 * n_weights)
            dve.wait_ge(consts_made, 5)

            def emit(g):
                if not g.last:
                    normalise(g.after(1))
                need(dve, lo_done, (g.n - 1) * 3)
                for c in range(3):
                    dve.wait_ge(qk_done, g.n * 3 + c + 1)
                    dve.tensor_scalar(full[g.s][:, c, :], qk_ps[c][:, :], b_qk[:, c:c + 1], s_qk[:, c:c + 1], ALU.add, ALU.mult).then_inc(f32_done, 1)
                dve.wait_ge(v_done, g.n + 1)
                need(dve, stored[g.s], g.it * (16 * per_group))
                for t in range(TILES):
                    last = dve.tensor_tensor(v_st[g.s][:, t, :, 0:HD], v_ps[:, t, 0:C].rearrange("p (h d) -> p h d", d=HD),
                                             b_v[:, :].rearrange("p (h d) -> p h d", d=HD), ALU.add)
                last.then_inc(v_out, 1)

            each_group(dve, emit)

        @block.scalar
        def _(act):
            def take_turned(g):
                act.wait_ge(t_done, g.n + 1)
                need(act, v_done, g.n - 1)
                act.activation(x_t[g.s][:, :, :], t_ps[0:HALF, :, :], ACT.Copy).then_inc(xt_ready, 1)

            take_turned(FIRST)

            def emit(g):
                need(act, stored[g.s], g.it * (16 * per_group))
                for c in range(3):
                    act.wait_ge(f32_done, g.n * 3 + c + 1)
                    act.activation(parts[g.s][:, c, 0, :], full[g.s][:, c, :], ACT.Copy).then_inc(hi_done, 1)
                    if c == 0 and not g.last:
                        take_turned(g.after(1))

            each_group(act, emit)

        @block.tensor
        def _(pe):
            def turn(g):
                pe.wait_ge(xn_done, g.n + 1)
                need(pe, xt_ready, g.n)
                for t in range(TILES):
                    for h in range(2):
                        last = pe.transpose(t_ps[0:HALF, h, t * P:(t + 1) * P], x_n[g.s][:, t, h * HALF:(h + 1) * HALF], ident[:, :])
                last.then_inc(t_done, 1)

            pe.wait_ge(ident_made, 1)
            turn(FIRST)
            pe.wait_ge(weights_in, 16 * n_weights)

            def emit(g):
                pe.wait_ge(xt_ready, g.n + 1)
                for c in range(3):
                    need(pe, f32_done, (g.n - 1) * 3 + c + 1)
                    for h in range(2):
                        last = pe.matmul(qk_ps[c][:, :], w_qk[:, h, c, :], x_t[g.s][:, h, :], start=(h == 0), stop=(h == 1))
                    last.then_inc(qk_done, 1)
                if not g.last:
                    turn(g.after(1))
                need(pe, v_out, g.n)
                for t in range(TILES):
                    for h in range(2):
                        last = pe.matmul(v_ps[:, t, 0:C], x_t[g.s][:, h, t * P:(t + 1) * P], w_v[:, h, :], start=(h == 0), stop=(h == 1))
                last.then_inc(v_done, 1)

            each_group(pe, emit)


def phase_rel_bias(nc, rel_h, rel_w, qk_dram, bias_dram, prepare):
    PER = 8
    RING = 3
    with Phase(nc, "rb") as ph:
        q_parts = [ph.sb(f"q_parts{i}", [P, BATCH, SEQ], F16) for i in range(NQUAD)]
        rel = [ph.sb(f"rel{t}", [P, 2, REL, QUAD], F16) for t in range(2)]
        rel_rows = [ph.sb(f"rel_rows{t}", [P, REL], F32) for t in range(2)]
        rel_parts = [ph.sb(f"rel_parts{t}", [P, 2, REL], F16) for t in range(2)]
        own2 = ph.sb("own2", [P, 2, QUAD], F32)
        own = ph.sb("own", [P, QUAD], F32)
        stage = [ph.sb(f"stage{i}", [P, 2, BATCH, SEQ], F16) for i in range(2)]
        b_ps = [ph.ps(f"b_ps{i}", [P, PER, BATCH, GRID], F32) for i in range(RING)]
        mask_step, rel_in, rel_step, rel_made, mm_done, hi_done, lo_done, own_made = (
            ph.sem(n) for n in ("mask_step", "rel_in", "rel_step", "rel_made", "mm_done", "hi_done", "lo_done", "own_made"))
        q_in = [ph.sem(f"q_in{i}") for i in range(NQUAD)]
        stored = [ph.sem(f"stored{i}") for i in range(2)]
        prep = prepare(ph)
        block = ph.block()
        work = [(quad, t) for quad in range(NQUAD) for t in range(2)]
        chunks = GRID // PER

        @block.gpsimd
        def _(pool):
            pool.memset(own2[:, :, :], 1.0).then_inc(mask_step, 1)
            pool.wait_ge(mask_step, 1)
            pool.affine_select(out=own2[:, :, :], in_=own2[:, :, :], compare_op=ALU.is_ge, fill=0.0, base=0,
                               pattern=[[-QC, 2], [-HD, QUAD]], channel_multiplier=1).then_inc(mask_step, 1)
            pool.wait_ge(mask_step, 2)
            pool.affine_select(out=own2[:, :, :], in_=own2[:, :, :], compare_op=ALU.is_ge, fill=0.0, base=HD - 1,
                               pattern=[[QC, 2], [HD, QUAD]], channel_multiplier=-1).then_inc(mask_step, 1)
            prep.pool(pool)

        @block.sync
        def _(sp):
            for t, src in enumerate((rel_h, rel_w)):
                for r in range(0, P, HD):
                    sp.dma_start(rel_rows[t][r:r + HD, :], src).then_inc(rel_in, 16)
            units = qk_dram.rearrange("(b g) w h r t -> g w h r b t", g=NQUAD)
            for quad in range(NQUAD):
                for part in range(2):
                    sp.dma_start(q_parts[quad][part * QC:(part + 1) * QC, :, :], units[quad, 0, part]).then_inc(q_in[quad], 16)
            prep.load(sp)
            for i, (quad, t) in enumerate(work):
                sp.wait_ge(hi_done, (i + 1) * chunks)
                sp.wait_ge(lo_done, (i + 1) * chunks)
                for part in range(2):
                    dst = bias_dram.rearrange("(b g) h t r q -> g h t r b q", g=NQUAD)[quad, part, t]
                    sp.dma_start(dst, stage[i % 2][:, part, :, :]).then_inc(stored[i % 2], 16)
            for i in range(2):
                sp.wait_ge(stored[i], 16 * len(work))

        @block.tensor
        def _(pe):
            pe.wait_ge(rel_made, 1)
            for i, (quad, t) in enumerate(work):
                pe.wait_ge(q_in[quad], 32)
                q = q_parts[quad][:, :, :].rearrange("p b (r c) -> p b r c", c=GRID)
                for ch in range(chunks):
                    k = i * chunks + ch
                    need(pe, lo_done, k - RING + 1)
                    for j in range(PER):
                        at = ch * PER + j
                        rhs = q[:, :, at, :] if t == 0 else q[:, :, :, at]
                        for part in range(2):
                            window = rel[t][:, part, GRID - 1 - at:REL - at, :].rearrange("p r h -> p (r h)")
                            last = pe.matmul(b_ps[k % RING][:, j, :, :], window, rhs, start=(part == 0), stop=(part == 1))
                    last.then_inc(mm_done, 1)
            prep.turn(pe)

        def spot(i, t, ch, part):
            st = stage[i % 2][:, part, :, :]
            if t == 0:
                return st.rearrange("p b (r c) -> p r b c", c=GRID)[:, ch * PER:(ch + 1) * PER]
            return st.rearrange("p b (r c) -> p c b r", c=GRID)[:, ch * PER:(ch + 1) * PER]

        @block.scalar
        def _(act):
            for i, (quad, t) in enumerate(work):
                need(act, stored[i % 2], 32 * (i // 2))
                for ch in range(chunks):
                    k = i * chunks + ch
                    act.wait_ge(mm_done, k + 1)
                    act.activation(spot(i, t, ch, 0), b_ps[k % RING][:, :, :, :], ACT.Copy).then_inc(hi_done, 1)

        @block.vector
        def _(dve):
            dve.wait_ge(mask_step, 3)
            dve.tensor_tensor(own[:, :], own2[:, 0, :], own2[:, 1, :], ALU.add).then_inc(own_made, 1)
            dve.wait_ge(own_made, 1)
            dve.wait_ge(rel_in, 16 * 2 * (P // HD))
            for t in range(2):
                dve.tensor_copy(rel_parts[t][:, 0, :], rel_rows[t][:, :]).then_inc(rel_step, 1)
                dve.wait_ge(rel_step, 2 * t + 1)
                dve.tensor_tensor(rel_parts[t][:, 1, :], rel_rows[t][:, :], rel_parts[t][:, 0, :], ALU.subtract).then_inc(rel_step, 1)
                dve.wait_ge(rel_step, 2 * t + 2)
                for head in range(QUAD):
                    last = dve.tensor_scalar(rel[t][:, :, :, head], rel_parts[t][:, :, :], own[:, head:head + 1], None, ALU.mult)
            last.then_inc(rel_made, 1)
            for i, (quad, t) in enumerate(work):
                for ch in range(chunks):
                    k = i * chunks + ch
                    dve.wait_ge(hi_done, k + 1)
                    dve.tensor_tensor(spot(i, t, ch, 1), b_ps[k % RING][:, :, :, :], spot(i, t, ch, 0), ALU.subtract).then_inc(lo_done, 1)
                prep.quantise(dve, i)
            prep.finish(dve)


def phase_attention(nc, qk_dram, v_dram, bias_dram, out_dram):
    STEPS = 2 * KT
    LAG = 2
    PRING = 4
    PIECES = QUAD * KT * 2
    PER_STEP = 6
    N_LOADS = 13
    with Phase(nc, "at") as ph:
        mix_q = [ph.sb(f"mix_q{i}", [P, QUAD, SEQ], F16) for i in range(3)]
        mix_k = [ph.sb(f"mix_k{i}", [P, QUAD, SEQ], F16) for i in range(3)]
        lo_q = [ph.sb(f"lo_q{i}", [NLO, QUAD, SEQ], F16) for i in range(3)]
        lo_k = ph.sb("lo_k", [NLO, SEQ], F16)
        v_u = [ph.sb(f"v_u{i}", [P, KT, QUAD, SLOT], F32) for i in range(3)]
        probs = [ph.sb(f"probs{i}", [P, QUAD, GROUP], F32) for i in range(PRING)]
        ident = ph.sb("ident", [P, P], F32)
        sum_pick = ph.sb("sum_pick", [P, QUAD], F32)
        piece_max = ph.sb("piece_max", [P, PIECES], F32)
        row_max = ph.sb("row_max", [P, QUAD * KT], F32)
        neg_max = ph.sb("neg_max", [QUAD * KT, 2, P], F16)
        o_sb = [ph.sb(f"o_sb{i}", [P, GROUP], F32) for i in range(2)]
        inv = ph.sb("inv", [P, TILES * QUAD], F32)
        inv_wide = ph.sb("inv_wide", [P, TILES * QUAD, SLOT], F32)
        o_n = [ph.sb(f"o_n{i}", [P, GROUP], F32) for i in range(2)]
        s_ps = [ph.ps(f"s_ps{i}", [P, 2, GROUP], F32) for i in range(2)]
        m_ps = [ph.ps(f"m_ps{i}", [P, GROUP], F32) for i in range(2)]
        o_ps = ph.ps("o_ps", [P, GROUP], F32)
        x_ps = ph.ps("x_ps", [P, GROUP], F32)

        consts, const_step, hot_out = ph.sem("consts"), ph.sem("const_step"), ph.sem("hot_out")
        loaded = [ph.sem(f"loaded{i}") for i in range(3)]
        max_loaded = [ph.sem(f"max_loaded{i}") for i in range(3)]
        scores_done, exp_done, pv_done = (ph.sem(n) for n in ("scores_done", "exp_done", "pv_done"))
        piece_done, reduced = ph.sem("piece_done"), ph.sem("reduced")
        max_done, max_turned, neg_hi, neg_done = (ph.sem(n) for n in ("max_done", "max_turned", "neg_hi", "neg_done"))
        o_out, sums_done, inv_done, wide_done, spread_done, norm_done = (
            ph.sem(n) for n in ("o_out", "sums_done", "inv_done", "wide_done", "spread_done", "norm_done"))
        o_stored = [ph.sem(f"o_stored{i}") for i in range(2)]
        block = ph.block()

        class Unit:

            def __init__(self, u, image, static):
                self.u, self.image, self.buf = u, image, static % 3
                self.quad = static % NQUAD
                self.turn = image
                self.first, self.last = isinstance(u, int) and u == 0, isinstance(u, int) and u == UNITS - 1

            def after(self, k):
                static = self.buf + k
                return Unit(self.u + k, self.image + static // 3, static)

        def each_unit(eng, emit):
            emit(Unit(0, 0, 0))
            with eng.Fori(0, 3) as r:
                for k in range(1, 4):
                    emit(Unit(r * 3 + k, r + k // 3, k))
            for u in (UNITS - 2, UNITS - 1):
                emit(Unit(u, u // 3, u))

        def pieces(n):
            return range(min(n * PER_STEP, PIECES), min((n + 1) * PER_STEP, PIECES))

        MAX_AT = -(-PIECES // PER_STEP)
        TURN_AT = MAX_AT + 2
        O_AT = (LAG - 1, KT + LAG - 1)
        SUMS_AT = (O_AT[0] + 1, O_AT[1] + 1)
        SPREAD_AT = (SUMS_AT[0] + 1, SUMS_AT[1] + 1)
        assert SPREAD_AT[0] < SUMS_AT[1] and SPREAD_AT[1] < TURN_AT < STEPS

        @block.gpsimd
        def _(pool):
            make_identity(pool, ident, const_step, consts)
            pool.memset(sum_pick[:, :], 0.0).then_inc(const_step, 1)
            pool.memset(lo_k[:, :], 0.0).then_inc(const_step, 1)
            pool.wait_ge(const_step, 3)
            pool.affine_select(out=sum_pick[:, :], in_=sum_pick[:, :], compare_op=ALU.not_equal, fill=1.0, base=-HD,
                               pattern=[[-SLOT, QUAD]], channel_multiplier=1).then_inc(consts, 1)
            hot = lo_k[0:2 * GRID, :].rearrange("p (r c) -> p r c", c=GRID)
            pool.affine_select(out=hot, in_=hot, compare_op=ALU.not_equal, fill=1.0, base=0,
                               pattern=[[-1, GRID], [0, GRID]], channel_multiplier=1).then_inc(const_step, 1)
            pool.wait_ge(const_step, 4)
            pool.affine_select(out=hot, in_=hot, compare_op=ALU.not_equal, fill=1.0, base=-GRID,
                               pattern=[[0, GRID], [-1, GRID]], channel_multiplier=1).then_inc(const_step, 1)
            pool.memset(lo_k[2 * GRID:NLO, :], 1.0).then_inc(const_step, 1)
            pool.wait_ge(const_step, 6)
            for i in range(3):
                for j in range(QUAD):
                    pool.dma_start(mix_k[i][2 * GRID:P, j, :], lo_k[0:2 * GRID, :]).then_inc(hot_out, 16)
            pool.wait_ge(hot_out, 16 * 3 * QUAD)
            pool.nop().then_inc(consts, 1)

        @block.sync
        def _(sp):
            def load(unit):
                u, i = unit.u, unit.buf

                def q_or_k(which, part):
                    src = qk_dram[bass.ds(u, 1), which, part, :, :]
                    return src.rearrange("u (j d) t -> (u d) j t", d=HD)

                for r, part in enumerate((0, 0, 1, 1)):
                    sp.dma_start(mix_q[i][r * HD:(r + 1) * HD, :, :], q_or_k(0, part)).then_inc(loaded[i], 16)
                for r, part in enumerate((0, 1, 0, 1)):
                    sp.dma_start(mix_k[i][r * HD:(r + 1) * HD, :, :], q_or_k(1, part)).then_inc(loaded[i], 16)
                for t in range(2):
                    for part, dst in ((0, mix_q[i][(2 + t) * GRID:(3 + t) * GRID, :, :]), (1, lo_q[i][t * GRID:(t + 1) * GRID, :, :])):
                        src = bias_dram[bass.ds(u, 1), part, t, :, :].rearrange("u (r j) q -> (u r) j q", j=QUAD)
                        sp.dma_start(dst, src).then_inc(loaded[i], 16)
                sp.dma_start(v_u[i][:, :, :, :].rearrange("p k h e -> p k (h e)"),
                             v_dram[bass.ds(u, 1), :, :, :].rearrange("u p k e -> (u p) k e")).then_inc(loaded[i], 16)

            def load_max(unit):
                sp.wait_ge(neg_done, unit.u + 1)
                for part in range(2):
                    sp.dma_start(lo_q[unit.buf][2 * GRID + part:2 * GRID + part + 1, :, :].rearrange("o j (t p) -> o (j t) p", p=P),
                                 neg_max[:, part, :]).then_inc(max_loaded[unit.buf], 16)

            def store(unit, half):
                sp.wait_ge(norm_done, unit.u * 2 + half + 1)
                dst = out_dram[bass.ds(unit.image * 2 + half, 1), :, unit.quad, :].rearrange("n p t -> (n p) t")
                sp.dma_start(dst, o_n[half][:, :]).then_inc(o_stored[half], 16)

            load(Unit(0, 0, 0))
            load(Unit(1, 0, 1))
            load_max(Unit(0, 0, 0))

            def emit(unit):
                if not (isinstance(unit.u, int) and unit.u + 2 >= UNITS):
                    need(sp, pv_done, unit.u * STEPS)
                    load(unit.after(2))
                if not unit.first:
                    store(unit.after(-1), 1)
                store(unit, 0)
                if not unit.last:
                    load_max(unit.after(1))

            each_unit(sp, emit)
            store(Unit(UNITS - 1, BATCH - 1, UNITS - 1), 1)
            for half in range(2):
                sp.wait_ge(o_stored[half], 16 * UNITS)

        @block.tensor
        def _(pe):
            def piece(unit, i):
                j, qt, kh = i // (2 * KT), i // 2 % KT, i % 2
                need(pe, reduced, unit.u * PIECES + i - 1)
                pe.matmul(m_ps[i % 2][:, :], mix_q[unit.buf][:, j, qt * P:(qt + 1) * P],
                          mix_k[unit.buf][:, j, kh * GROUP:(kh + 1) * GROUP], start=True, stop=True).then_inc(piece_done, 1)

            def turn(unit):
                pe.wait_ge(max_done, unit.u + 1)
                need(pe, norm_done, unit.u * 2 - 1)
                pe.transpose(x_ps[0:QUAD * KT, 0:P], row_max[:, :], ident[:, :]).then_inc(max_turned, 1)

            def scores(unit, n, j):
                half, kt = divmod(n, KT)
                pair = j // 2
                step = unit.u * STEPS + n
                if j % 2 == 0:
                    need(pe, exp_done, step * 2 + pair - 1)
                keys, queries = slice(kt * P, (kt + 1) * P), slice(half * GROUP, (half + 1) * GROUP)
                pe.matmul(s_ps[pair][:, j % 2, :], mix_k[unit.buf][:, j, keys], mix_q[unit.buf][:, j, queries], start=True, stop=False)
                last = pe.matmul(s_ps[pair][:, j % 2, :], lo_k[:, keys], lo_q[unit.buf][:, j, queries], start=False, stop=True)
                if j % 2 == 1:
                    last.then_inc(scores_done, 1)

            def weigh(unit, n):
                half, kt = divmod(n, KT)
                step = unit.u * STEPS + n
                pe.wait_ge(exp_done, step * 2 + 2)
                if kt == 0:
                    need(pe, o_out, unit.u * 2 + half)
                for j in range(QUAD):
                    last = pe.matmul(o_ps[j * SLOT:(j + 1) * SLOT, :], v_u[unit.buf][:, kt, j, :], probs[n % PRING][:, j, :],
                                     start=(kt == 0), stop=(kt == KT - 1), tile_position=(0, j * SLOT))
                last.then_inc(pv_done, 1)

            def sums(unit, half):
                pe.wait_ge(o_out, unit.u * 2 + half + 1)
                need(pe, norm_done, unit.u * 2 + half)
                if half == 1 and not unit.last:
                    pe.wait_ge(neg_done, unit.u + 2)
                for t in range(TILES):
                    last = pe.matmul(x_ps[:, t * QUAD:(t + 1) * QUAD], o_sb[half][:, t * P:(t + 1) * P], sum_pick[:, :], start=True, stop=True)
                last.then_inc(sums_done, 1)

            def spread(unit, half):
                pe.wait_ge(wide_done, unit.u * 2 + half + 1)
                for t in range(TILES):
                    last = pe.transpose(x_ps[:, t * P:(t + 1) * P],
                                        inv_wide[:, t * QUAD:(t + 1) * QUAD, :].rearrange("p h r -> p (h r)"), ident[:, :])
                last.then_inc(spread_done, 1)

            pe.wait_ge(consts, 3)
            first = Unit(0, 0, 0)
            pe.wait_ge(loaded[0], 16 * N_LOADS)
            for i in range(PIECES):
                piece(first, i)
            turn(first)

            def emit(unit):
                nxt = unit.after(1)
                pe.wait_ge(max_loaded[unit.buf], (unit.turn + 1) * 32)
                if not unit.last:
                    pe.wait_ge(loaded[nxt.buf], (nxt.turn + 1) * (16 * N_LOADS))
                for n in range(STEPS):
                    todo = [] if unit.last else list(pieces(n))
                    for j in range(QUAD):
                        scores(unit, n, j)
                        for i in todo[j:j + 1]:
                            piece(nxt, i)
                    if n >= LAG:
                        weigh(unit, n - LAG)
                    elif not unit.first:
                        weigh(unit.after(-1), STEPS + n - LAG)
                    for i in todo[QUAD:]:
                        piece(nxt, i)
                    for half, owner in ((1, None if unit.first else unit.after(-1)), (0, unit)):
                        if owner and n == SUMS_AT[1 - half]:
                            sums(owner, half)
                        if owner and n == SPREAD_AT[1 - half]:
                            spread(owner, half)
                    if n == TURN_AT and not unit.last:
                        turn(nxt)

            each_unit(pe, emit)
            last = Unit(UNITS - 1, BATCH - 1, UNITS - 1)
            for n in range(STEPS - LAG, STEPS):
                weigh(last, n)
            sums(last, 1)
            spread(last, 1)

        @block.scalar
        def _(act):
            def exps(unit, n):
                step = unit.u * STEPS + n
                need(act, pv_done, step - PRING + 1)
                for pair in range(2):
                    act.wait_ge(scores_done, step * 2 + pair + 1)
                    act.activation(probs[n % PRING][:, 2 * pair:2 * pair + 2, :], s_ps[pair][:, :, :], ACT.Exp).then_inc(exp_done, 1)

            def take_out(unit, half):
                act.wait_ge(pv_done, unit.u * STEPS + (half + 1) * KT)
                need(act, norm_done, unit.u * 2 + half - 1)
                act.activation(o_sb[half][:, :], o_ps[:, :], ACT.Copy).then_inc(o_out, 1)

            def emit(unit):
                for n in range(STEPS):
                    exps(unit, n)
                    if n == O_AT[0] and not unit.first:
                        take_out(unit.after(-1), 1)
                    if n == O_AT[1]:
                        take_out(unit, 0)

            each_unit(act, emit)
            take_out(Unit(UNITS - 1, BATCH - 1, UNITS - 1), 1)

        @block.vector
        def _(dve):
            def reduce_piece(unit, i):
                dve.wait_ge(piece_done, unit.u * PIECES + i + 1)
                dve.tensor_reduce(piece_max[:, i:i + 1], m_ps[i % 2][:, :], AX_X, ALU.max).then_inc(reduced, 1)

            def join_max(unit):
                dve.wait_ge(reduced, (unit.u + 1) * PIECES)
                need(dve, max_turned, unit.u)
                halves = piece_max[:, :].rearrange("p (r k) -> p r k", k=2)
                dve.tensor_tensor(row_max[:, :], halves[:, :, 0], halves[:, :, 1], ALU.max).then_inc(max_done, 1)

            def negate(unit):
                dve.wait_ge(max_turned, unit.u + 1)
                if not unit.first:
                    prev = unit.after(-1)
                    dve.wait_ge(max_loaded[prev.buf], (prev.turn + 1) * 32)
                turned = x_ps[0:QUAD * KT, 0:P]
                dve.tensor_scalar(neg_max[:, 0, :], turned, -1.0, None, ALU.mult).then_inc(neg_hi, 1)
                dve.wait_ge(neg_hi, unit.u + 1)
                dve.scalar_tensor_tensor(out=neg_max[:, 1, :], in0=turned, scalar=-1.0, in1=neg_max[:, 0, :],
                                         op0=ALU.mult, op1=ALU.subtract).then_inc(neg_done, 1)

            def invert(unit, half):
                dve.wait_ge(sums_done, unit.u * 2 + half + 1)
                dve.reciprocal(inv[:, :], x_ps[:, 0:TILES * QUAD]).then_inc(inv_done, 1)
                dve.wait_ge(inv_done, unit.u * 2 + half + 1)
                need(dve, spread_done, unit.u * 2 + half)
                dve.tensor_copy(inv_wide[:, :, :], inv[:, :].unsqueeze(2).to_broadcast([P, TILES * QUAD, SLOT])).then_inc(wide_done, 1)

            def normalise(unit, half):
                dve.wait_ge(spread_done, unit.u * 2 + half + 1)
                need(dve, o_stored[half], unit.u * 16)
                dve.tensor_tensor(o_n[half][:, :], o_sb[half][:, :], x_ps[:, :], ALU.mult).then_inc(norm_done, 1)

            first = Unit(0, 0, 0)
            for i in range(PIECES):
                reduce_piece(first, i)
            join_max(first)
            negate(first)

            def emit(unit):
                nxt = unit.after(1)
                for n in range(STEPS):
                    if not unit.last:
                        for i in pieces(n):
                            reduce_piece(nxt, i)
                        if n == MAX_AT:
                            join_max(nxt)
                    for half, owner in ((1, None if unit.first else unit.after(-1)), (0, unit)):
                        if owner and n == SUMS_AT[1 - half]:
                            invert(owner, half)
                        if owner and n == SPREAD_AT[1 - half]:
                            normalise(owner, half)
                    if n == TURN_AT and not unit.last:
                        negate(nxt)

            each_unit(dve, emit)
            last = Unit(UNITS - 1, BATCH - 1, UNITS - 1)
            invert(last, 1)
            normalise(last, 1)


class Weights:

    def __init__(self, stack, nc, w1, aw1, aa1, w2, aw2, aw2_cols, aa2):
        def sb(name, shape, dt):
            return stack.enter_context(nc.sbuf_tensor(f"wt_{name}", shape, dt))

        self.dram = (w1, aw1, aa1, w2, aw2, aw2_cols, aa2)
        self.w1_t = sb("w1_t", [HALF, 2, HID], BF16)
        self.w2_t = sb("w2_t", [P, HT, C], BF16)
        self.s1 = sb("s1", [P, HT], F32)
        self.s2_row = sb("s2_row", [P, C], F32)
        self.step = sb("step", [P, 6], F32)
        self.bound = sb("bound", [P, 4], F32)
        self.inv_a1, self.inv_a2 = self.step[:, 4:5], self.step[:, 5:6]

    def __call__(self, ph):
        self.aw1_sb, self.inv_w1 = ph.sb("aw1_sb", [P, HT], F32), ph.sb("inv_w1", [P, HT], F32)
        self.aw2_sb, self.inv_w2 = ph.sb("aw2_sb", [HALF, 2], F32), ph.sb("inv_w2", [HALF, 2], F32)
        self.aa1_row, self.aa2_row = ph.sb("aa1_row", [P, C], F32), ph.sb("aa2_row", [P, HID], F32)
        self.w1_f, self.w1_g = ph.sb("w1_f", [P, HT, C], F32), ph.sb("w1_g", [P, HT, C], F32)
        self.w2_f, self.w2_g = ph.sb("w2_f", [HALF, 2, HID], F32), ph.sb("w2_g", [HALF, 2, HID], F32)
        self.w1_q, self.w2_q = ph.sb("w1_q", [P, HT, C], BF16), ph.sb("w2_q", [HALF, 2, HID], BF16)
        self.ident = ph.sb("ident", [P, P], BF16)
        self.w_ps = ph.ps("w_ps", [P, 2, 2 * GROUP], BF16)
        self.zeroed, self.ident_made, self.params_in, self.chained, self.turned, self.copied = (
            ph.sem(n) for n in ("zeroed", "ident_made", "params_in", "chained", "turned", "copied"))
        self.quantised = ph.sem("quantised")
        self.links = 0
        return self

    def pool(self, pool):
        make_identity(pool, self.ident, self.zeroed, self.ident_made)

    def load(self, sp):
        w1, aw1, aa1, w2, aw2, aw2_cols, aa2 = self.dram
        for dst, src in ((self.w1_f[:, :, :], w1.rearrange("(t p) c -> p t c", p=P)), (self.w2_f[:, :, :], w2.rearrange("(h p) c -> p h c", h=2)),
                         (self.aw1_sb[:, :], aw1), (self.aw2_sb[:, :], aw2_cols), (self.s2_row[:, :], aw2.partition_broadcast(P)),
                         (self.aa1_row[:, :], aa1.partition_broadcast(P)), (self.aa2_row[:, :], aa2.partition_broadcast(P))):
            sp.dma_start(dst, src).then_inc(self.params_in, 16)

    def chain(self, dve, ins):
        ins.then_inc(self.chained, 1)
        self.links += 1
        dve.wait_ge(self.chained, self.links)

    def quantise(self, dve, i):
        step, link = self.step, lambda ins: self.chain(dve, ins)
        if i == 0:
            dve.wait_ge(self.params_in, 16 * 7)
            link(dve.tensor_reduce(step[:, 0:1], self.aa1_row[:, :], AX_X, ALU.add))
            link(dve.tensor_reduce(step[:, 1:2], self.aa2_row[:, :], AX_X, ALU.add))
            link(dve.tensor_scalar(step[:, 2:3], step[:, 0:1], 1.0 / C, None, ALU.mult))
            link(dve.tensor_scalar(step[:, 3:4], step[:, 1:2], 1.0 / HID, None, ALU.mult))
            link(dve.reciprocal(step[:, 4:6], step[:, 2:4]))
            link(dve.tensor_scalar(self.s1[:, :], self.aw1_sb[:, :], step[:, 2:3], None, ALU.mult))
            link(dve.tensor_scalar(self.s2_row[:, :], self.s2_row[:, :], step[:, 3:4], None, ALU.mult))
            link(dve.reciprocal(self.inv_w1[:, :], self.aw1_sb[:, :]))
            link(dve.reciprocal(self.inv_w2[:, :], self.aw2_sb[:, :]))
            for at, edge, limit, op in ((0, 10.0, QP, ALU.min), (1, -10.0, QN, ALU.max)):
                link(dve.tensor_scalar(self.bound[:, at:at + 1], self.inv_a2, edge, MAGIC, ALU.mult, ALU.add))
                link(dve.tensor_scalar(self.bound[:, 2 + at:3 + at], self.bound[:, at:at + 1], MAGIC + limit, None, op))
        for src, tmp, dst, inv in [(self.w1_f[:, i, :], self.w1_g[:, i, :], self.w1_q[:, i, :], self.inv_w1[:, i:i + 1])] + (
                [(self.w2_f[:, i, :], self.w2_g[:, i, :], self.w2_q[:, i, :], self.inv_w2[:, i:i + 1])] if i < 2 else []):
            link(dve.tensor_scalar(tmp, src, inv, MAGIC, ALU.mult, ALU.add))
            link(dve.tensor_scalar(src, tmp, MAGIC + QP, MAGIC + QN, ALU.min, ALU.max))
            link(dve.tensor_scalar(dst, src, -MAGIC, None, ALU.add))
        if i == HT - 1:
            dve.nop().then_inc(self.quantised, 1)

    def turn(self, pe):
        pe.wait_ge(self.ident_made, 1)
        pe.wait_ge(self.quantised, 1)
        for h in range(2):
            for t in range(HT):
                last = pe.transpose(self.w_ps[0:HALF, h, t * P:(t + 1) * P], self.w1_q[:, t, h * HALF:(h + 1) * HALF], self.ident[:, :])
        last.then_inc(self.turned, 1)
        pe.wait_ge(self.copied, 1)
        for t in range(HT):
            for h in range(2):
                last = pe.transpose(self.w_ps[:, t // 3, t % 3 * 256 + h * HALF:t % 3 * 256 + (h + 1) * HALF],
                                    self.w2_q[:, h, t * P:(t + 1) * P], self.ident[0:HALF, 0:HALF])
        last.then_inc(self.turned, 1)

    def finish(self, dve):
        dve.wait_ge(self.turned, 1)
        dve.tensor_copy(self.w1_t[:, :, :], self.w_ps[0:HALF, :, 0:HID]).then_inc(self.copied, 1)
        dve.wait_ge(self.turned, 2)
        for i in range(2):
            dve.tensor_copy(self.w2_t[:, 3 * i:3 * i + 3, :],
                            self.w_ps[:, i, 0:HID].rearrange("p (t c) -> p t c", c=256)[:, :, 0:C])


def phase_ffn(nc, x, wp, bp, b1, b2, wt, att_dram, out):
    with Phase(nc, "ff") as ph:
        ident = ph.sb("ident", [P, P], BF16)
        wp_sb = ph.sb("wp_sb", [P, NQUAD, C], F32)
        bp_row = ph.sb("bp_row", [P, C], F32)
        b2_row = ph.sb("b2_row", [P, C], F32)
        b1_sb = ph.sb("b1_sb", [P, HT], F32)
        magic = ph.sb("magic", [P, 1], F32)
        half_neg = ph.sb("half_neg", [P, TILES], F32)
        eps = ph.sb("eps", [P, TILES], F32)
        x_in = [ph.sb(f"x_in{s}", [P, TILES, C], F32) for s in range(2)]
        att = [ph.sb(f"att{s}", [P, NQUAD, GROUP], F32) for s in range(2)]
        y = [ph.sb(f"y{s}", [P, TILES, C], F32) for s in range(2)]
        y_b = [ph.sb(f"y_b{s}", [P, TILES, C], F32) for s in range(2)]
        stats = [ph.sb(f"stats{s}", [P, TILES, 6], F32) for s in range(2)]
        meanvar = [ph.sb(f"meanvar{s}", [P, TILES, 2], F32) for s in range(2)]
        var_eps = [ph.sb(f"var_eps{s}", [P, TILES], F32) for s in range(2)]
        rstd = [ph.sb(f"rstd{s}", [P, 3, TILES], F32) for s in range(2)]
        y_n = ph.sb("y_n", [P, TILES, C], F32)
        y_r = ph.sb("y_r", [P, TILES, C], F32)
        y_q = [ph.sb(f"y_q{s}", [P, TILES, C], BF16) for s in range(2)]
        y_t = [ph.sb(f"y_t{s}", [HALF, 2, GROUP], BF16) for s in range(2)]
        hid = ph.sb("hid", [P, HT, GROUP], F32)
        hid_r = ph.sb("hid_r", [P, HT, GROUP], F32)
        hid_q = [ph.sb(f"hid_q{s}", [P, HT, GROUP], BF16) for s in range(2)]
        ffn = [ph.sb(f"ffn{s}", [P, TILES, C], F32) for s in range(2)]
        res = [ph.sb(f"res{s}", [P, TILES, C], F32) for s in range(2)]
        p_ps = ph.ps("p_ps", [P, TILES, 256], F32)
        t_ps = ph.ps("t_ps", [P, 2, GROUP], BF16)
        h_ps = [ph.ps(f"h_ps{i}", [P, GROUP], F32) for i in range(3)]
        f_ps = ph.ps("f_ps", [P, TILES, 256], F32)

        zeroed, ident_made, wp_zeroed, pool_consts, magic_made, params_in = (
            ph.sem(n) for n in ("zeroed", "ident_made", "wp_zeroed", "pool_consts", "magic_made", "params_in"))
        x_loaded = [ph.sem(f"x_loaded{s}") for s in range(2)]
        att_loaded = [ph.sem(f"att_loaded{s}") for s in range(2)]
        stored = [ph.sem(f"stored{s}") for s in range(2)]
        xb_done, proj_done, y_done, yb_done, stats_done, aggr_done, eps_done, pow_done, newton = (
            ph.sem(n) for n in ("xb_done", "proj_done", "y_done", "yb_done", "stats_done", "aggr_done", "eps_done", "pow_done", "newton"))
        yn_done, yr_done, yi_done, yq_done, t_done, yt_ready = (
            ph.sem(n) for n in ("yn_done", "yr_done", "yi_done", "yq_done", "t_done", "yt_ready"))
        h_done, gelu_done, round_done, bound_done, hq_done = (
            ph.sem(n) for n in ("h_done", "gelu_done", "round_done", "bound_done", "hq_done"))
        f_done, scaled, res_done = (ph.sem(n) for n in ("f_done", "scaled", "res_done"))
        N_PARAMS = 3 + NH
        block = ph.block()
        x_v = x.rearrange("(n t p) c -> n p t c", t=TILES, p=P)
        out_v = out.rearrange("(n t p) c -> n p t c", t=TILES, p=P)
        half_h = HT // 2

        @block.sync
        def _(sp):
            def load(g):
                sp.dma_start(att[g.s][:, :, :], att_dram[bass.ds(g.n, 1), :, :, :].rearrange("n p g t -> (n p) g t")).then_inc(att_loaded[g.s], 16)
                sp.dma_start(x_in[g.s][:, :, :], x_v[bass.ds(g.n, 1), :, :, :].rearrange("n p t c -> (n p) t c")).then_inc(x_loaded[g.s], 16)

            load(FIRST)
            for dst, src in ((bp_row, bp.partition_broadcast(P)), (b2_row, b2.partition_broadcast(P)), (b1_sb, b1)):
                sp.dma_start(dst[:, :], src).then_inc(params_in, 16)
            sp.wait_ge(wp_zeroed, 1)
            for quad in range(NQUAD):
                for head in range(QUAD):
                    r = (quad * QUAD + head) * HD
                    sp.dma_start(wp_sb[head * SLOT:head * SLOT + HD, quad, :], wp[r:r + HD, :]).then_inc(params_in, 16)
            load(FIRST.after(1))

            def store(g):
                sp.wait_ge(res_done, g.n + 1)
                sp.dma_start(out_v[bass.ds(g.n, 1), :, :, :].rearrange("n p t c -> (n p) t c"), res[g.s][:, :, :]).then_inc(stored[g.s], 16)

            def emit(g):
                if not (g.last or g.after(1).last):
                    sp.wait_ge(y_done, g.n + 1)
                    load(g.after(2))
                if not g.first:
                    store(g.after(-1))

            each_group(sp, emit)
            store(LAST)
            for s in range(2):
                sp.wait_ge(stored[s], 16 * (GROUPS // 2))

        @block.gpsimd
        def _(pool):
            pool.memset(wp_sb[:, :, :], 0.0).then_inc(wp_zeroed, 1)
            make_identity(pool, ident, zeroed, ident_made)
            pool.memset(eps[:, :], 1e-5).then_inc(pool_consts, 1)
            pool.memset(half_neg[:, :], -0.5).then_inc(pool_consts, 1)
            pool.wait_ge(pool_consts, 2)
            pool.wait_ge(params_in, 16 * N_PARAMS)

            def add_bias(g):
                pool.wait_ge(x_loaded[g.s], (g.it + 1) * 16)
                for t in range(TILES):
                    last = pool.tensor_tensor(out=x_in[g.s][:, t, :], in0=x_in[g.s][:, t, :], in1=bp_row[:, :], op=ALU.add)
                last.then_inc(xb_done, 1)

            def stage_a(g):
                pool.wait_ge(aggr_done, g.n + 1)
                pool.tensor_tensor(out=var_eps[g.s][:, :], in0=meanvar[g.s][:, :, 1], in1=eps[:, :], op=ALU.add).then_inc(eps_done, 1)
                pool.wait_ge(eps_done, g.n + 1)
                pool.tensor_tensor(out=rstd[g.s][:, 0, :], in0=var_eps[g.s][:, :], in1=half_neg[:, :], op=ALU.pow).then_inc(pow_done, 1)

            def add_b2(g):
                pool.wait_ge(y_done, g.n + 1)
                need(pool, res_done, g.n - 1)
                for t in range(TILES):
                    last = pool.tensor_tensor(out=y_b[g.s][:, t, :], in0=y[g.s][:, t, :], in1=b2_row[:, :], op=ALU.add)
                last.then_inc(yb_done, 1)

            def stage_c(g):
                pool.wait_ge(scaled, g.n + 1)
                pool.wait_ge(yb_done, g.n + 1)
                need(pool, stored[g.s], g.it * 16)
                pool.tensor_tensor(out=res[g.s][:, :, :], in0=ffn[g.s][:, :, :], in1=y_b[g.s][:, :, :], op=ALU.add).then_inc(res_done, 1)

            add_bias(FIRST)
            stage_a(FIRST)
            add_b2(FIRST)
            add_bias(FIRST.after(1))

            def emit(g):
                if not g.last:
                    stage_a(g.after(1))
                if not (g.last or g.after(1).last):
                    add_bias(g.after(2))
                if not g.first:
                    stage_c(g.after(-1))
                if not g.last:
                    add_b2(g.after(1))

            each_group(pool, emit)
            stage_c(LAST)

        @block.vector
        def _(dve):
            def stage_a(g):
                st, mv, rs = stats[g.s], meanvar[g.s], rstd[g.s]
                dve.wait_ge(xb_done, g.n + 1)
                dve.wait_ge(proj_done, g.n + 1)
                need(dve, yb_done, g.n - 1)
                dve.tensor_tensor(y[g.s][:, :, :], p_ps[:, :, 0:C], x_in[g.s][:, :, :], ALU.add).then_inc(y_done, 1)
                dve.wait_ge(y_done, g.n + 1)
                for t in range(TILES):
                    last = dve.bn_stats(st[:, t, :], y[g.s][:, t, :])
                last.then_inc(stats_done, 1)
                dve.wait_ge(stats_done, g.n + 1)
                dve.memset(rs[:, 1, :], 0.0)
                for t in range(TILES):
                    last = dve.bn_aggr(mv[:, t, :], st[:, t, :])
                last.then_inc(aggr_done, 1)
                dve.wait_ge(pow_done, g.n + 1)
                r0, r1, r2 = (rs[:, i, :] for i in range(3))
                dve.tensor_tensor(r1, r0, r0, ALU.mult).then_inc(newton, 1)
                dve.wait_ge(newton, g.n * 3 + 1)
                dve.scalar_tensor_tensor(out=r2, in0=r1, scalar=-0.5, in1=var_eps[g.s][:, :], op0=ALU.mult, op1=ALU.mult).then_inc(newton, 1)
                dve.wait_ge(newton, g.n * 3 + 2)
                dve.scalar_tensor_tensor(out=r1, in0=r2, scalar=1.5, in1=r0, op0=ALU.add, op1=ALU.mult).then_inc(newton, 1)
                dve.wait_ge(newton, g.n * 3 + 3)
                for t in range(TILES):
                    last = dve.tensor_scalar(y_n[:, t, :], y[g.s][:, t, :], mv[:, t, 0:1], rs[:, 1, t:t + 1], ALU.subtract, ALU.mult)
                last.then_inc(yn_done, 1)
                dve.wait_ge(yn_done, g.n + 1)
                dve.tensor_scalar(y_r[:, :, :], y_n[:, :, :], wt.inv_a1, MAGIC, ALU.mult, ALU.add).then_inc(yr_done, 1)
                dve.wait_ge(yr_done, g.n + 1)
                dve.tensor_scalar(y_n[:, :, :], y_r[:, :, :], MAGIC + QP, MAGIC + QN, ALU.min, ALU.max).then_inc(yi_done, 1)
                dve.wait_ge(yi_done, g.n + 1)
                need(dve, t_done, g.n - 1)
                dve.tensor_scalar(y_q[g.s][:, :, :], y_n[:, :, :], -MAGIC, None, ALU.add).then_inc(yq_done, 1)

            def stage_b(g):
                need(dve, f_done, g.n - 1)
                for hf in range(2):
                    part = slice(hf * half_h, (hf + 1) * half_h)
                    dve.wait_ge(round_done, g.n * 2 + hf + 1)
                    dve.tensor_scalar(hid_r[:, part, :], hid_r[:, part, :], wt.bound[:, 2:3], wt.bound[:, 3:4], ALU.min, ALU.max).then_inc(bound_done, 1)
                    dve.wait_ge(bound_done, g.n * 2 + hf + 1)
                    dve.tensor_scalar(hid_q[g.s][:, part, :], hid_r[:, part, :], -MAGIC, None, ALU.add).then_inc(hq_done, 1)

            def stage_c(g):
                dve.wait_ge(f_done, g.n + 1)
                need(dve, res_done, g.n - 1)
                for t in range(TILES):
                    last = dve.tensor_tensor(ffn[g.s][:, t, :], f_ps[:, t, 0:C], wt.s2_row[:, :], ALU.mult)
                last.then_inc(scaled, 1)

            dve.memset(magic[:, :], MAGIC).then_inc(magic_made, 1)
            stage_a(FIRST)

            def emit(g):
                if not g.last:
                    stage_a(g.after(1))
                stage_b(g)
                if not g.first:
                    stage_c(g.after(-1))

            each_group(dve, emit)
            stage_c(LAST)

        @block.scalar
        def _(act):
            act.wait_ge(magic_made, 1)
            act.wait_ge(params_in, 16 * N_PARAMS)

            def emit(g):
                act.wait_ge(t_done, g.n + 1)
                need(act, h_done, (g.n - 1) * HT)
                act.activation(y_t[g.s][:, :, :], t_ps[0:HALF, :, :], ACT.Copy).then_inc(yt_ready, 1)
                need(act, round_done, g.n * 2)
                for t in range(HT):
                    act.wait_ge(h_done, g.n * HT + t + 1)
                    act.activation(hid[:, t, :], h_ps[t % 3][:, :], ACT.Gelu, bias=b1_sb[:, t:t + 1], scale=wt.s1[:, t:t + 1]).then_inc(gelu_done, 1)
                need(act, hq_done, g.n * 2)
                for hf in range(2):
                    part = slice(hf * half_h, (hf + 1) * half_h)
                    act.wait_ge(gelu_done, g.n * HT + (hf + 1) * half_h)
                    act.activation(hid_r[:, part, :], hid[:, part, :], ACT.Identity, bias=magic[:, 0:1], scale=wt.inv_a2).then_inc(round_done, 1)

            each_group(act, emit)

        @block.tensor
        def _(pe):
            def project(g):
                pe.wait_ge(att_loaded[g.s], (g.it + 1) * 16)
                need(pe, y_done, g.n)
                for t in range(TILES):
                    for quad in range(NQUAD):
                        last = pe.matmul(p_ps[:, t, 0:C], att[g.s][:, quad, t * P:(t + 1) * P], wp_sb[:, quad, :],
                                         start=(quad == 0), stop=(quad == NQUAD - 1))
                last.then_inc(proj_done, 1)

            def hidden(g):
                pe.wait_ge(yq_done, g.n + 1)
                need(pe, yt_ready, g.n)
                for t in range(TILES):
                    for h in range(2):
                        last = pe.transpose(t_ps[0:HALF, h, t * P:(t + 1) * P], y_q[g.s][:, t, h * HALF:(h + 1) * HALF], ident[:, :])
                last.then_inc(t_done, 1)
                pe.wait_ge(yt_ready, g.n + 1)
                for t in range(HT):
                    need(pe, gelu_done, g.n * HT + t - 2)
                    for h in range(2):
                        last = pe.matmul(h_ps[t % 3][:, :], wt.w1_t[:, h, t * P:(t + 1) * P], y_t[g.s][:, h, :], start=(h == 0), stop=(h == 1))
                    last.then_inc(h_done, 1)

            def second(g):
                need(pe, scaled, g.n)
                pe.wait_ge(hq_done, g.n * 2 + 2)
                for t in range(TILES):
                    for k in range(HT):
                        last = pe.matmul(f_ps[:, t, 0:C], hid_q[g.s][:, k, t * P:(t + 1) * P], wt.w2_t[:, k, :], start=(k == 0), stop=(k == HT - 1))
                last.then_inc(f_done, 1)

            pe.wait_ge(ident_made, 1)
            pe.wait_ge(params_in, 16 * N_PARAMS)
            project(FIRST)

            def emit(g):
                if not g.last:
                    project(g.after(1))
                hidden(g)
                if not g.first:
                    second(g.after(-1))

            each_group(pe, emit)
            second(LAST)


def build(nc, a, out):
    qk_dram = nc.dram_tensor("qk_parts", (UNITS, 2, 2, QC, SEQ), F16).ap()
    v_dram = nc.dram_tensor("v_units", (UNITS, P, KT, QUAD * SLOT), F32).ap()
    bias_dram = nc.dram_tensor("bias_parts", (UNITS, 2, 2, P, SEQ), F16).ap()
    att_dram = nc.dram_tensor("att", (GROUPS, P, NQUAD, GROUP), F32).ap()
    phase_project(nc, a["x"], a["Wq"], a["bq"], a["Wk"], a["bk"], a["Wv"], a["bv"], qk_dram, v_dram)
    with ExitStack() as kept:
        weights = Weights(kept, nc, a["w1"], a["alpha_w1"], a["alpha_a1"], a["w2"], a["alpha_w2"], a["alpha_w2_cols"], a["alpha_a2"])
        phase_rel_bias(nc, a["rel_h"], a["rel_w"], qk_dram, bias_dram, weights)
        phase_attention(nc, qk_dram, v_dram, bias_dram, att_dram)
        phase_ffn(nc, a["x"], a["Wp"], a["bp"], a["b1"], a["b2"], weights, att_dram, out)


def kernel(**inputs):
    import numpy as _np
    import concourse.bacc as _bacc
    from concourse import mybir as _mybir
    from concourse.bass_utils import run_bass_kernel_spmd as _run

    nc = _bacc.Bacc("TRN2", target_bir_lowering=False, num_devices=1)
    arrays, args = {}, {}
    for name, value in inputs.items():
        value = _np.asarray(value)
        short = name.replace("L0_conv_", "").replace("L0_ffn_", "")
        if short == "x":
            value = value.reshape(TOKENS, C)
        if short in ("rel_h", "rel_w"):
            value = value[::-1].T
        laid = {short: value}
        if short in ("b1", "alpha_w1"):
            laid = {short: value.reshape(HT, P).T}
        if short == "alpha_w2":
            laid["alpha_w2_cols"] = value.reshape(2, HALF).T
        for key, array in laid.items():
            array = _np.ascontiguousarray(array)
            arrays[f"in_{key}"] = array
            args[key] = nc.dram_tensor(f"in_{key}", array.shape, _mybir.dt.from_np(array.dtype), kind="ExternalInput").ap()
    out = nc.dram_tensor("out_0", (TOKENS, C), _mybir.dt.float32, kind="ExternalOutput").ap()
    build(nc, args, out)
    r = _run(nc, [arrays], core_ids=[0])
    return r.results[0]["out_0"].reshape(BATCH, GRID, GRID, C)
```

```python
from contextlib import ExitStack

import concourse.bass as bass
from concourse import mybir

F32 = mybir.dt.float32
F16 = mybir.dt.float16
BF16 = mybir.dt.bfloat16
ALU = mybir.AluOpType
ACT = mybir.ActivationFunctionType
AX_X = mybir.AxisListType.X

P = 128
BATCH, GRID, C = 4, 32, 192
SEQ = GRID * GRID
TOKENS = BATCH * SEQ
NH = 12
HD = C // NH
QUAD = 4
NQUAD = NH // QUAD
QC = QUAD * HD
UNITS = BATCH * NQUAD
REL = 2 * GRID - 1
HALF = C // 2
GROUP = 512
TILES = GROUP // P
GROUPS = TOKENS // GROUP
HID = 768
HT = HID // P
KT = SEQ // P
SLOT = 32
BLK = GRID // 2
MAGIC = 1.5 * 2.0 ** 23
QN, QP = -8.0, 7.0


def need(eng, sem, value):
    if not isinstance(value, int) or value > 0:
        eng.wait_ge(sem, value)


class Group:

    def __init__(self, it, s):
        self.it, self.s, self.n = it, s, it * 2 + s
        self.first = isinstance(it, int) and self.n == 0
        self.last = isinstance(it, int) and self.n == GROUPS - 1

    def after(self, k):
        return Group(self.it + (self.s + k) // 2, (self.s + k) % 2)


FIRST, LAST = Group(0, 0), Group(GROUPS // 2 - 1, 1)


def each_group(eng, emit):
    for s in range(2):
        emit(Group(0, s))
    with eng.Fori(1, GROUPS // 2 - 1) as it:
        for s in range(2):
            emit(Group(it, s))
    for s in range(2):
        emit(Group(GROUPS // 2 - 1, s))


class Phase:

    def __init__(self, nc, name):
        self.nc, self.name, self.stack = nc, name, ExitStack()

    def __enter__(self):
        self.stack.__enter__()
        return self

    def __exit__(self, *a):
        return self.stack.__exit__(*a)

    def sb(self, name, shape, dt):
        return self.stack.enter_context(self.nc.sbuf_tensor(f"{self.name}_{name}", shape, dt))

    def ps(self, name, shape, dt):
        return self.stack.enter_context(self.nc.psum_tensor(f"{self.name}_{name}", shape, dt))

    def sem(self, name):
        return self.stack.enter_context(self.nc.semaphore(f"{self.name}_{name}"))

    def block(self):
        return self.stack.enter_context(self.nc.Block())


def make_identity(pool, tile, cleared, done):
    n = tile.shape[0]
    pool.memset(tile[:, :], 0.0).then_inc(cleared, 1)
    pool.wait_ge(cleared, 1)
    pool.affine_select(out=tile[:, :], in_=tile[:, :], compare_op=ALU.not_equal, fill=1.0, base=0,
                       pattern=[[-1, n]], channel_multiplier=1).then_inc(done, 1)




class Keep:

    def __init__(self, nc, stack, name):
        self.nc, self.stack, self.name = nc, stack, name

    sb, sem = Phase.sb, Phase.sem


class Operands(Keep):

    VARIANTS = 5
    TILE_ORDER = (2, 3, 4, 5, 6, 7, 0, 1)
    VARIANT_OF = (3, 4, 0, 0, 1, 1, 2, 2)
    SEGMENTS = ((3, 0, P), (4, P, P), (0, 2 * P, 2 * P), (1, 4 * P, 2 * P), (2, 6 * P, 2 * P))
    A_AT, B_AT, MAX_ROW = 4 * HD, 4 * HD + 2 * BLK, 4 * HD + 2 * BLK + 2 * (BLK - 1)
    N_LOADS = 4 + 4 + 1 + 2 * (4 + 5)
    assert MAX_ROW == P - 2

    def __init__(self, nc, stack, kept, qk_dram, v_dram, bias_dram):
        super().__init__(nc, stack, "op")
        self.qk_dram, self.v_dram, self.bias_dram = qk_dram, v_dram, bias_dram
        self.mix_q = [kept] + [self.sb(f"mix_q{i}", [P, self.VARIANTS, QUAD, SEQ], F16) for i in (1, 2)]
        self.mix_k = [self.sb(f"mix_k{i}", [P, QUAD, SEQ], F16) for i in range(3)]
        self.v_u = [self.sb(f"v_u{i}", [P, KT, QUAD, SLOT], F32) for i in range(3)]
        self.ident = self.sb("ident", [P, P], F32)
        self.sum_pick = self.sb("sum_pick", [P, QUAD], F32)
        self.consts, self.const_step, self.hot_out = self.sem("consts"), self.sem("const_step"), self.sem("hot_out")
        self.loaded = [self.sem(f"loaded{i}") for i in range(3)]
        early, late = (m[:, :, :, :].rearrange("p v j t -> p (v j t)") for m in self.mix_q[1:])
        tokens = BATCH * SEQ
        self.q_parts = [early[:, i * tokens:(i + 1) * tokens].rearrange("p (b t) -> p b t", b=BATCH) for i in range(NQUAD)]
        self.row_table = early[:, NQUAD * tokens:NQUAD * tokens + 2 * GRID * P]
        self.stage = [late[:, i * 2 * tokens:(i + 1) * 2 * tokens].rearrange("p (h b t) -> p h b t", h=2, b=BATCH) for i in range(2)]
        self.parts_area = late[:, 0:12 * GROUP]
        self.spare = late[:, 4 * tokens:].bitcast(F32)
        self.last_stored = self.sem("last_stored")

    def make_consts(self, pool, hot_a, hot_b, ones):
        consts, const_step, sum_pick = self.consts, self.const_step, self.sum_pick
        make_identity(pool, self.ident, const_step, consts)
        pool.memset(sum_pick[:, :], 0.0).then_inc(const_step, 1)
        pool.memset(hot_a[:, :], 0.0).then_inc(const_step, 1)
        pool.memset(hot_b[:, :], 0.0).then_inc(const_step, 1)
        pool.memset(ones[:, :], 1.0).then_inc(const_step, 1)
        pool.wait_ge(const_step, 5)
        pool.affine_select(out=sum_pick[:, :], in_=sum_pick[:, :], compare_op=ALU.not_equal, fill=1.0, base=-HD,
                           pattern=[[-SLOT, QUAD]], channel_multiplier=1).then_inc(consts, 1)
        rows, cols = [[-1, BLK], [0, BLK]], [[0, BLK], [-1, BLK]]
        block = BLK * BLK
        marks = []
        for upper in (0, 2 * block):
            marks.append((hot_a, upper, block, cols))
            marks.append((hot_a, upper + block, block, rows))
            marks.append((hot_b, upper + block, block, cols))
        marks += [(hot_b, 2 * block, block, rows), (hot_b, 0, P, rows), (hot_b, P, P, rows)]
        for tile, at, n, pattern in marks:
            keys = tile[:, at:at + n].rearrange("p (r c) -> p r c", c=BLK)
            pool.affine_select(out=keys, in_=keys, compare_op=ALU.not_equal, fill=1.0, base=0,
                               pattern=[[pattern[0][0], n // BLK], pattern[1]], channel_multiplier=1).then_inc(const_step, 1)
        pool.wait_ge(const_step, 5 + len(marks))
        for i in range(3):
            for part in range(2):
                for at, hot, n in ((self.A_AT + part * BLK, hot_a, BLK), (self.B_AT + part * (BLK - 1), hot_b, BLK - 1)):
                    pool.dma_start(self.mix_k[i][at:at + n, :, :], hot[0:n, :].unsqueeze(1).to_broadcast([n, QUAD, SEQ])).then_inc(self.hot_out, 16)
            pool.dma_start(self.mix_k[i][self.MAX_ROW:P, :, :], ones[:, :].unsqueeze(1).to_broadcast([2, QUAD, SEQ])).then_inc(self.hot_out, 16)
        pool.wait_ge(self.hot_out, 16 * 15)
        pool.nop().then_inc(consts, 1)

    def load_qkv(self, sp, image, i):
        def q_or_k(which, part):
            chunk, half = ((which, i), (2, which))[i == 2]
            src = self.qk_dram[bass.ds(image, 1), chunk, part, half * QC:(half + 1) * QC, :]
            return src.rearrange("b (d j) t -> (b d) (j t)", d=HD)

        for r, part in enumerate((0, 0, 1, 1)):
            src = q_or_k(0, part).unsqueeze(1).to_broadcast([HD, self.VARIANTS, QUAD * SEQ])
            sp.dma_start(self.mix_q[i][r * HD:(r + 1) * HD, :, :, :].rearrange("p v j t -> p v (j t)"), src).then_inc(self.loaded[i], 16)
        for r, part in enumerate((0, 1, 0, 1)):
            sp.dma_start(self.mix_k[i][r * HD:(r + 1) * HD, :, :].rearrange("p j t -> p (j t)"), q_or_k(1, part)).then_inc(self.loaded[i], 16)
        sp.dma_start(self.v_u[i][:, :, :, :].rearrange("p k h e -> p k (h e)"),
                     self.v_dram[bass.ds(image, 1), :, :, i * QUAD * SLOT:(i + 1) * QUAD * SLOT].rearrange("b p k e -> (b p) k e")).then_inc(self.loaded[i], 16)

    def load_bias(self, sp, u, i):
        ROW, COL = 0, 1
        a_parts = ((3, COL, 0), (0, ROW, 0), (1, COL, 0), (2, ROW, BLK))
        b_parts = ((3, ROW, 0), (4, ROW, BLK // 2), (0, COL, BLK), (1, ROW, BLK), (2, COL, BLK))
        for part in range(2):
            for at, n, fill in ((self.A_AT + part * BLK, BLK, a_parts), (self.B_AT + part * (BLK - 1), BLK - 1, b_parts)):
                for variant, t, first in fill:
                    src = self.bias_dram[bass.ds(u, 1), part, t, first * QUAD:(first + n) * QUAD, :]
                    src = src.rearrange("u (r j) q -> (u r) (j q)", j=QUAD)
                    if fill is a_parts and variant == 3:
                        sp.dma_start(self.mix_q[i][at:at + n, 3:5, :, :].rearrange("p v j t -> p v (j t)"),
                                     src.unsqueeze(1).to_broadcast([n, 2, QUAD * SEQ])).then_inc(self.loaded[i], 16)
                        continue
                    sp.dma_start(self.mix_q[i][at:at + n, variant, :, :].rearrange("p j t -> p (j t)"), src).then_inc(self.loaded[i], 16)


class FfnInputs(Keep):

    N_PARAMS = 3 + NH

    def __init__(self, nc, stack, area, x, wp, bp, b1, b2, att_dram):
        super().__init__(nc, stack, "fi")
        self.wp, self.bp, self.b1, self.b2, self.att_dram = wp, bp, b1, b2, att_dram
        self.x_v = x.rearrange("(n t p) c -> n p t c", t=TILES, p=P)
        self.wp_sb = self.sb("wp_sb", [P, NQUAD, C], F32)
        area, x_len, att_len = area[:, :, :, :].bitcast(F32).rearrange("p v j t -> p (v j t)"), TILES * C, NQUAD * GROUP
        self.x_in = [area[:, s * x_len:(s + 1) * x_len].rearrange("p (t c) -> p t c", c=C) for s in range(2)]
        self.att = [area[:, 2 * x_len + s * att_len:2 * x_len + (s + 1) * att_len].rearrange("p (g t) -> p g t", t=GROUP) for s in range(2)]
        rest = area[:, 2 * (x_len + att_len):]
        self.bp_row, self.b2_row, self.b1_sb = rest[:, 0:C], rest[:, C:2 * C], rest[:, 2 * C:2 * C + HT]
        self.params_in, self.wp_zeroed = self.sem("params_in"), self.sem("wp_zeroed")
        self.x_loaded = [self.sem(f"x_loaded{s}") for s in range(2)]
        self.att_loaded = [self.sem(f"att_loaded{s}") for s in range(2)]

    def clear(self, pool):
        pool.memset(self.wp_sb[:, :, :], 0.0).then_inc(self.wp_zeroed, 1)

    def load_biases(self, sp):
        for dst, src in ((self.bp_row, self.bp.partition_broadcast(P)), (self.b2_row, self.b2.partition_broadcast(P)), (self.b1_sb, self.b1)):
            sp.dma_start(dst[:, :], src).then_inc(self.params_in, 16)

    def load_wp(self, sp):
        sp.wait_ge(self.wp_zeroed, 1)
        for quad in range(NQUAD):
            for head in range(QUAD):
                r = (quad * QUAD + head) * HD
                sp.dma_start(self.wp_sb[head * SLOT:head * SLOT + HD, quad, :], self.wp[r:r + HD, :]).then_inc(self.params_in, 16)

    def load(self, sp, g):
        sp.dma_start(self.att[g.s][:, :, :], self.att_dram[bass.ds(g.n, 1), :, :, :].rearrange("n p g t -> (n p) g t")).then_inc(self.att_loaded[g.s], 16)
        sp.dma_start(self.x_in[g.s][:, :, :], self.x_v[bass.ds(g.n, 1), :, :, :].rearrange("n p t c -> (n p) t c")).then_inc(self.x_loaded[g.s], 16)


class RelTables(Keep):

    def __init__(self, nc, stack, rel_h, rel_w):
        super().__init__(nc, stack, "rt")
        self.rel_h, self.rel_w = rel_h, rel_w
        self.rel = [self.sb(f"rel{t}", [P, REL, QUAD], F32) for t in range(2)]
        self.rel_rows = [self.sb(f"rel_rows{t}", [P, REL], F32) for t in range(2)]
        self.own2 = self.sb("own2", [P, P // QUAD, QUAD], F32)
        self.own = self.sb("own", [P, QUAD], F32)
        self.mask_step, self.rel_in, self.own_made = (self.sem(n) for n in ("mask_step", "rel_in", "own_made"))

    def make_mask(self, pool):
        own2, mask_step = self.own2, self.mask_step
        pool.memset(own2[:, :, :], 0.0).then_inc(mask_step, 1)
        pool.wait_ge(mask_step, 1)
        pool.affine_select(out=own2[:, :, :], in_=own2[:, :, :], compare_op=ALU.not_equal, fill=1.0, base=0,
                           pattern=[[-QUAD, P // QUAD], [-1, QUAD]], channel_multiplier=1).then_inc(mask_step, 1)

    def load(self, sp):
        for t, src in enumerate((self.rel_h, self.rel_w)):
            for part in range(2):
                sp.dma_start(self.rel_rows[t][part * QC:(part + 1) * QC, :], src.unsqueeze(1).to_broadcast([HD, QUAD, REL])).then_inc(self.rel_in, 16)

    def make(self, dve):
        own, own2 = self.own, self.own2
        dve.wait_ge(self.mask_step, 2)
        dve.tensor_reduce(own[:, :], own2[:, :, :].rearrange("p a j -> p j a"), AX_X, ALU.add).then_inc(self.own_made, 1)
        dve.wait_ge(self.rel_in, 16 * 4)
        dve.wait_ge(self.own_made, 1)
        for t in range(2):
            for head in range(QUAD):
                dve.tensor_scalar(self.rel[t][:, :, head], self.rel_rows[t][:, :], own[:, head:head + 1], None, ALU.mult)


def phase_project(nc, x, wq, bq, wk, bk, wv, bv, tables, ops, qk_dram, v_dram):
    with Phase(nc, "pr") as ph:
        ident = ph.sb("ident", [P, P], F32)
        w_qk = ph.sb("w_qk", [HALF, 2, 3, P], F32)
        w_v = ph.sb("w_v", [HALF, 2, C], F32)
        b_qk = ph.sb("b_qk", [P, 3], F32)
        s_qk = ph.sb("s_qk", [P, 3], F32)
        b_v = ph.sb("b_v", [P, C], F32)
        half_neg = ph.sb("half_neg", [P, TILES], F32)
        eps = ph.sb("eps", [P, TILES], F32)
        x_in = [ph.sb(f"x_in{s}", [P, TILES, C], F32) for s in range(2)]
        x_n = [ph.sb(f"x_n{s}", [P, TILES, C], F32) for s in range(2)]
        x_t = [ph.sb(f"x_t{s}", [HALF, 2, GROUP], F32) for s in range(2)]
        stats = [ph.sb(f"stats{s}", [P, TILES, 6], F32) for s in range(2)]
        meanvar = [ph.sb(f"meanvar{s}", [P, TILES, 2], F32) for s in range(2)]
        var_eps = [ph.sb(f"var_eps{s}", [P, TILES], F32) for s in range(2)]
        rstd = [ph.sb(f"rstd{s}", [P, 3, TILES], F32) for s in range(2)]
        early = ops.mix_q[0][:, :, :, :].bitcast(F32).rearrange("p v j t -> p (v j t)")
        full = [early[:, s * 3 * GROUP:(s + 1) * 3 * GROUP].rearrange("p (c t) -> p c t", c=3) for s in range(2)]
        parts = [ops.parts_area[:, s * 6 * GROUP:(s + 1) * 6 * GROUP].rearrange("p (c h t) -> p c h t", c=3, h=2) for s in range(2)]
        v_st = [ph.sb(f"v_st{s}", [P, TILES, NH, SLOT], F32) for s in range(2)]
        t_ps = ph.ps("t_ps", [P, 2, GROUP], F32)
        qk_ps = [ph.ps(f"qk_ps{c}", [P, GROUP], F32) for c in range(3)]
        v_ps = ph.ps("v_ps", [P, TILES, 256], F32)

        weights_in = ph.sem("weights_in")
        zeroed, ident_made, consts_made, pool_consts = (ph.sem(n) for n in ("zeroed", "ident_made", "consts_made", "pool_consts"))
        x_loaded = [ph.sem(f"x_loaded{s}") for s in range(2)]
        stored = [ph.sem(f"stored{s}") for s in range(2)]
        stats_done, aggr_done, eps_done, pow_done = (ph.sem(n) for n in ("stats_done", "aggr_done", "eps_done", "pow_done"))
        newton, xn_done, xt_ready, t_done = (ph.sem(n) for n in ("newton", "xn_done", "xt_ready", "t_done"))
        qk_done, v_done, f32_done, hi_done, lo_done, v_out = (
            ph.sem(n) for n in ("qk_done", "v_done", "f32_done", "hi_done", "lo_done", "v_out"))
        n_weights, per_group = 10, 10
        block = ph.block()
        x_v = x.rearrange("(n t p) c -> n p t c", t=TILES, p=P)

        @block.sync
        def _(sp):
            def load(g):
                sp.dma_start(x_in[g.s][:, :, :], x_v[bass.ds(g.n, 1), :, :, :].rearrange("n p t c -> (n p) t c")).then_inc(x_loaded[g.s], 16)

            load(Group(0, 0))
            load(Group(0, 1))
            for w, c0, c1, q0 in ((wq, 0, P, 0), (wk, 0, P, 1)):
                sp.dma_start(w_qk[:, :, q0, :], w[:, c0:c1].rearrange("(h p) c -> p h c", h=2)).then_inc(weights_in, 16)
            for w, b, at in ((wq, bq, 0), (wk, bk, QC)):
                sp.dma_start(w_qk[:, :, 2, at:at + QC], w[:, P:C].rearrange("(h p) c -> p h c", h=2)).then_inc(weights_in, 16)
                sp.dma_start(b_qk[at:at + QC, 2:3], b[P:C].rearrange("(p o) -> p o", o=1)).then_inc(weights_in, 16)
            for b, q0 in ((bq, 0), (bk, 1)):
                sp.dma_start(b_qk[:, q0:q0 + 1], b[0:P].rearrange("(p o) -> p o", o=1)).then_inc(weights_in, 16)
            sp.dma_start(w_v[:, :, :], wv.rearrange("(h p) c -> p h c", h=2)).then_inc(weights_in, 16)
            sp.dma_start(b_v[:, :], bv.partition_broadcast(P)).then_inc(weights_in, 16)
            tables.load(sp)

            def emit(g):
                if not (g.last or g.after(1).last):
                    sp.wait_ge(xn_done, g.n + 1)
                    load(g.after(2))
                image = g.it
                for c in range(3):
                    sp.wait_ge(hi_done, g.n * 3 + c + 1)
                    sp.wait_ge(lo_done, g.n * 3 + c + 1)
                    dst = qk_dram[bass.ds(image, 1), c, :, :, g.s * GROUP:(g.s + 1) * GROUP]
                    sp.dma_start(dst.rearrange("b h r t -> (b r) h t"), parts[g.s][:, c, :, :]).then_inc(stored[g.s], 16)
                    for half, quad in (((0, 0), (1, 1)), (), ((0, 2),))[c]:
                        for part in range(2):
                            sp.dma_start(ops.q_parts[quad][part * QC:(part + 1) * QC, bass.ds(image, 1), g.s * GROUP:(g.s + 1) * GROUP],
                                         parts[g.s][half * QC:(half + 1) * QC, c, part:part + 1, :]).then_inc(stored[g.s], 16)
                sp.wait_ge(v_out, g.n + 1)
                sp.dma_start(v_dram[bass.ds(image, 1), :, g.s * TILES:(g.s + 1) * TILES, :].rearrange("b p t e -> (b p) t e"),
                             v_st[g.s][:, :, :, :].rearrange("p t h e -> p t (h e)")).then_inc(stored[g.s], 16)

            each_group(sp, emit)
            for s in range(2):
                sp.wait_ge(stored[s], 16 * per_group * (GROUPS // 2))

        @block.gpsimd
        def _(pool):
            make_identity(pool, ident, zeroed, ident_made)
            pool.memset(eps[:, :], 1e-6).then_inc(pool_consts, 1)
            pool.memset(half_neg[:, :], -0.5).then_inc(pool_consts, 1)
            pool.wait_ge(pool_consts, 2)

            def inverse_std(g):
                pool.wait_ge(aggr_done, g.n + 1)
                pool.tensor_tensor(out=var_eps[g.s][:, :], in0=meanvar[g.s][:, :, 1], in1=eps[:, :], op=ALU.add).then_inc(eps_done, 1)
                pool.wait_ge(eps_done, g.n + 1)
                pool.tensor_tensor(out=rstd[g.s][:, 0, :], in0=var_eps[g.s][:, :], in1=half_neg[:, :], op=ALU.pow).then_inc(pow_done, 1)

            inverse_std(FIRST)
            tables.make_mask(pool)

            def emit(g):
                if not g.last:
                    inverse_std(g.after(1))
                for c in range(3):
                    pool.wait_ge(hi_done, g.n * 3 + c + 1)
                    pool.tensor_tensor(out=parts[g.s][:, c, 1, :], in0=full[g.s][:, c, :], in1=parts[g.s][:, c, 0, :],
                                       op=ALU.subtract).then_inc(lo_done, 1)

            each_group(pool, emit)

        @block.vector
        def _(dve):
            def normalise(g):
                x_g, st, mv, rs = x_in[g.s], stats[g.s], meanvar[g.s], rstd[g.s]
                dve.wait_ge(x_loaded[g.s], (g.it + 1) * 16)
                for t in range(TILES):
                    last = dve.bn_stats(st[:, t, :], x_g[:, t, :])
                last.then_inc(stats_done, 1)
                dve.wait_ge(stats_done, g.n + 1)
                dve.memset(rs[:, 1, :], 0.0)
                for t in range(TILES):
                    last = dve.bn_aggr(mv[:, t, :], st[:, t, :])
                last.then_inc(aggr_done, 1)
                dve.wait_ge(pow_done, g.n + 1)
                r0, r1, r2 = (rs[:, i, :] for i in range(3))
                dve.tensor_tensor(r1, r0, r0, ALU.mult).then_inc(newton, 1)
                dve.wait_ge(newton, g.n * 3 + 1)
                dve.scalar_tensor_tensor(out=r2, in0=r1, scalar=-0.5, in1=var_eps[g.s][:, :], op0=ALU.mult, op1=ALU.mult).then_inc(newton, 1)
                dve.wait_ge(newton, g.n * 3 + 2)
                dve.scalar_tensor_tensor(out=r1, in0=r2, scalar=1.5, in1=r0, op0=ALU.add, op1=ALU.mult).then_inc(newton, 1)
                dve.wait_ge(newton, g.n * 3 + 3)
                need(dve, t_done, g.n - 1)
                for t in range(TILES):
                    last = dve.tensor_scalar(x_n[g.s][:, t, :], x_g[:, t, :], mv[:, t, 0:1], rs[:, 1, t:t + 1], ALU.subtract, ALU.mult)
                last.then_inc(xn_done, 1)

            dve.memset(s_qk[:, :], 1.0).then_inc(consts_made, 1)
            dve.wait_ge(consts_made, 1)
            dve.memset(s_qk[:, 1:2], HD ** -0.5).then_inc(consts_made, 1)
            dve.memset(s_qk[QC:P, 2:3], HD ** -0.5).then_inc(consts_made, 1)
            for s in range(2):
                dve.memset(v_st[s][:, :, :, :], 1.0).then_inc(consts_made, 1)
            normalise(FIRST)
            dve.wait_ge(weights_in, 16 * n_weights)
            dve.wait_ge(consts_made, 5)

            def emit(g):
                if not g.last:
                    normalise(g.after(1))
                need(dve, lo_done, (g.n - 1) * 3)
                for c in range(3):
                    dve.wait_ge(qk_done, g.n * 3 + c + 1)
                    dve.tensor_scalar(full[g.s][:, c, :], qk_ps[c][:, :], b_qk[:, c:c + 1], s_qk[:, c:c + 1], ALU.add, ALU.mult).then_inc(f32_done, 1)
                dve.wait_ge(v_done, g.n + 1)
                need(dve, stored[g.s], g.it * (16 * per_group))
                for t in range(TILES):
                    last = dve.tensor_tensor(v_st[g.s][:, t, :, 0:HD], v_ps[:, t, 0:C].rearrange("p (h d) -> p h d", d=HD),
                                             b_v[:, :].rearrange("p (h d) -> p h d", d=HD), ALU.add)
                last.then_inc(v_out, 1)

            each_group(dve, emit)
            tables.make(dve)

        @block.scalar
        def _(act):
            def take_turned(g):
                act.wait_ge(t_done, g.n + 1)
                need(act, v_done, g.n - 1)
                act.activation(x_t[g.s][:, :, :], t_ps[0:HALF, :, :], ACT.Copy).then_inc(xt_ready, 1)

            take_turned(FIRST)

            def emit(g):
                need(act, stored[g.s], g.it * (16 * per_group))
                for c in range(3):
                    act.wait_ge(f32_done, g.n * 3 + c + 1)
                    act.activation(parts[g.s][:, c, 0, :], full[g.s][:, c, :], ACT.Copy).then_inc(hi_done, 1)
                    if c == 0 and not g.last:
                        take_turned(g.after(1))

            each_group(act, emit)

        @block.tensor
        def _(pe):
            def turn(g):
                pe.wait_ge(xn_done, g.n + 1)
                need(pe, xt_ready, g.n)
                for t in range(TILES):
                    for h in range(2):
                        last = pe.transpose(t_ps[0:HALF, h, t * P:(t + 1) * P], x_n[g.s][:, t, h * HALF:(h + 1) * HALF], ident[:, :])
                last.then_inc(t_done, 1)

            pe.wait_ge(ident_made, 1)
            turn(FIRST)
            pe.wait_ge(weights_in, 16 * n_weights)

            def emit(g):
                pe.wait_ge(xt_ready, g.n + 1)
                for c in range(3):
                    need(pe, f32_done, (g.n - 1) * 3 + c + 1)
                    for h in range(2):
                        last = pe.matmul(qk_ps[c][:, :], w_qk[:, h, c, :], x_t[g.s][:, h, :], start=(h == 0), stop=(h == 1))
                    last.then_inc(qk_done, 1)
                if not g.last:
                    turn(g.after(1))
                need(pe, v_out, g.n)
                for t in range(TILES):
                    for h in range(2):
                        last = pe.matmul(v_ps[:, t, 0:C], x_t[g.s][:, h, t * P:(t + 1) * P], w_v[:, h, :], start=(h == 0), stop=(h == 1))
                last.then_inc(v_done, 1)

            each_group(pe, emit)


def phase_rel_bias(nc, tables, bias_dram, ops, prepare):
    PER = 8
    RING = 3
    TURN_AFTER = 4
    with Phase(nc, "rb") as ph:
        q_parts = ops.q_parts
        tab = [ops.row_table, ph.sb("col_table", [P, 2 * GRID * P], F16)]
        tab = [x[:, :].rearrange("p (h a m) -> p h a m", h=2, a=GRID) for x in tab]
        diff = [ph.sb(f"diff{i}", [P, PER, GRID, QUAD], F32) for i in range(2)]
        hot_a, hot_b, ones = ph.sb("hot_a", [BLK, SEQ], F16), ph.sb("hot_b", [BLK, SEQ], F16), ph.sb("ones", [2, SEQ], F16)
        stage = ops.stage
        b_ps = [ph.ps(f"b_ps{i}", [P, PER, BATCH, GRID], F32) for i in range(RING)]
        mm_done, hi_done, lo_done = (ph.sem(n) for n in ("mm_done", "hi_done", "lo_done"))
        diff_done, tab_hi, tab_lo = (ph.sem(n) for n in ("diff_done", "tab_hi", "tab_lo"))
        stored = [ph.sem("stored0"), ops.last_stored]
        prep = prepare(ph, ops)
        block = ph.block()
        work = [(quad, t) for quad in range(NQUAD) for t in range(2)]
        chunks = GRID // PER

        def first_row(c):
            return GRID - (c % chunks + 1) * PER

        def table_part(c, part):
            return tab[c // chunks][:, part, first_row(c):first_row(c) + PER, :]

        @block.gpsimd
        def _(pool):
            for c in range(2 * chunks):
                need(pool, tab_lo, c - 1)
                rel = tables.rel[c // chunks]
                for n in range(PER):
                    a = first_row(c) + n
                    last = pool.tensor_tensor(out=diff[c % 2][:, n, :, :], in0=rel[:, a:a + GRID, :],
                                              in1=rel[:, a + GRID - 1:a + GRID, :].to_broadcast([P, GRID, QUAD]), op=ALU.subtract)
                last.then_inc(diff_done, 1)
            ops.make_consts(pool, hot_a, hot_b, ones)
            prep.pool(pool)
            prep.quantise(pool)

        @block.sync
        def _(sp):
            prep.load(sp)
            for i, (quad, t) in enumerate(work):
                sp.wait_ge(hi_done, (i + 1) * chunks)
                sp.wait_ge(lo_done, (i + 1) * chunks)
                for part in range(2):
                    dst = bias_dram.rearrange("(b g) h t r q -> g h t r b q", g=NQUAD)[quad, part, t]
                    sp.dma_start(dst, stage[i % 2][:, part, :, :]).then_inc(stored[i % 2], 16)
                if i == 3:
                    ops.load_qkv(sp, 0, 0)
                    sp.wait_ge(stored[1], 64)
                    sp.wait_ge(stored[0], 64)
                    ops.load_bias(sp, 0, 0)
            sp.wait_ge(stored[0], 32 * NQUAD)

        @block.tensor
        def _(pe):
            for i, (quad, t) in enumerate(work):
                q = q_parts[quad][:, :, :].rearrange("p b (R C r c) -> p b R C r c", R=2, C=2, r=BLK)
                for ch in range(chunks):
                    k = i * chunks + ch
                    if i < 2:
                        pe.wait_ge(tab_lo, k + 1)
                    need(pe, lo_done, k - RING + 1)
                    for j in range(PER):
                        at = ch * PER + j
                        rhs = q[:, :, at // BLK, :, at % BLK, :] if t == 0 else q[:, :, :, at // BLK, :, at % BLK]
                        for part in range(2):
                            last = pe.matmul(b_ps[k % RING][:, j, :, :], tab[t][:, part, GRID - 1 - at, :], rhs, start=(part == 0), stop=(part == 1))
                    last.then_inc(mm_done, 1)
                if i == TURN_AFTER:
                    prep.turn(pe, 0)
            prep.turn(pe, 1)

        def spots(i, t, ch):
            half, first = divmod(ch * PER, BLK)
            for other in range(2):
                places = []
                for part in range(2):
                    st = stage[i % 2][:, part, :, :].rearrange("p b (R C r c) -> p b R C r c", R=2, C=2, r=BLK)
                    if t == 0:
                        places.append(st[:, :, half, other, first:first + PER, :].rearrange("p b r c -> p r b c"))
                    else:
                        places.append(st[:, :, other, half, :, first:first + PER].rearrange("p b r c -> p c b r"))
                yield b_ps[(i * chunks + ch) % RING][:, :, :, other * BLK:(other + 1) * BLK], places[0], places[1]

        @block.scalar
        def _(act):
            for i, (quad, t) in enumerate(work):
                if i < 2:
                    for c in range(i * chunks, (i + 1) * chunks):
                        act.wait_ge(diff_done, c + 1)
                        act.activation(table_part(c, 0), diff[c % 2][:, :, :, :].rearrange("p a r h -> p a (r h)"), ACT.Copy).then_inc(tab_hi, 1)
                need(act, stored[i % 2], 32 * (i // 2))
                for ch in range(chunks):
                    k = i * chunks + ch
                    act.wait_ge(mm_done, k + 1)
                    for value, hi, lo in spots(i, t, ch):
                        last = act.activation(hi, value, ACT.Copy)
                    last.then_inc(hi_done, 1)

        @block.vector
        def _(dve):
            for i, (quad, t) in enumerate(work):
                if i < 2:
                    for c in range(i * chunks, (i + 1) * chunks):
                        dve.wait_ge(tab_hi, c + 1)
                        dve.tensor_tensor(table_part(c, 1), diff[c % 2][:, :, :, :].rearrange("p a r h -> p a (r h)"), table_part(c, 0),
                                          ALU.subtract).then_inc(tab_lo, 1)
                for ch in range(chunks):
                    k = i * chunks + ch
                    dve.wait_ge(hi_done, k + 1)
                    for value, hi, lo in spots(i, t, ch):
                        last = dve.tensor_tensor(lo, value, hi, ALU.subtract)
                    last.then_inc(lo_done, 1)
                if i == 0:
                    prep.scales(dve)
                if i == TURN_AFTER:
                    prep.finish(dve, 0)
            prep.finish(dve, 1)


def phase_attention(nc, ops, ffn_in, max_dram, out_dram):
    STEPS = 2 * KT
    LAG = 2
    PRING = 4
    PIECES = QUAD * KT * 2
    PER_STEP = PIECES // STEPS
    LEAD = 3
    RING = 3
    with Phase(nc, "at") as ph:
        mix_q, mix_k, v_u, ident, sum_pick = ops.mix_q, ops.mix_k, ops.v_u, ops.ident, ops.sum_pick
        MAX_ROW, TILE_ORDER = ops.MAX_ROW, ops.TILE_ORDER
        consts, loaded, N_LOADS = ops.consts, ops.loaded, ops.N_LOADS
        probs = [ph.sb(f"probs{i}", [P, QUAD, GROUP], F32) for i in range(PRING)]
        piece_max = [ph.sb(f"piece_max{h}", [P, PIECES // 2], F32) for h in range(2)]
        row_max = [ph.sb(f"row_max{h}", [P, QUAD * TILES], F32) for h in range(2)]
        neg_max = [ph.sb(f"neg_max{h}", [QUAD * TILES, 2, P], F16) for h in range(2)]
        o_sb = [ph.sb(f"o_sb{i}", [P, GROUP], F32) for i in range(2)]
        inv = ph.sb("inv", [P, TILES * QUAD], F32)
        o_n = [ph.sb(f"o_n{i}", [P, GROUP], F32) for i in range(2)]
        inv_wide = [o[:, :].rearrange("p (a r) -> p a r", r=SLOT) for o in o_n]
        s_ps = [ph.ps(f"s_ps{i}", [P, 2, GROUP], F32) for i in range(2)]
        r_ps = [ph.ps(f"r_ps{i}", [P, GROUP], F32) for i in range(RING)]
        o_ps = ph.ps("o_ps", [P, GROUP], F32)

        max_loaded = [ph.sem(f"max_loaded{h}") for h in range(2)]
        max_spread = [ph.sem(f"max_spread{h}") for h in range(2)]
        neg_out = [ph.sem(f"neg_out{h}") for h in range(2)]
        scores_done, exp_done, pv_done = (ph.sem(n) for n in ("scores_done", "exp_done", "pv_done"))
        piece_done, reduced = ph.sem("piece_done"), ph.sem("reduced")
        max_done, max_turned, neg_hi, neg_done = (ph.sem(n) for n in ("max_done", "max_turned", "neg_hi", "neg_done"))
        o_out, sums_done, inv_done, wide_done, spread_done, norm_done = (
            ph.sem(n) for n in ("o_out", "sums_done", "inv_done", "wide_done", "spread_done", "norm_done"))
        o_stored = [ph.sem(f"o_stored{i}") for i in range(2)]
        block = ph.block()

        class Unit:

            def __init__(self, u, image, static):
                self.u, self.image, self.buf = u, image, static % 3
                self.quad = static % NQUAD
                self.turn = image
                self.first, self.last = isinstance(u, int) and u == 0, isinstance(u, int) and u == UNITS - 1

            def after(self, k):
                static = self.buf + k
                return Unit(self.u + k, self.image + static // 3, static)

        BEFORE_FIRST = Unit(-1, -1, -1)

        def each_unit(eng, emit):
            emit(Unit(0, 0, 0))
            with eng.Fori(0, 3) as r:
                for k in range(1, 4):
                    emit(Unit(r * 3 + k, r + k // 3, k))
            for u in (UNITS - 2, UNITS - 1):
                emit(Unit(u, u // 3, u))

        def pieces(n):
            at = PIECES // 2 + (LEAD + n) * PER_STEP
            return list(range(at, at + PER_STEP))

        TURN_AT = {1: STEPS // 2 - LEAD, 0: STEPS - LEAD}
        O_AT = (LAG - 1, KT + LAG - 1)
        SUMS_AT = (O_AT[0] + 1, O_AT[1] + 1)
        SPREAD_AT = (SUMS_AT[0] + 1, SUMS_AT[1] + 1)
        BEFORE, AFTER = (0, 1, 1, 2, 2), 4
        bank_of, before_of, had = {}, {}, {}

        def assign(lag):
            free = list(range(RING))

            def take(*use):
                bank_of[use] = free.pop(0)
                before_of[use] = had.get(bank_of[use])
                had[bank_of[use]] = (use, lag)

            for n in range(STEPS):
                for at in pieces(n)[:BEFORE[2]]:
                    take("piece", at)
                    free.append(bank_of["piece", at])
                for half, step in TURN_AT.items():
                    if n == step:
                        take("maxima", half)
                        free.append(bank_of["maxima", half])
                for at in pieces(n)[BEFORE[2]:]:
                    take("piece", at)
                    free.append(bank_of["piece", at])
                for k in range(2):
                    if n == SUMS_AT[k]:
                        take("half", 1 - k)
                    if n == SPREAD_AT[k]:
                        free.append(bank_of["half", 1 - k])

        assign(1)
        assign(0)

        def r_bank(*use):
            return r_ps[bank_of[use]]

        def wait_bank(pe, unit, *use):
            (kind, i), lag = before_of[use]
            if kind == "piece" and not (unit.last and lag == 0 and i >= PIECES):
                need(pe, reduced, (unit.u - lag) * PIECES + i + 1)
            if kind == "piece" and unit.last and lag == 0 and i >= PIECES:
                pe.wait_ge(neg_done, unit.u * 2 + 2)
            if kind == "half":
                need(pe, norm_done, (unit.u - lag) * 2 + 1 - i)
            if kind == "maxima":
                need(pe, neg_done, (unit.u - lag) * 2 + (2 if i == 1 else 3))

        @block.gpsimd
        def _(pool):
            ffn_in.clear(pool)

        @block.sync
        def _(sp):
            def load(unit):
                ops.load_qkv(sp, unit.image, unit.buf)
                ops.load_bias(sp, unit.u, unit.buf)

            def load_max(unit, half):
                sp.wait_ge(neg_done, unit.u * 2 + half + 1)
                sp.dma_start(max_dram[half].rearrange("h r p -> r h p"), neg_max[half][:, :, :]).then_inc(neg_out[half], 16)
                sp.wait_ge(neg_out[half], (unit.u + 1) * 16)
                for variant in range(ops.VARIANTS):
                    sp.dma_start(mix_q[unit.buf][MAX_ROW:P, variant, :, half * GROUP:(half + 1) * GROUP],
                                 max_dram[half].rearrange("h (j t) p -> h j (t p)", j=QUAD)
                                 ).then_inc((max_spread if variant else max_loaded)[half], 16)

            def store(unit, half):
                sp.wait_ge(norm_done, unit.u * 2 + half + 1)
                dst = out_dram[bass.ds(unit.image * 2 + half, 1), :, unit.quad, :].rearrange("n p t -> (n p) t")
                sp.dma_start(dst, o_n[half][:, :]).then_inc(o_stored[half], 16)

            ops.load_qkv(sp, 0, 1)
            sp.wait_ge(ops.last_stored, 32 * NQUAD)
            ops.load_bias(sp, 1, 1)
            ffn_in.load_wp(sp)
            load_max(Unit(0, 0, 0), 0)

            def emit(unit):
                if not unit.first:
                    store(unit.after(-1), 1)
                load_max(unit, 1)
                if not (isinstance(unit.u, int) and unit.u + 2 >= UNITS):
                    need(sp, pv_done, unit.u * STEPS)
                    load(unit.after(2))
                store(unit, 0)
                if not unit.last:
                    load_max(unit.after(1), 0)

            each_unit(sp, emit)
            sp.wait_ge(o_stored[0], 16 * UNITS)
            sp.wait_ge(o_stored[1], 16 * (UNITS - 1))
            ffn_in.load_biases(sp)
            ffn_in.load(sp, FIRST)
            ffn_in.load(sp, FIRST.after(1))
            store(Unit(UNITS - 1, BATCH - 1, UNITS - 1), 1)
            for half in range(2):
                sp.wait_ge(o_stored[half], 16 * UNITS)

        @block.tensor
        def _(pe):
            def piece(unit, at):
                owner, i = (unit, at) if at < PIECES else (unit.after(1), at - PIECES)
                j, kh = i // (2 * TILES) % QUAD, i % 2
                qt = i // (PIECES // 2) * TILES + i // 2 % TILES
                wait_bank(pe, unit, "piece", at)
                for variant, first, n in ops.SEGMENTS:
                    if first // GROUP == kh:
                        last = pe.matmul(r_bank("piece", at)[:, first % GROUP:first % GROUP + n],
                                         mix_q[owner.buf][0:MAX_ROW, variant, j, qt * P:(qt + 1) * P],
                                         mix_k[owner.buf][0:MAX_ROW, j, first:first + n], start=True, stop=True)
                last.then_inc(piece_done, 1)

            def turn(unit, half):
                owner = unit if half == 1 else unit.after(1)
                pe.wait_ge(max_done, owner.u * 2 + half + 1)
                wait_bank(pe, unit, "maxima", half)
                pe.transpose(r_bank("maxima", half)[0:QUAD * TILES, 0:P], row_max[half][:, :], ident[:, :]).then_inc(max_turned, 1)

            def scores(unit, n, j):
                half, kt = n // KT, TILE_ORDER[n % KT]
                pair = j // 2
                step = unit.u * STEPS + n
                if j % 2 == 0:
                    need(pe, exp_done, step * 2 + pair - 1)
                keys, queries = slice(kt * P, (kt + 1) * P), slice(half * GROUP, (half + 1) * GROUP)
                last = pe.matmul(s_ps[pair][:, j % 2, :], mix_k[unit.buf][:, j, keys], mix_q[unit.buf][:, ops.VARIANT_OF[kt], j, queries],
                                 start=True, stop=True)
                if j % 2 == 1:
                    last.then_inc(scores_done, 1)

            def weigh(unit, n):
                half, at = divmod(n, KT)
                kt = TILE_ORDER[at]
                step = unit.u * STEPS + n
                pe.wait_ge(exp_done, step * 2 + 2)
                if at == 0:
                    need(pe, o_out, unit.u * 2 + half)
                for j in range(QUAD):
                    last = pe.matmul(o_ps[j * SLOT:(j + 1) * SLOT, :], v_u[unit.buf][:, kt, j, :], probs[n % PRING][:, j, :],
                                     start=(at == 0), stop=(at == KT - 1), tile_position=(0, j * SLOT))
                last.then_inc(pv_done, 1)

            def sums(unit, half):
                pe.wait_ge(o_out, unit.u * 2 + half + 1)
                need(pe, norm_done, unit.u * 2 + half)
                if not (unit.last and half == 1):
                    wait_bank(pe, unit.after(half), "half", half)
                for t in range(TILES):
                    last = pe.matmul(r_bank("half", half)[:, t * QUAD:(t + 1) * QUAD], o_sb[half][:, t * P:(t + 1) * P], sum_pick[:, :], start=True, stop=True)
                last.then_inc(sums_done, 1)

            def spread(unit, half):
                pe.wait_ge(wide_done, unit.u * 2 + half + 1)
                for t in range(TILES):
                    last = pe.transpose(r_bank("half", half)[:, t * P:(t + 1) * P],
                                        inv_wide[half][:, t * QUAD:(t + 1) * QUAD, :].rearrange("p h r -> p (h r)"), ident[:, :])
                last.then_inc(spread_done, 1)

            pe.wait_ge(consts, 3)
            pe.wait_ge(loaded[0], 16 * N_LOADS)
            for at in [at for n in range(STEPS) for at in pieces(n)]:
                if at >= PIECES:
                    piece(BEFORE_FIRST, at)
                if at == PIECES + PIECES // 2 + BEFORE[2] - 1:
                    turn(BEFORE_FIRST, 0)

            def emit(unit):
                nxt = unit.after(1)
                for n in range(STEPS):
                    if n % KT == 0:
                        pe.wait_ge(max_loaded[n // KT], (unit.u + 1) * 16)
                    if n % KT == 2:
                        pe.wait_ge(max_spread[n // KT], (unit.u + 1) * (16 * (ops.VARIANTS - 1)))
                    todo = [at for at in pieces(n) if at < PIECES or not unit.last]
                    if PIECES in todo:
                        pe.wait_ge(loaded[nxt.buf], (nxt.turn + 1) * (16 * N_LOADS))
                    for j in range(QUAD):
                        for at in todo[BEFORE[j]:BEFORE[j + 1]]:
                            piece(unit, at)
                        scores(unit, n, j)
                        for half, step in TURN_AT.items():
                            if (n, j) == (step, 1) and (half == 1 or not unit.last):
                                turn(unit, half)
                    for at in todo[BEFORE[QUAD]:AFTER]:
                        piece(unit, at)
                    if n >= LAG:
                        weigh(unit, n - LAG)
                    elif not unit.first:
                        weigh(unit.after(-1), STEPS + n - LAG)
                    for at in todo[AFTER:]:
                        piece(unit, at)
                    for half, owner in ((1, None if unit.first else unit.after(-1)), (0, unit)):
                        if owner and n == SUMS_AT[1 - half]:
                            sums(owner, half)
                        if owner and n == SPREAD_AT[1 - half]:
                            spread(owner, half)

            each_unit(pe, emit)
            last = Unit(UNITS - 1, BATCH - 1, UNITS - 1)
            for n in range(STEPS - LAG, STEPS):
                weigh(last, n)
            sums(last, 1)
            spread(last, 1)

        @block.scalar
        def _(act):
            def exps(unit, n):
                step = unit.u * STEPS + n
                need(act, pv_done, step - PRING + 1)
                for pair in range(2):
                    act.wait_ge(scores_done, step * 2 + pair + 1)
                    act.activation(probs[n % PRING][:, 2 * pair:2 * pair + 2, :], s_ps[pair][:, :, :], ACT.Exp).then_inc(exp_done, 1)

            def take_out(unit, half):
                act.wait_ge(pv_done, unit.u * STEPS + (half + 1) * KT)
                need(act, norm_done, unit.u * 2 + half - 1)
                act.activation(o_sb[half][:, :], o_ps[:, :], ACT.Copy).then_inc(o_out, 1)

            def emit(unit):
                for n in range(STEPS):
                    exps(unit, n)
                    if n == O_AT[0] and not unit.first:
                        take_out(unit.after(-1), 1)
                    if n == O_AT[1]:
                        take_out(unit, 0)

            each_unit(act, emit)
            take_out(Unit(UNITS - 1, BATCH - 1, UNITS - 1), 1)

        @block.vector
        def _(dve):
            def reduce_piece(unit, at):
                half, i = at // (PIECES // 2) % 2, at % (PIECES // 2)
                need(dve, piece_done, unit.u * PIECES + at + 1)
                dve.tensor_reduce(piece_max[half][:, i:i + 1], r_bank("piece", at)[:, :], AX_X, ALU.max).then_inc(reduced, 1)

            def join_max(unit, half):
                owner = unit if half == 1 else unit.after(1)
                dve.wait_ge(reduced, owner.u * PIECES + (half + 1) * (PIECES // 2))
                need(dve, max_turned, owner.u * 2 + half - 1)
                halves = piece_max[half][:, :].rearrange("p (r k) -> p r k", k=2)
                dve.tensor_tensor(row_max[half][:, :], halves[:, :, 0], halves[:, :, 1], ALU.max).then_inc(max_done, 1)

            def negate(unit, half):
                owner = unit if half == 1 else unit.after(1)
                count = owner.u * 2 + half + 1
                dve.wait_ge(max_turned, count)
                need(dve, neg_out[half], owner.u * 16)
                turned = r_bank("maxima", half)[0:QUAD * TILES, 0:P]
                dve.tensor_scalar(neg_max[half][:, 0, :], turned, -1.0, None, ALU.mult).then_inc(neg_hi, 1)
                dve.wait_ge(neg_hi, count)
                dve.scalar_tensor_tensor(out=neg_max[half][:, 1, :], in0=turned, scalar=-1.0, in1=neg_max[half][:, 0, :],
                                         op0=ALU.mult, op1=ALU.subtract).then_inc(neg_done, 1)

            def invert(unit, half):
                dve.wait_ge(sums_done, unit.u * 2 + half + 1)
                dve.reciprocal(inv[:, :], r_bank("half", half)[:, 0:TILES * QUAD]).then_inc(inv_done, 1)
                dve.wait_ge(inv_done, unit.u * 2 + half + 1)
                need(dve, o_stored[half], unit.u * 16)
                dve.tensor_copy(inv_wide[half][:, :, :], inv[:, :].unsqueeze(2).to_broadcast([P, TILES * QUAD, SLOT])).then_inc(wide_done, 1)

            def normalise(unit, half):
                dve.wait_ge(spread_done, unit.u * 2 + half + 1)
                dve.tensor_tensor(o_n[half][:, :], o_sb[half][:, :], r_bank("half", half)[:, :], ALU.mult).then_inc(norm_done, 1)

            def step_pieces(unit, n):
                turned = [half for half, step in TURN_AT.items() if n == step and (half == 1 or not unit.last)]
                for half in turned:
                    join_max(unit, half)
                for k, at in enumerate(pieces(n)):
                    if at < PIECES or not unit.last:
                        reduce_piece(unit, at)
                    if k == BEFORE[2]:
                        for half in turned:
                            negate(unit, half)

            for at in [at for n in range(STEPS) for at in pieces(n)]:
                if at == PIECES + PIECES // 2:
                    join_max(BEFORE_FIRST, 0)
                if at >= PIECES:
                    reduce_piece(BEFORE_FIRST, at)
                if at == PIECES + PIECES // 2 + BEFORE[2]:
                    negate(BEFORE_FIRST, 0)

            def emit(unit):
                for n in range(STEPS):
                    step_pieces(unit, n)
                    for half, owner in ((1, None if unit.first else unit.after(-1)), (0, unit)):
                        if owner and n == SUMS_AT[1 - half]:
                            invert(owner, half)
                        if owner and n == SPREAD_AT[1 - half]:
                            normalise(owner, half)

            each_unit(dve, emit)
            last = Unit(UNITS - 1, BATCH - 1, UNITS - 1)
            invert(last, 1)
            normalise(last, 1)


class Weights:

    def __init__(self, stack, nc, w1, aw1, aa1, w2, aw2, aw2_cols, aa2):
        def sb(name, shape, dt):
            return stack.enter_context(nc.sbuf_tensor(f"wt_{name}", shape, dt))

        self.dram = (w1, aw1, aa1, w2, aw2, aw2_cols, aa2)
        self.w1_t = sb("w1_t", [HALF, 2, HID], BF16)
        self.w2_t = sb("w2_t", [P, HT, C], BF16)
        self.s1 = sb("s1", [P, HT], F32)
        self.s2_row = sb("s2_row", [P, C], F32)
        self.step = sb("step", [P, 6], F32)
        self.bound = sb("bound", [P, 4], F32)
        self.inv_a1, self.inv_a2 = self.step[:, 4:5], self.step[:, 5:6]

    def __call__(self, ph, ops):
        self.aw1_sb, self.inv_w1 = ph.sb("aw1_sb", [P, HT], F32), ph.sb("inv_w1", [P, HT], F32)
        self.aw2_sb, self.inv_w2 = ph.sb("aw2_sb", [HALF, 2], F32), ph.sb("inv_w2", [HALF, 2], F32)
        self.aa1_row, self.aa2_row = ops.spare[:, 2 * HID:2 * HID + C], ph.sb("aa2_row", [P, HID], F32)
        self.w1_f, self.w2_f = ph.sb("w1_f", [P, HT, C], F32), ops.spare[0:HALF, 0:2 * HID].rearrange("p (h c) -> p h c", h=2)
        wide1, wide2 = (v[:, :, :, :].bitcast(BF16).rearrange("p k h e -> p (k h e)") for v in ops.v_u[1:])
        self.w1_q = wide1[:, 0:HT * C].rearrange("p (t c) -> p t c", c=C)
        self.w2_q = wide2[0:HALF, 0:2 * HID].rearrange("p (h c) -> p h c", h=2)
        self.ident = ph.sb("ident", [P, P], BF16)
        self.w_ps = ph.ps("w_ps", [P, 2, 2 * GROUP], BF16)
        self.zeroed, self.ident_made, self.params_in, self.chained, self.turned, self.copied = (
            ph.sem(n) for n in ("zeroed", "ident_made", "params_in", "chained", "turned", "copied"))
        self.scaled, self.stepped, self.quantised = ph.sem("scaled"), ph.sem("stepped"), ph.sem("quantised")
        self.links = 0
        return self

    def pool(self, pool):
        make_identity(pool, self.ident, self.zeroed, self.ident_made)

    def load(self, sp):
        w1, aw1, aa1, w2, aw2, aw2_cols, aa2 = self.dram
        for dst, src in ((self.w1_f[:, :, :], w1.rearrange("(t p) c -> p t c", p=P)), (self.w2_f[:, :, :], w2.rearrange("(h p) c -> p h c", h=2)),
                         (self.aw1_sb[:, :], aw1), (self.aw2_sb[:, :], aw2_cols), (self.s2_row[:, :], aw2.partition_broadcast(P)),
                         (self.aa1_row[:, :], aa1.partition_broadcast(P)), (self.aa2_row[:, :], aa2.partition_broadcast(P))):
            sp.dma_start(dst, src).then_inc(self.params_in, 16)

    def chain(self, dve, ins):
        ins.then_inc(self.chained, 1)
        self.links += 1
        dve.wait_ge(self.chained, self.links)

    def scales(self, dve):
        step, link = self.step, lambda ins: self.chain(dve, ins)
        dve.wait_ge(self.params_in, 16 * 7)
        dve.reciprocal(self.inv_w1[:, :], self.aw1_sb[:, :]).then_inc(self.scaled, 1)
        dve.reciprocal(self.inv_w2[:, :], self.aw2_sb[:, :]).then_inc(self.scaled, 1)
        link(dve.tensor_reduce(step[:, 0:1], self.aa1_row[:, :], AX_X, ALU.add))
        link(dve.tensor_reduce(step[:, 1:2], self.aa2_row[:, :], AX_X, ALU.add))
        link(dve.tensor_scalar(step[:, 2:3], step[:, 0:1], 1.0 / C, None, ALU.mult))
        link(dve.tensor_scalar(step[:, 3:4], step[:, 1:2], 1.0 / HID, None, ALU.mult))
        link(dve.reciprocal(step[:, 4:6], step[:, 2:4]))
        link(dve.tensor_scalar(self.s1[:, :], self.aw1_sb[:, :], step[:, 2:3], None, ALU.mult))
        link(dve.tensor_scalar(self.s2_row[:, :], self.s2_row[:, :], step[:, 3:4], None, ALU.mult))
        for at, edge, limit, op in ((0, 10.0, QP, ALU.min), (1, -10.0, QN, ALU.max)):
            link(dve.tensor_scalar(self.bound[:, at:at + 1], self.inv_a2, edge, MAGIC, ALU.mult, ALU.add))
            link(dve.tensor_scalar(self.bound[:, 2 + at:3 + at], self.bound[:, at:at + 1], MAGIC + limit, None, op))

    def quantise(self, pool):
        pool.wait_ge(self.scaled, 2)
        w1 = [(self.w1_f[:, i, :], self.w1_q[:, i, :], self.inv_w1[:, i:i + 1]) for i in range(HT)]
        w2 = [(self.w2_f[:, i, :], self.w2_q[:, i, :], self.inv_w2[:, i:i + 1]) for i in range(2)]
        steps = 0
        for work in (w1, w2):
            for src, dst, inv in work:
                pool.tensor_scalar(src, src, inv, MAGIC, ALU.mult, ALU.add).then_inc(self.stepped, 1)
            steps += len(work)
            pool.wait_ge(self.stepped, steps)
            for src, dst, inv in work:
                pool.tensor_scalar(src, src, MAGIC + QP, MAGIC + QN, ALU.min, ALU.max).then_inc(self.stepped, 1)
            steps += len(work)
            pool.wait_ge(self.stepped, steps)
            for src, dst, inv in work:
                last = pool.tensor_scalar(dst, src, -MAGIC, None, ALU.add)
            last.then_inc(self.quantised, 1)

    def turn(self, pe, which):
        pe.wait_ge(self.quantised, which + 1)
        if which == 0:
            pe.wait_ge(self.ident_made, 1)
            for h in range(2):
                for t in range(HT):
                    last = pe.transpose(self.w_ps[0:HALF, h, t * P:(t + 1) * P], self.w1_q[:, t, h * HALF:(h + 1) * HALF], self.ident[:, :])
        else:
            pe.wait_ge(self.copied, 1)
            for t in range(HT):
                for h in range(2):
                    last = pe.transpose(self.w_ps[:, t // 3, t % 3 * 256 + h * HALF:t % 3 * 256 + (h + 1) * HALF],
                                        self.w2_q[:, h, t * P:(t + 1) * P], self.ident[0:HALF, 0:HALF])
        last.then_inc(self.turned, 1)

    def finish(self, dve, which):
        dve.wait_ge(self.turned, which + 1)
        if which == 0:
            dve.tensor_copy(self.w1_t[:, :, :], self.w_ps[0:HALF, :, 0:HID]).then_inc(self.copied, 1)
        else:
            for i in range(2):
                dve.tensor_copy(self.w2_t[:, 3 * i:3 * i + 3, :],
                                self.w_ps[:, i, 0:HID].rearrange("p (t c) -> p t c", c=256)[:, :, 0:C])


def phase_ffn(nc, ffn_in, wt, out):
    with Phase(nc, "ff") as ph:
        wp_sb, bp_row, b2_row, b1_sb, x_in, att = ffn_in.wp_sb, ffn_in.bp_row, ffn_in.b2_row, ffn_in.b1_sb, ffn_in.x_in, ffn_in.att
        params_in, x_loaded, att_loaded, N_PARAMS = ffn_in.params_in, ffn_in.x_loaded, ffn_in.att_loaded, ffn_in.N_PARAMS
        ident = ph.sb("ident", [P, P], BF16)
        magic = ph.sb("magic", [P, 1], F32)
        half_neg = ph.sb("half_neg", [P, TILES], F32)
        eps = ph.sb("eps", [P, TILES], F32)
        y = [ph.sb(f"y{s}", [P, TILES, C], F32) for s in range(2)]
        y_b = [ph.sb(f"y_b{s}", [P, TILES, C], F32) for s in range(2)]
        stats = [ph.sb(f"stats{s}", [P, TILES, 6], F32) for s in range(2)]
        meanvar = [ph.sb(f"meanvar{s}", [P, TILES, 2], F32) for s in range(2)]
        var_eps = [ph.sb(f"var_eps{s}", [P, TILES], F32) for s in range(2)]
        rstd = [ph.sb(f"rstd{s}", [P, 3, TILES], F32) for s in range(2)]
        y_n = ph.sb("y_n", [P, TILES, C], F32)
        y_r = ph.sb("y_r", [P, TILES, C], F32)
        y_q = [ph.sb(f"y_q{s}", [P, TILES, C], BF16) for s in range(2)]
        y_t = [ph.sb(f"y_t{s}", [HALF, 2, GROUP], BF16) for s in range(2)]
        hid = ph.sb("hid", [P, HT, GROUP], F32)
        hid_r = ph.sb("hid_r", [P, HT, GROUP], F32)
        hid_q = [ph.sb(f"hid_q{s}", [P, HT, GROUP], BF16) for s in range(2)]
        ffn = [ph.sb(f"ffn{s}", [P, TILES, C], F32) for s in range(2)]
        res = [ph.sb(f"res{s}", [P, TILES, C], F32) for s in range(2)]
        p_ps = ph.ps("p_ps", [P, TILES, 256], F32)
        t_ps = ph.ps("t_ps", [P, 2, GROUP], BF16)
        h_ps = [ph.ps(f"h_ps{i}", [P, GROUP], F32) for i in range(3)]
        f_ps = ph.ps("f_ps", [P, TILES, 256], F32)

        zeroed, ident_made, pool_consts, magic_made = (ph.sem(n) for n in ("zeroed", "ident_made", "pool_consts", "magic_made"))
        stored = [ph.sem(f"stored{s}") for s in range(2)]
        xb_done, proj_done, y_done, yb_done, stats_done, aggr_done, eps_done, pow_done, newton = (
            ph.sem(n) for n in ("xb_done", "proj_done", "y_done", "yb_done", "stats_done", "aggr_done", "eps_done", "pow_done", "newton"))
        yn_done, yr_done, yi_done, yq_done, t_done, yt_ready = (
            ph.sem(n) for n in ("yn_done", "yr_done", "yi_done", "yq_done", "t_done", "yt_ready"))
        h_done, gelu_done, round_done, bound_done, hq_done = (
            ph.sem(n) for n in ("h_done", "gelu_done", "round_done", "bound_done", "hq_done"))
        f_done, scaled, res_done = (ph.sem(n) for n in ("f_done", "scaled", "res_done"))
        block = ph.block()
        out_v = out.rearrange("(n t p) c -> n p t c", t=TILES, p=P)
        half_h = HT // 2

        @block.sync
        def _(sp):
            def store(g):
                sp.wait_ge(res_done, g.n + 1)
                sp.dma_start(out_v[bass.ds(g.n, 1), :, :, :].rearrange("n p t c -> (n p) t c"), res[g.s][:, :, :]).then_inc(stored[g.s], 16)

            def emit(g):
                if not (g.last or g.after(1).last):
                    sp.wait_ge(y_done, g.n + 1)
                    ffn_in.load(sp, g.after(2))
                if not (g.first or g.after(-1).first):
                    store(g.after(-2))

            each_group(sp, emit)
            store(LAST.after(-1))
            store(LAST)
            for s in range(2):
                sp.wait_ge(stored[s], 16 * (GROUPS // 2))

        @block.gpsimd
        def _(pool):
            make_identity(pool, ident, zeroed, ident_made)
            pool.memset(eps[:, :], 1e-5).then_inc(pool_consts, 1)
            pool.memset(half_neg[:, :], -0.5).then_inc(pool_consts, 1)
            pool.wait_ge(pool_consts, 2)
            pool.wait_ge(params_in, 16 * N_PARAMS)

            def add_bias(g):
                pool.wait_ge(x_loaded[g.s], (g.it + 1) * 16)
                for t in range(TILES):
                    last = pool.tensor_tensor(out=x_in[g.s][:, t, :], in0=x_in[g.s][:, t, :], in1=bp_row[:, :], op=ALU.add)
                last.then_inc(xb_done, 1)

            def inverse_std(g):
                pool.wait_ge(aggr_done, g.n + 1)
                pool.tensor_tensor(out=var_eps[g.s][:, :], in0=meanvar[g.s][:, :, 1], in1=eps[:, :], op=ALU.add).then_inc(eps_done, 1)
                pool.wait_ge(eps_done, g.n + 1)
                pool.tensor_tensor(out=rstd[g.s][:, 0, :], in0=var_eps[g.s][:, :], in1=half_neg[:, :], op=ALU.pow).then_inc(pow_done, 1)

            def add_b2(g):
                pool.wait_ge(y_done, g.n + 1)
                need(pool, res_done, g.n - 1)
                for t in range(TILES):
                    last = pool.tensor_tensor(out=y_b[g.s][:, t, :], in0=y[g.s][:, t, :], in1=b2_row[:, :], op=ALU.add)
                last.then_inc(yb_done, 1)

            def stage_c(g):
                pool.wait_ge(scaled, g.n + 1)
                pool.wait_ge(yb_done, g.n + 1)
                need(pool, stored[g.s], g.it * 16)
                pool.tensor_tensor(out=res[g.s][:, :, :], in0=ffn[g.s][:, :, :], in1=y_b[g.s][:, :, :], op=ALU.add).then_inc(res_done, 1)

            add_bias(FIRST)
            inverse_std(FIRST)
            add_bias(FIRST.after(1))
            inverse_std(FIRST.after(1))
            add_b2(FIRST)

            def emit(g):
                if not (g.last or g.after(1).last):
                    add_bias(g.after(2))
                    inverse_std(g.after(2))
                if not g.first:
                    stage_c(g.after(-1))
                if not g.last:
                    add_b2(g.after(1))

            each_group(pool, emit)
            stage_c(LAST)

        @block.vector
        def _(dve):
            def residual(g):
                st, mv, rs = stats[g.s], meanvar[g.s], rstd[g.s]
                dve.wait_ge(xb_done, g.n + 1)
                dve.wait_ge(proj_done, g.n + 1)
                need(dve, yb_done, g.n - 1)
                dve.tensor_tensor(y[g.s][:, :, :], p_ps[:, :, 0:C], x_in[g.s][:, :, :], ALU.add).then_inc(y_done, 1)
                dve.wait_ge(y_done, g.n + 1)
                for t in range(TILES):
                    last = dve.bn_stats(st[:, t, :], y[g.s][:, t, :])
                last.then_inc(stats_done, 1)
                dve.wait_ge(stats_done, g.n + 1)
                dve.memset(rs[:, 1, :], 0.0)
                for t in range(TILES):
                    last = dve.bn_aggr(mv[:, t, :], st[:, t, :])
                last.then_inc(aggr_done, 1)

            def normalise(g):
                mv, rs = meanvar[g.s], rstd[g.s]
                dve.wait_ge(pow_done, g.n + 1)
                r0, r1, r2 = (rs[:, i, :] for i in range(3))
                dve.tensor_tensor(r1, r0, r0, ALU.mult).then_inc(newton, 1)
                dve.wait_ge(newton, g.n * 3 + 1)
                dve.scalar_tensor_tensor(out=r2, in0=r1, scalar=-0.5, in1=var_eps[g.s][:, :], op0=ALU.mult, op1=ALU.mult).then_inc(newton, 1)
                dve.wait_ge(newton, g.n * 3 + 2)
                dve.scalar_tensor_tensor(out=r1, in0=r2, scalar=1.5, in1=r0, op0=ALU.add, op1=ALU.mult).then_inc(newton, 1)
                dve.wait_ge(newton, g.n * 3 + 3)
                for t in range(TILES):
                    last = dve.tensor_scalar(y_n[:, t, :], y[g.s][:, t, :], mv[:, t, 0:1], rs[:, 1, t:t + 1], ALU.subtract, ALU.mult)
                last.then_inc(yn_done, 1)
                dve.wait_ge(yn_done, g.n + 1)
                dve.tensor_scalar(y_r[:, :, :], y_n[:, :, :], wt.inv_a1, MAGIC, ALU.mult, ALU.add).then_inc(yr_done, 1)
                dve.wait_ge(yr_done, g.n + 1)
                dve.tensor_scalar(y_n[:, :, :], y_r[:, :, :], MAGIC + QP, MAGIC + QN, ALU.min, ALU.max).then_inc(yi_done, 1)
                dve.wait_ge(yi_done, g.n + 1)
                need(dve, t_done, g.n - 1)
                dve.tensor_scalar(y_q[g.s][:, :, :], y_n[:, :, :], -MAGIC, None, ALU.add).then_inc(yq_done, 1)

            def stage_b(g, hf):
                part = slice(hf * half_h, (hf + 1) * half_h)
                if hf == 0:
                    need(dve, f_done, g.n - 1)
                dve.wait_ge(round_done, g.n * 2 + hf + 1)
                dve.tensor_scalar(hid_r[:, part, :], hid_r[:, part, :], wt.bound[:, 2:3], wt.bound[:, 3:4], ALU.min, ALU.max).then_inc(bound_done, 1)
                dve.wait_ge(bound_done, g.n * 2 + hf + 1)
                dve.tensor_scalar(hid_q[g.s][:, part, :], hid_r[:, part, :], -MAGIC, None, ALU.add).then_inc(hq_done, 1)

            def stage_c(g):
                dve.wait_ge(f_done, g.n + 1)
                need(dve, res_done, g.n - 1)
                for t in range(TILES):
                    last = dve.tensor_tensor(ffn[g.s][:, t, :], f_ps[:, t, 0:C], wt.s2_row[:, :], ALU.mult)
                last.then_inc(scaled, 1)

            dve.memset(magic[:, :], MAGIC).then_inc(magic_made, 1)
            residual(FIRST)
            normalise(FIRST)
            residual(FIRST.after(1))

            def emit(g):
                if not g.last:
                    normalise(g.after(1))
                stage_b(g, 0)
                if not (g.last or g.after(1).last):
                    residual(g.after(2))
                stage_b(g, 1)
                if not g.first:
                    stage_c(g.after(-1))

            each_group(dve, emit)
            stage_c(LAST)

        @block.scalar
        def _(act):
            act.wait_ge(magic_made, 1)
            act.wait_ge(params_in, 16 * N_PARAMS)

            def emit(g):
                act.wait_ge(t_done, g.n + 1)
                need(act, h_done, (g.n - 1) * HT)
                act.activation(y_t[g.s][:, :, :], t_ps[0:HALF, :, :], ACT.Copy).then_inc(yt_ready, 1)
                need(act, round_done, g.n * 2)
                for t in range(HT):
                    act.wait_ge(h_done, g.n * HT + t + 1)
                    act.activation(hid[:, t, :], h_ps[t % 3][:, :], ACT.Gelu, bias=b1_sb[:, t:t + 1], scale=wt.s1[:, t:t + 1]).then_inc(gelu_done, 1)
                need(act, hq_done, g.n * 2)
                for hf in range(2):
                    part = slice(hf * half_h, (hf + 1) * half_h)
                    act.wait_ge(gelu_done, g.n * HT + (hf + 1) * half_h)
                    act.activation(hid_r[:, part, :], hid[:, part, :], ACT.Identity, bias=magic[:, 0:1], scale=wt.inv_a2).then_inc(round_done, 1)

            each_group(act, emit)

        @block.tensor
        def _(pe):
            def project(g):
                pe.wait_ge(att_loaded[g.s], (g.it + 1) * 16)
                need(pe, y_done, g.n)
                for t in range(TILES):
                    for quad in range(NQUAD):
                        last = pe.matmul(p_ps[:, t, 0:C], att[g.s][:, quad, t * P:(t + 1) * P], wp_sb[:, quad, :],
                                         start=(quad == 0), stop=(quad == NQUAD - 1))
                last.then_inc(proj_done, 1)

            def hidden(g):
                pe.wait_ge(yq_done, g.n + 1)
                need(pe, yt_ready, g.n)
                for t in range(TILES):
                    for h in range(2):
                        last = pe.transpose(t_ps[0:HALF, h, t * P:(t + 1) * P], y_q[g.s][:, t, h * HALF:(h + 1) * HALF], ident[:, :])
                last.then_inc(t_done, 1)
                pe.wait_ge(yt_ready, g.n + 1)
                for t in range(HT):
                    need(pe, gelu_done, g.n * HT + t - 2)
                    for h in range(2):
                        last = pe.matmul(h_ps[t % 3][:, :], wt.w1_t[:, h, t * P:(t + 1) * P], y_t[g.s][:, h, :], start=(h == 0), stop=(h == 1))
                    last.then_inc(h_done, 1)

            def second(g):
                need(pe, scaled, g.n)
                pe.wait_ge(hq_done, g.n * 2 + 2)
                for t in range(TILES):
                    for k in range(HT):
                        last = pe.matmul(f_ps[:, t, 0:C], hid_q[g.s][:, k, t * P:(t + 1) * P], wt.w2_t[:, k, :], start=(k == 0), stop=(k == HT - 1))
                last.then_inc(f_done, 1)

            pe.wait_ge(ident_made, 1)
            pe.wait_ge(params_in, 16 * N_PARAMS)
            project(FIRST)
            project(FIRST.after(1))

            def emit(g):
                hidden(g)
                if not (g.last or g.after(1).last):
                    project(g.after(2))
                if not g.first:
                    second(g.after(-1))

            each_group(pe, emit)
            second(LAST)


def build(nc, a, out):
    qk_dram = nc.dram_tensor("qk_parts", (BATCH, 3, 2, P, SEQ), F16).ap()
    v_dram = nc.dram_tensor("v_rows", (BATCH, P, KT, NH * SLOT), F32).ap()
    bias_dram = nc.dram_tensor("bias_parts", (UNITS, 2, 2, P, SEQ), F16).ap()
    max_dram = nc.dram_tensor("max_rows", (2, 2, QUAD * TILES, P), F16).ap()
    att_dram = nc.dram_tensor("att", (GROUPS, P, NQUAD, GROUP), F32).ap()
    with ExitStack() as kept:
        weights = Weights(kept, nc, a["w1"], a["alpha_w1"], a["alpha_a1"], a["w2"], a["alpha_w2"], a["alpha_w2_cols"], a["alpha_a2"])
        mix_q0 = kept.enter_context(nc.sbuf_tensor("op_mix_q0", [P, Operands.VARIANTS, QUAD, SEQ], F16))
        ffn_in = FfnInputs(nc, kept, mix_q0, a["x"], a["Wp"], a["bp"], a["b1"], a["b2"], att_dram)
        with ExitStack() as attending:
            ops = Operands(nc, attending, mix_q0, qk_dram, v_dram, bias_dram)
            with ExitStack() as relating:
                tables = RelTables(nc, relating, a["rel_h"], a["rel_w"])
                phase_project(nc, a["x"], a["Wq"], a["bq"], a["Wk"], a["bk"], a["Wv"], a["bv"], tables, ops, qk_dram, v_dram)
                phase_rel_bias(nc, tables, bias_dram, ops, weights)
            phase_attention(nc, ops, ffn_in, max_dram, att_dram)
        phase_ffn(nc, ffn_in, weights, out)


def kernel(**inputs):
    import numpy as _np
    import concourse.bacc as _bacc
    from concourse import mybir as _mybir
    from concourse.bass_utils import run_bass_kernel_spmd as _run

    nc = _bacc.Bacc("TRN2", target_bir_lowering=False, num_devices=1)
    arrays, args = {}, {}
    for name, value in inputs.items():
        value = _np.asarray(value)
        short = name.replace("L0_conv_", "").replace("L0_ffn_", "")
        if short == "x":
            value = value.reshape(BATCH, 2, BLK, 2, BLK, C).transpose(0, 1, 3, 2, 4, 5).reshape(TOKENS, C)
        if short in ("Wq", "Wk", "bq", "bk"):
            value = value.reshape(-1, NQUAD, QUAD, HD).swapaxes(2, 3).reshape(value.shape)
        if short in ("rel_h", "rel_w"):
            value = value[::-1].T
        laid = {short: value}
        if short in ("b1", "alpha_w1"):
            laid = {short: value.reshape(HT, P).T}
        if short == "alpha_w2":
            laid["alpha_w2_cols"] = value.reshape(2, HALF).T
        for key, array in laid.items():
            array = _np.ascontiguousarray(array)
            arrays[f"in_{key}"] = array
            args[key] = nc.dram_tensor(f"in_{key}", array.shape, _mybir.dt.from_np(array.dtype), kind="ExternalInput").ap()
    out = nc.dram_tensor("out_0", (TOKENS, C), _mybir.dt.float32, kind="ExternalOutput").ap()
    build(nc, args, out)
    r = _run(nc, [arrays], core_ids=[0])
    return r.results[0]["out_0"].reshape(BATCH, 2, 2, BLK, BLK, C).transpose(0, 1, 3, 2, 4, 5).reshape(BATCH, GRID, GRID, C)
```
